# Optimizing a Trainium2 kernel written in Bass

```python
import numpy as np
import jax
import jax.numpy as jnp

def _softmax(x, axis=-1):
    return jax.nn.softmax(x, axis=axis)

def _gelu(x):
    return jax.nn.gelu(x, approximate=True)

def _silu(x):
    return jax.nn.silu(x)

def _sigmoid(x):
    return jax.nn.sigmoid(x)

def _layernorm(x, axis=-1, eps=1e-05):
    m = jnp.mean(x, axis=axis, keepdims=True)
    v = jnp.var(x, axis=axis, keepdims=True)
    return (x - m) / jnp.sqrt(v + eps)

def _scatter_add(tgt, idx, src, axis=0):
    return tgt.at[idx].add(src)

def _segment_sum(src, seg, n):
    return jax.ops.segment_sum(src, seg, n)
kernel_name = 'mk_conv_attn_hybrid_d2_conv_nhwc768_r4_8cf580'

def setup_inputs(seed: int=0):
    np.random.seed(seed)
    _w = jnp.asarray

    def _rec_inputs():
        import jax
        import jax.numpy as jnp
        _gk = jax.random.key(seed)
        x = -0.0004039 + 1 * jax.random.normal(jax.random.fold_in(_gk, 1), (4, 16, 16, 192), jnp.float32)
        return x
    x = _rec_inputs()

    def _L0_conv_setup():
        import jax, jax.numpy as jnp
        import numpy as np
        B_, H_, W_, DM = (4, 16, 16, 192)
        DI = int(0.5 * DM)
        N = 16
        R = -(-DM // 16)
        K = 4

        def selective_scan(xs, dts, As, Bs, Cs, Dsk):
            u = jnp.moveaxis(xs, -1, 0)
            d = jnp.moveaxis(dts, -1, 0)
            Bt = jnp.moveaxis(Bs, -1, 0)
            Ct = jnp.moveaxis(Cs, -1, 0)

            def step(h, inp):
                u_t, d_t, B_t, C_t = inp
                dA = jnp.exp(d_t[..., None] * As)
                h = h * dA + (d_t * u_t)[..., None] * B_t[:, :, None, :]
                y = jnp.einsum('bkcn,bkn->bkc', h, C_t)
                return (h, y)
            h0 = jnp.zeros(u.shape[1:] + (As.shape[-1],), u.dtype)
            _, ys = jax.lax.scan(step, h0, (u, d, Bt, Ct))
            ys = jnp.moveaxis(ys, 0, -1)
            return ys + Dsk[None, :, :, None] * xs
        key = jax.random.key(seed)
        ks = jax.random.split(key, 8)
        s = lambda i, shape, sc=0.02: jax.random.normal(ks[i], shape, jnp.float32) * sc
        return dict(x=jax.random.normal(ks[0], (B_, H_, W_, DM), jnp.float32), in_proj_w=s(1, (2 * DI, DM)), conv_w=s(2, (DI, 1, 3, 3)), conv_b=jnp.zeros((DI,), jnp.float32), x_proj_w=s(3, (K, R + 2 * N, DI)), dt_projs_w=s(4, (K, DI, R)), dt_projs_b=s(5, (K, DI)), A_logs=jnp.log(jnp.tile(jnp.arange(1, N + 1, dtype=jnp.float32)[None, :], (K * DI, 1))), Ds=jnp.ones((K * DI,), jnp.float32), out_norm_g=jnp.ones((DI,), jnp.float32), out_norm_b=jnp.zeros((DI,), jnp.float32), out_proj_w=s(6, (DM, DI)))
    _L0_conv_all = _L0_conv_setup()
    _L0_conv_in = {k: v for k, v in _L0_conv_all.items() if k in ('in_proj_w', 'conv_w', 'conv_b', 'x_proj_w', 'dt_projs_w', 'dt_projs_b', 'A_logs', 'Ds', 'out_norm_g', 'out_norm_b', 'out_proj_w')}
    del _L0_conv_all

    def _L1_attn_setup():
        import jax, jax.numpy as jnp
        import numpy as np
        NUM_HEADS = 12
        KERNEL_EPS = 0.001

        def _performer_relu_attention(q, k, v, projection):
            d = q.shape[-1]
            data_normalizer = 1.0 / jnp.sqrt(jnp.sqrt(jnp.asarray(d, q.dtype)))
            qp = jax.nn.relu(jnp.einsum('bhnd,md->bhnm', q * data_normalizer, projection)) + KERNEL_EPS
            kp = jax.nn.relu(jnp.einsum('bhnd,md->bhnm', k * data_normalizer, projection)) + KERNEL_EPS
            k_sum = kp.sum(axis=2)
            d_inv = 1.0 / jnp.einsum('bhnm,bhm->bhn', qp, k_sum)
            context = jnp.einsum('bhnm,bhnd->bhmd', kp, v)
            out = jnp.einsum('bhnm,bhmd->bhnd', qp, context) * d_inv[..., None]
            return out
        key = jax.random.key(seed)
        ks = jax.random.split(key, 6)
        B, N, C = (4, 1024, 192)
        H = NUM_HEADS
        d = C // H
        m = 64
        x = jax.random.normal(ks[0], (B, N, C), dtype=jnp.float32)
        w_qkv = jax.random.normal(ks[1], (3 * C, C), dtype=jnp.float32) * 0.02
        b_qkv = jnp.zeros((3 * C,), dtype=jnp.float32)
        w_proj = jax.random.normal(ks[2], (C, C), dtype=jnp.float32) * 0.02
        b_proj = jnp.zeros((C,), dtype=jnp.float32)
        projection = jax.random.normal(ks[3], (m, d), dtype=jnp.float32)
        return {'x': x, 'w_qkv': w_qkv, 'b_qkv': b_qkv, 'w_proj': w_proj, 'b_proj': b_proj, 'projection': projection}
    _L1_attn_all = _L1_attn_setup()
    _L1_attn_in = {k: v for k, v in _L1_attn_all.items() if k in ('w_qkv', 'b_qkv', 'w_proj', 'b_proj', 'projection')}
    del _L1_attn_all

    def _L1_ffn_setup():
        import jax, jax.numpy as jnp
        import numpy as np
        H = 12
        D = 16
        K = 6
        EPS = 1e-12
        key = jax.random.key(seed)
        ks = jax.random.split(key, 8)
        hid = H * D
        sc = 0.02
        return {'hidden_states': jax.random.normal(ks[0], (8, 256, hid), jnp.float32), 'Wq': jax.random.normal(ks[1], (hid, hid), jnp.float32) * sc, 'bq': jnp.zeros((hid,), jnp.float32), 'Wk': jax.random.normal(ks[2], (hid, hid), jnp.float32) * sc, 'bk': jnp.zeros((hid,), jnp.float32), 'Wv': jax.random.normal(ks[3], (hid, hid), jnp.float32) * sc, 'bv': jnp.zeros((hid,), jnp.float32), 'Wr': jax.random.normal(ks[4], (hid, H), jnp.float32) * sc, 'br': jnp.zeros((H,), jnp.float32), 'Wo': jax.random.normal(ks[5], (hid, hid), jnp.float32) * sc, 'bo': jnp.zeros((hid,), jnp.float32), 'ln_g': jnp.ones((hid,), jnp.float32), 'ln_b': jnp.zeros((hid,), jnp.float32)}
    _L1_ffn_all = _L1_ffn_setup()
    _L1_ffn_in = {k: v for k, v in _L1_ffn_all.items() if k in ('Wq', 'bq', 'Wk', 'bk', 'Wv', 'bv', 'Wr', 'br', 'Wo', 'bo', 'ln_g', 'ln_b')}
    del _L1_ffn_all
    return {'x': x, 'L0_conv_in_proj_w': _L0_conv_in['in_proj_w'], 'L0_conv_conv_w': _L0_conv_in['conv_w'], 'L0_conv_conv_b': _L0_conv_in['conv_b'], 'L0_conv_x_proj_w': _L0_conv_in['x_proj_w'], 'L0_conv_dt_projs_w': _L0_conv_in['dt_projs_w'], 'L0_conv_dt_projs_b': _L0_conv_in['dt_projs_b'], 'L0_conv_A_logs': _L0_conv_in['A_logs'], 'L0_conv_Ds': _L0_conv_in['Ds'], 'L0_conv_out_norm_g': _L0_conv_in['out_norm_g'], 'L0_conv_out_norm_b': _L0_conv_in['out_norm_b'], 'L0_conv_out_proj_w': _L0_conv_in['out_proj_w'], 'L1_attn_w_qkv': _L1_attn_in['w_qkv'], 'L1_attn_b_qkv': _L1_attn_in['b_qkv'], 'L1_attn_w_proj': _L1_attn_in['w_proj'], 'L1_attn_b_proj': _L1_attn_in['b_proj'], 'L1_attn_projection': _L1_attn_in['projection'], 'L1_ffn_Wq': _L1_ffn_in['Wq'], 'L1_ffn_bq': _L1_ffn_in['bq'], 'L1_ffn_Wk': _L1_ffn_in['Wk'], 'L1_ffn_bk': _L1_ffn_in['bk'], 'L1_ffn_Wv': _L1_ffn_in['Wv'], 'L1_ffn_bv': _L1_ffn_in['bv'], 'L1_ffn_Wr': _L1_ffn_in['Wr'], 'L1_ffn_br': _L1_ffn_in['br'], 'L1_ffn_Wo': _L1_ffn_in['Wo'], 'L1_ffn_bo': _L1_ffn_in['bo'], 'L1_ffn_ln_g': _L1_ffn_in['ln_g'], 'L1_ffn_ln_b': _L1_ffn_in['ln_b']}

def reference(x, L0_conv_in_proj_w, L0_conv_conv_w, L0_conv_conv_b, L0_conv_x_proj_w, L0_conv_dt_projs_w, L0_conv_dt_projs_b, L0_conv_A_logs, L0_conv_Ds, L0_conv_out_norm_g, L0_conv_out_norm_b, L0_conv_out_proj_w, L1_attn_w_qkv, L1_attn_b_qkv, L1_attn_w_proj, L1_attn_b_proj, L1_attn_projection, L1_ffn_Wq, L1_ffn_bq, L1_ffn_Wk, L1_ffn_bk, L1_ffn_Wv, L1_ffn_bv, L1_ffn_Wr, L1_ffn_br, L1_ffn_Wo, L1_ffn_bo, L1_ffn_ln_g, L1_ffn_ln_b):
    import jax
    import jax.numpy as jnp

    def _L0_conv_ref(x, in_proj_w, conv_w, conv_b, x_proj_w, dt_projs_w, dt_projs_b, A_logs, Ds, out_norm_g, out_norm_b, out_proj_w):
        import jax, jax.numpy as jnp
        import numpy as np
        B_, H_, W_, DM = (4, 16, 16, 192)
        DI = int(0.5 * DM)
        N = 16
        R = -(-DM // 16)
        K = 4

        def selective_scan(xs, dts, As, Bs, Cs, Dsk):
            u = jnp.moveaxis(xs, -1, 0)
            d = jnp.moveaxis(dts, -1, 0)
            Bt = jnp.moveaxis(Bs, -1, 0)
            Ct = jnp.moveaxis(Cs, -1, 0)

            def step(h, inp):
                u_t, d_t, B_t, C_t = inp
                dA = jnp.exp(d_t[..., None] * As)
                h = h * dA + (d_t * u_t)[..., None] * B_t[:, :, None, :]
                y = jnp.einsum('bkcn,bkn->bkc', h, C_t)
                return (h, y)
            h0 = jnp.zeros(u.shape[1:] + (As.shape[-1],), u.dtype)
            _, ys = jax.lax.scan(step, h0, (u, d, Bt, Ct))
            ys = jnp.moveaxis(ys, 0, -1)
            return ys + Dsk[None, :, :, None] * xs
        B, H, W, _ = x.shape
        L = H * W
        xz = x @ in_proj_w.T
        xh, z = jnp.split(xz, 2, axis=-1)
        xc = jnp.transpose(xh, (0, 3, 1, 2))
        xc = jax.lax.conv_general_dilated(xc, conv_w, (1, 1), 'SAME', feature_group_count=DI)
        xc = jax.nn.silu(xc + conv_b[None, :, None, None])
        x_flat = xc.reshape(B, DI, L)
        x_t = jnp.transpose(xc, (0, 1, 3, 2)).reshape(B, DI, L)
        x_hwwh = jnp.stack([x_flat, x_t], 1)
        xs = jnp.concatenate([x_hwwh, jnp.flip(x_hwwh, -1)], 1)
        x_dbl = jnp.einsum('bkdl,kcd->bkcl', xs, x_proj_w)
        dts, Bs, Cs = jnp.split(x_dbl, [R, R + N], axis=2)
        dts = jnp.einsum('bkrl,kdr->bkdl', dts, dt_projs_w)
        dts = jax.nn.softplus(dts + dt_projs_b[None, :, :, None])
        As = -jnp.exp(A_logs).reshape(K, DI, N)
        out_y = selective_scan(xs, dts, As, Bs, Cs, Ds.reshape(K, DI))
        inv_y = jnp.flip(out_y[:, 2:4], -1)
        wh_y = jnp.transpose(out_y[:, 1].reshape(B, DI, W, H), (0, 1, 3, 2)).reshape(B, DI, L)
        invwh_y = jnp.transpose(inv_y[:, 1].reshape(B, DI, W, H), (0, 1, 3, 2)).reshape(B, DI, L)
        y = out_y[:, 0] + inv_y[:, 0] + wh_y + invwh_y
        y = jnp.transpose(y, (0, 2, 1)).reshape(B, H, W, DI)
        mu = y.mean(-1, keepdims=True)
        var = y.var(-1, keepdims=True)
        y = (y - mu) / jnp.sqrt(var + 1e-05) * out_norm_g + out_norm_b
        y = y * jax.nn.silu(z)
        return y @ out_proj_w.T

    def _L1_attn_ref(x, w_qkv, b_qkv, w_proj, b_proj, projection):
        import jax, jax.numpy as jnp
        import numpy as np
        NUM_HEADS = 12
        KERNEL_EPS = 0.001

        def _performer_relu_attention(q, k, v, projection):
            d = q.shape[-1]
            data_normalizer = 1.0 / jnp.sqrt(jnp.sqrt(jnp.asarray(d, q.dtype)))
            qp = jax.nn.relu(jnp.einsum('bhnd,md->bhnm', q * data_normalizer, projection)) + KERNEL_EPS
            kp = jax.nn.relu(jnp.einsum('bhnd,md->bhnm', k * data_normalizer, projection)) + KERNEL_EPS
            k_sum = kp.sum(axis=2)
            d_inv = 1.0 / jnp.einsum('bhnm,bhm->bhn', qp, k_sum)
            context = jnp.einsum('bhnm,bhnd->bhmd', kp, v)
            out = jnp.einsum('bhnm,bhmd->bhnd', qp, context) * d_inv[..., None]
            return out
        B, N, C = x.shape
        H = NUM_HEADS
        d = C // H
        qkv = x @ w_qkv.T + b_qkv
        qkv = qkv.reshape(B, N, 3, H, d).transpose(0, 3, 2, 1, 4)
        q, k, v = (qkv[:, :, 0], qkv[:, :, 1], qkv[:, :, 2])
        out = _performer_relu_attention(q, k, v, projection)
        out = out.transpose(0, 2, 1, 3).reshape(B, N, C)
        return out @ w_proj.T + b_proj

    def _L1_ffn_ref(hidden_states, Wq, bq, Wk, bk, Wv, bv, Wr, br, Wo, bo, ln_g, ln_b):
        import jax, jax.numpy as jnp
        import numpy as np
        H = 12
        D = 16
        K = 6
        EPS = 1e-12
        B, S, hid = hidden_states.shape
        router_in = hidden_states.mean(axis=1)
        logits = router_in @ Wr + br
        _, top_idx = jax.lax.top_k(logits, K)
        hard = jax.nn.one_hot(top_idx, H, dtype=logits.dtype).sum(axis=1)
        head_mask = hard + logits - jax.lax.stop_gradient(logits)
        m = head_mask[:, :, None, None]

        def proj(W, b):
            return (hidden_states @ W + b).reshape(B, S, H, D).transpose(0, 2, 1, 3)
        q = proj(Wq, bq) * m
        k = proj(Wk, bk) * m
        v = proj(Wv, bv) * m
        scores = jnp.einsum('bhqd,bhkd->bhqk', q, k) / jnp.sqrt(jnp.float32(D))
        probs = jax.nn.softmax(scores, axis=-1)
        ctx = jnp.einsum('bhqk,bhkd->bhqd', probs, v)
        ctx = ctx.transpose(0, 2, 1, 3).reshape(B, S, hid)
        x = ctx @ Wo + bo + hidden_states
        mu = x.mean(axis=-1, keepdims=True)
        var = ((x - mu) ** 2).mean(axis=-1, keepdims=True)
        return (x - mu) / jnp.sqrt(var + EPS) * ln_g + ln_b

    def _gn(v, G=32, eps=1e-05):
        B_, H_, W_, C_ = v.shape
        g = v.reshape(B_, H_, W_, G, C_ // G)
        m = jnp.mean(g, axis=(1, 2, 4), keepdims=True)
        s = jnp.var(g, axis=(1, 2, 4), keepdims=True)
        return ((g - m) / jnp.sqrt(s + eps)).reshape(v.shape)

    def _ln_c(v, eps=1e-06):
        m = jnp.mean(v, axis=-1, keepdims=True)
        s = jnp.var(v, axis=-1, keepdims=True)
        return (v - m) / jnp.sqrt(s + eps)

    def _ln_t(v, eps=1e-05):
        m = jnp.mean(v, axis=-1, keepdims=True)
        s = jnp.var(v, axis=-1, keepdims=True)
        return (v - m) / jnp.sqrt(s + eps)

    def _to_tokens(v):
        B_, H_, W_, C_ = v.shape
        return v.reshape(B_, H_ * W_, C_)

    def _from_tokens(t, like):
        return t.reshape(like.shape)
    x = x + _L0_conv_ref(_gn(x), L0_conv_in_proj_w, L0_conv_conv_w, L0_conv_conv_b, L0_conv_x_proj_w, L0_conv_dt_projs_w, L0_conv_dt_projs_b, L0_conv_A_logs, L0_conv_Ds, L0_conv_out_norm_g, L0_conv_out_norm_b, L0_conv_out_proj_w)
    t = _to_tokens(x)
    t = t + _L1_attn_ref(_ln_t(t), L1_attn_w_qkv, L1_attn_b_qkv, L1_attn_w_proj, L1_attn_b_proj, L1_attn_projection)
    t = t + _L1_ffn_ref(_ln_t(t), L1_ffn_Wq, L1_ffn_bq, L1_ffn_Wk, L1_ffn_bk, L1_ffn_Wv, L1_ffn_bv, L1_ffn_Wr, L1_ffn_br, L1_ffn_Wo, L1_ffn_bo, L1_ffn_ln_g, L1_ffn_ln_b)
    x = _from_tokens(t, x)
    return x

_drawn_inputs = setup_inputs


def setup_inputs(seed=0):
    import zlib

    import numpy as np

    out = dict(_drawn_inputs(seed))
    spreads = {'L0_conv_conv_b': (0.0, 0.1),
     'L0_conv_Ds': (1.0, 0.6),
     'L0_conv_out_norm_g': (1.0, 0.6),
     'L0_conv_out_norm_b': (0.0, 0.8),
     'L1_attn_b_qkv': (0.0, 0.301),
     'L1_attn_b_proj': (0.0, 0.1),
     'L1_ffn_bq': (0.0, 0.8),
     'L1_ffn_bk': (0.0, 2.0),
     'L1_ffn_bv': (0.0, 0.8),
     'L1_ffn_br': (0.0, 0.8),
     'L1_ffn_bo': (0.0, 0.317),
     'L1_ffn_ln_g': (1.0, 0.2),
     'L1_ffn_ln_b': (0.0, 0.1)}
    factors = {'L0_conv_conv_w': 8.0,
     'L0_conv_x_proj_w': 64.0,
     'L0_conv_dt_projs_w': 64.0,
     'L0_conv_dt_projs_b': 200.0,
     'L0_conv_A_logs': 200.0,
     'L1_attn_w_qkv': 8.0,
     'L1_attn_projection': 8.0,
     'L1_ffn_Wq': 8.0,
     'L1_ffn_Wk': 8.0,
     'L1_ffn_Wv': 8.0,
     'L1_ffn_Wr': 8.0,
     'L1_ffn_Wo': 5.661}
    for name, (base, spread) in spreads.items():
        noise = np.random.default_rng([zlib.crc32(name.encode()), seed]).standard_normal(out[name].shape)
        drawn = base * np.exp(spread * noise) if base else spread * noise
        out[name] = jnp.asarray(drawn.astype(out[name].dtype))
    for name, factor in factors.items():
        out[name] = (out[name] * factor).astype(out[name].dtype)
    return out
```

```python
from contextlib import ExitStack

import concourse.bass as bass
from concourse import mybir

F32 = mybir.dt.float32
BF16 = mybir.dt.bfloat16
ALU = mybir.AluOpType
ACT = mybir.ActivationFunctionType
AX_X = mybir.AxisListType.X

P = 128
IMAGES, SIDE, CH = 4, 16, 192
L = SIDE * SIDE
HALVES = 2
IMG = IMAGES // HALVES
TOK = IMG * L
TILES = TOK // P
CK = CH // 2
DI, NS, RANK, DIRS = 96, 16, 12, 4
GRP = P // NS
UNITS = DI // GRP
CHUNK = 32
CHUNKS = DI // CHUNK
PER_CHUNK = CHUNK // GRP
XROWS = RANK + 2 * NS
GN_SIZE = CH // 32
HEADS, HD, FEAT, TOPK = 12, 16, 64, 6
HPC = CK // HD
PAIRS = HEADS // 2
KERNEL_EPS = 0.001
RING = 3
SLOTS = 3
Y_LAG = 3
SOFTPLUS_LINEAR = 40.0
SERIES_BELOW = 0.0025
LOG_MAX = 82.0

CONST2 = 3 + 1 + HPC + TOPK
ONES = 5


def ring_plan():
    def pre(h, k):
        return [f"d{h}{k}", f"B{h}{k}", f"C{h}{k}"]

    def merge(h):
        return [f"yT{h}", f"gT{h}", f"o{h}0", f"o{h}1"]

    def attn(h):
        return ([f"tT{h}0", f"tT{h}1"] + [f"q{h}{i}" for i in range(PAIRS)]
                + [f"kv{h}{t}{j}" for t in range(TILES) for j in range(2)] + [f"cx{h}{b}" for b in range(IMG)]
                + [f"at{h}{b}" for b in range(IMG)] + [f"aT{h}0", f"aT{h}1", f"p{h}0", f"p{h}1"])

    def ffn(h):
        out = [f"hT{h}0", f"hT{h}1", f"lg{h}", f"cr{h}"]
        for b in range(IMG):
            out += [f"wq{h}{b}", f"wk{h}{b}", f"wv{h}{b}", f"fq{h}{b}", f"fk{h}{b}", f"fv{h}{b}"]
            for j in range(TOPK + 2):
                out += [f"s{h}{b}{j}"] * (j < TOPK) + [f"pt{h}{b}{j - 1}"] * (0 < j <= TOPK) + [f"pv{h}{b}{j - 2}"] * (j > 1)
            out += [f"cT{h}{b}", f"fo{h}{b}"]
        return out

    names = ["w_in", "gm", "gv", "w_xp", "w_dt", "w_fold", "w_alog"]
    for h in range(HALVES):
        names += [f"xh{h}", f"z{h}", f"cv{h}"]
    names += ["w_out", "w_pbd"] + [f"w_qk{i}{rc}{c}" for i in range(2) for rc in range(2) for c in range(2)]
    names += ["w_v", "w_proj", "w_f0", "w_f1", "w_f2"]
    for k in range(DIRS):
        names += pre(0, k)
    for k in range(DIRS):
        names += pre(1, k)
    for h in range(HALVES):
        names += merge(h) + attn(h) + ffn(h)
    return {n: i for i, n in enumerate(names)}


def hybrid_kernel(nc, x, in_proj_w, conv_w, conv_b, x_proj_w, dt_w, dt_b, A_logs, Ds, norm_g, norm_b, out_proj_w,
                  w_qkv, b_qkv, w_proj, b_proj, projection, Wq, bq, Wk, bk, Wv, bv, Wr, br, Wo, bo, ln_g, ln_b, out):
    ring = ring_plan()
    x_d = x.rearrange("b h w c -> (b h w) c").rearrange("(t p) c -> p t c", p=P)
    out_d = out.rearrange("b h w c -> (b h w) c").rearrange("(t p) c -> p t c", p=P)

    with ExitStack() as ctx:
        ctx.enter_context(nc.allow_non_contiguous_dma(reason="small parameter vectors"))

        def sb(name, shape, dt=F32):
            return ctx.enter_context(nc.sbuf_tensor(name, shape, dt))

        def shared(name, *tenants):
            def words(shape, dt):
                n = 1
                for d in shape[1:]:
                    n *= d
                return n * (2 if dt == BF16 else 4) // 4
            room = sb(name, [P, max(sum(words(*t) for t in tenant) for tenant in tenants)])
            views = []
            for tenant in tenants:
                at = 0
                for shape, dt in tenant:
                    ap = room[0:shape[0], at:at + words(shape, dt)]
                    at += words(shape, dt)
                    if dt == BF16:
                        ap = ap.bitcast(BF16)
                    dims = "abcde"[:len(shape) - 1]
                    if len(dims) > 1:
                        ap = ap.rearrange(f"p ({' '.join(dims)}) -> p {' '.join(dims)}",
                                          **{d: shape[1 + i] for i, d in enumerate(dims)})
                    views.append(ap)
            return views

        def sem(name):
            return ctx.enter_context(nc.semaphore(name))

        step_bc = [ctx.enter_context(nc.psum_tensor(f"step_bc{i}", [P, TOK], F32)) for i in range(2)]
        inp_bc = [ctx.enter_context(nc.psum_tensor(f"inp_bc{i}", [P, TOK], F32)) for i in range(2)]
        y_acc = ctx.enter_context(nc.psum_tensor("y_acc", [P, TOK], F32))
        banks = [ctx.enter_context(nc.psum_tensor(f"ring{i}", [P, TOK], F32)) for i in range(RING)]

        def bank(name):
            return banks[ring[name] % RING]

        x_tok = sb("x_tok", [P, HALVES * TILES, CH])
        opw = sb("opw", [CK, 2, DI])
        cw = sb("cw", [DI, 9])
        cb = sb("cb", [DI, 2])
        dtb = sb("dtb", [DI, DIRS])
        dsk = sb("dsk", [DI, DIRS])
        gb = sb("gb", [P, 4, CH])
        proj = sb("proj", [FEAT, HD])
        wr = sb("wr", [CK + 1, 2, HEADS])
        wo = sb("wo", [CK, 2, CH])
        ident = sb("ident", [P, P])
        avg6 = sb("avg6", [CK, CK])
        band = sb("band", [P, 2 * DI - GRP])
        spread = sb("spread", [DI, PER_CHUNK, P], BF16)
        dmatch = sb("dmatch", [CK, 2 * HD])
        tri = sb("tri", [IMG, HEADS, HEADS])
        slot_no = sb("slot_no", [CK, TOPK])
        neg_half = sb("neg_half", [P, 8])
        xpT = sb("xpT", [DI, DIRS, XROWS])
        cur_w = sb("cur_w", [DI, DI + 2 * P])
        a_log = sb("a_log", [P, DIRS * UNITS])
        a_neg = sb("a_neg", [P, DIRS * UNITS])
        outT = sb("outT", [DI, CH])
        dsum = sb("dsum", [DI, 1])
        qw = sb("qw", [CK + 1, 2, HEADS * FEAT])
        kvw = sb("kvw", [CK + 1, 2, 2, HPC * FEAT + CK])
        pjT = sb("pjT", [CK + 1, 2, CH])
        fT = sb("fT", [CK, 3, 2, CH + 1])
        qkvw, pjw, fw, kp = shared("room_a", [([CK, 6, CH + 1], F32), ([CK, 2, CH + 1], F32), ([CK, 3, 2, CH], F32)],
                                   [([P, TILES, HEADS * FEAT], F32)])
        xnT, irep, prep, pmask, qp, gt, eq, eqt, valr, wsv, cx = shared("room_b", [([CK, 2, HALVES * TOK], F32), ([FEAT, HPC, FEAT], F32),
                                                       ([FEAT, HPC, HD], F32), ([CK, HPC, FEAT], F32)],
                                            [([P, PAIRS, TOK], F32)],
                                            [([IMG, HEADS, HEADS], F32)] * 3 + [([IMG, 3 * HEADS, HD], F32), ([CK + 1, 2, CK], F32),
                                                                               ([P, 2, CK], F32)])
        spl, spe, sps, step2, hi, mid, lo, prob, probT, sel_m, sel_u, wsel = shared(
            "room_c", [([DI, TOK], F32)] * 3 + [([DI, 2, TOK], F32), ([DI, 2, TOK], BF16),
                       ([DI, 2, TOK], BF16), ([DI, 2, TOK], BF16)],
            [([P, 2, 2, L], F32), ([P, 2, 2, L], F32), ([CK, IMG, 2, TOPK, 2 * HD], F32), ([CK, IMG, 2, TOPK, HD], F32),
             ([CK + 1, 2, 2, TOPK * 2 * HD], F32)])
        pre_w, fq, fk, fv = shared("room_d", [([DI, DIRS, DI + 2 * P], F32)],
                                   [([P, 2, L], F32), ([P, 2, L], F32), ([P, 2, CK], F32)])
        taps, hn = shared("room_e", [([DI, 9, DI], F32)], [([P, TILES, CH], F32)])
        inT, dtT, ze, yn = shared("room_f", [([CK, 2, CH], F32), ([RANK, DIRS, DI], F32)],
                                  [([P, TILES, DI], F32), ([P, TILES, DI], F32)])
        inw, xpw, dtw, alog, tn = shared("room_h", [([DI, 2, CH], F32), ([XROWS, DIRS, DI], F32), ([DI, DIRS, RANK], F32),
                                                    ([DIRS * UNITS, P], F32)], [([P, TILES, CH], F32)])
        sg, gT = shared("room_i", [([DI, TOK], F32)], [([DI, TOK], F32)])
        pbd, cT = shared("room_j", [([CK, HPC * FEAT], F32)], [([CK + 1, L], F32)])
        (xs_room,) = shared("room_g", [([P, HALVES, DIRS, TOK], F32)])
        xs = xs_room[0:DI]
        later = xs_room[:, 0, 1:DIRS, :].rearrange("p k t -> p (k t)")
        n = TILES * CH
        ao = res = later[:, 0:n].rearrange("p (t c) -> p t c", t=TILES)
        fin = later[:, n:2 * n].rearrange("p (t c) -> p t c", t=TILES)
        gst = sb("gst", [CK, 2 * IMAGES, 6])
        gmv = sb("gmv", [CK, 2 * IMAGES, 2])
        gdv = sb("gdv", [CK, 2 * IMAGES])
        gmean = sb("gmean", [CK, 2 * IMAGES])
        gva = sb("gva", [CK, 2 * IMAGES])
        gve = sb("gve", [CK, 2 * IMAGES])
        gsq = sb("gsq", [CK, 2 * IMAGES])
        grs = sb("grs", [CK, 2 * IMAGES])
        gbi = sb("gbi", [CK, 2 * IMAGES])
        xpad = sb("xpad", [DI, IMG, SIDE + 2, SIDE + 2])
        z = sb("z", [P, HALVES, TILES, DI])
        stack = sb("stack", [DI, DIRS, CHUNKS, 2 * TOK], BF16)
        b_rep = sb("b_rep", [P, DIRS, TOK])
        c_rep = sb("c_rep", [P, DIRS, TOK])
        decay = sb("decay", [P, SLOTS, IMG, L])
        drive = sb("drive", [P, SLOTS, TOK])
        state = sb("state", [P, SLOTS, TOK])
        outp = sb("outp", [P, SLOTS, TOK])
        y_dir = sb("y_dir", [DI, DIRS, TOK])
        y_sum = sb("y_sum", [DI, HALVES, TOK])
        mst = sb("mst", [P, 4, TILES, 6])
        mv = sb("mv", [P, 4, TILES, 2])
        rs = sb("rs", [P, 4, TILES])
        tT = sb("tT", [CK + 1, 2, TOK])
        aT = hT = tT
        v1 = sb("v1", [P, TILES, HEADS, HD + 1])
        cbd = sb("cbd", [P, IMG, PAIRS, 2 * (HD + 1)])
        arec = sb("arec", [P, TILES, HEADS])
        rin = sb("rin", [CK + 1, 2, IMG])
        lg = sb("lg", [IMG, HEADS])
        rank = sb("rank", [IMG, HEADS])
        val = sb("val", [IMG, 3, HEADS])
        msum = sb("msum", [IMG, HEADS])
        col = sb("col", [CK, 3, 2, IMG])
        hot = sb("hot", [CK, 2, 2, IMG, TOPK])
        wos = sb("wos", [CK + 1, CH])
        nmax = sb("nmax", [P, 2, 2])
        nmaxs = sb("nmaxs", [P, 2, 2])
        psum_row = sb("psum_row", [P, 2, 2])
        prec = sb("prec", [P, 2, 2])

        gn_banks = [step_bc[0], step_bc[1], inp_bc[0], inp_bc[1]]
        S = {n: sem("s_" + n) for n in (
            "w_in w_xp w_alog w_small w_gb w_qkv w_proj w_ffn w_wo w_bo zeroed const const2 ones ident filled dup repl taps small neg_a "
            "gn_turned gn_stats gn_dev gn_var gn_eps gn_rsqrt gn_bias xn padded gate_e conv_e conv_s xs0 xs "
            "cur a_exp sp_t sp_s sp_l sp_max sp_in sp_exp sp_ln step hi rest mid lo stack bc_step bc_inp decay drive state outp y_mm y_ev y_part y_sum "
            "stat_y agg_y eps_y rsqrt_y norm_y gated gate stat_t agg_t eps_t rsqrt_t norm_t key ctx_lo a_rec att "
            "stat_u agg_u eps_u rsqrt_u norm_u router_in logit_eq rank slot_of vals val_rows hot sel prob_max prob_bias prob "
            "prob_rec stat_r agg_r eps_r rsqrt_r norm_r affine fin outd"
        ).split()}
        S["x"] = [sem(f"s_x{h}") for h in range(HALVES)]
        free = [sem(f"s_free{i}") for i in range(RING)]

        def fetched(eng, name, more=0):
            eng.wait_ge(S["filled"], ring[name] + 1 + more)

        def reuse(eng, name, more=0):
            i = ring[name]
            if i >= RING:
                eng.wait_ge(free[i % RING], i // RING + more)

        def taken(eng, name, more=0):
            eng.wait_ge(freed(name), ring[name] // RING + 1 + more)

        def freed(name):
            return free[ring[name] % RING]

        block = ctx.enter_context(nc.Block())

        @block.sync
        def _(sp):
            for h in range(HALVES):
                sp.dma_start(x_tok[:, h * TILES:(h + 1) * TILES, :], x_d[:, h * TILES:(h + 1) * TILES, :]).then_inc(S["x"][h], 16)
            sp.dma_start(inw[:], in_proj_w.rearrange("(o p) c -> p o c", p=DI)).then_inc(S["w_in"], 16)
            sp.dma_start(xpw[:], x_proj_w.rearrange("k r c -> r k c")).then_inc(S["w_xp"], 16)
            sp.dma_start(dtw[:], dt_w.rearrange("k c r -> c k r")).then_inc(S["w_xp"], 16)
            sp.dma_start(alog[:], A_logs.rearrange("(g c) n -> g (c n)", c=GRP)).then_inc(S["w_alog"], 16)
            sp.dma_start(cw[:], conv_w.rearrange("c a y x -> c (a y x)")).then_inc(S["w_small"], 16)
            sp.dma_start(cb[:, 0:1], conv_b.rearrange("(c a) -> c a", a=1)).then_inc(S["w_small"], 16)
            sp.dma_start(dtb[:], dt_b.rearrange("k c -> c k")).then_inc(S["w_small"], 16)
            sp.dma_start(dsk[:], Ds.rearrange("(k c) -> c k", c=DI)).then_inc(S["w_small"], 16)
            sp.dma_start(opw[:], out_proj_w.rearrange("(o p) c -> p o c", p=CK)).then_inc(S["w_in"], 16)
            for i, v in enumerate((norm_g, norm_b)):
                sp.dma_start(gb[:, i, 0:DI], v.rearrange("(a c) -> a c", a=1).to_broadcast([P, DI])).then_inc(S["w_gb"], 16)
            for i, v in enumerate((ln_g, ln_b)):
                sp.dma_start(gb[:, 2 + i, :], v.rearrange("(a c) -> a c", a=1).to_broadcast([P, CH])).then_inc(S["w_gb"], 16)
            sp.dma_start(qkvw[:, :, 0:CH], w_qkv.rearrange("(o p) c -> p o c", p=CK)).then_inc(S["w_qkv"], 16)
            sp.dma_start(qkvw[:, :, CH], b_qkv.rearrange("(o p) -> p o", p=CK)).then_inc(S["w_qkv"], 16)
            sp.dma_start(proj[:], projection).then_inc(S["w_qkv"], 16)
            sp.dma_start(pjw[:, :, 0:CH], w_proj.rearrange("(o p) c -> p o c", p=CK)).then_inc(S["w_proj"], 16)
            sp.dma_start(pjw[:, :, CH], b_proj.rearrange("(o p) -> p o", p=CK)).then_inc(S["w_proj"], 16)
            for i, (w, b) in enumerate(((Wq, bq), (Wk, bk), (Wv, bv))):
                sp.dma_start(fw[:, i, :, :], w.rearrange("(o p) c -> p o c", p=CK)).then_inc(S["w_ffn"], 16)
                sp.dma_start(fT[:, i, :, CH], b.rearrange("(o p) -> p o", p=CK)).then_inc(S["w_ffn"], 16)
            sp.dma_start(wr[0:CK, :, :], Wr.rearrange("(o p) c -> p o c", p=CK)).then_inc(S["w_wo"], 16)
            sp.dma_start(wr[CK:CK + 1, 1, :], br.rearrange("(a c) -> a c", a=1)).then_inc(S["w_wo"], 16)
            sp.dma_start(wo[:], Wo.rearrange("(o p) c -> p o c", p=CK)).then_inc(S["w_wo"], 16)
            sp.dma_start(wos[CK:CK + 1, :], bo.rearrange("(a c) -> a c", a=1)).then_inc(S["w_bo"], 16)

            def restack(n, k, unit_base):
                if unit_base is not None:
                    sp.wait_ge(S["bc_inp"], unit_base)
                for part, (src, s) in enumerate(((hi, "hi"), (mid, "mid"), (lo, "lo"))):
                    sp.wait_ge(S[s], n + 1)
                    for j in range(CHUNKS):
                        sp.dma_start(stack[CHUNK * part:CHUNK * (part + 1), k, j, :],
                                     src[CHUNK * j:CHUNK * (j + 1), :, :]).then_inc(S["stack"], 16)
            for k in range(DIRS):
                restack(k, k, None)
            for k in range(DIRS):
                restack(DIRS + k, k, UNITS * (k + 1))
            for h in range(HALVES):
                for t in range(TILES):
                    sp.wait_ge(S["fin"], h * TILES + t + 1)
                    sp.dma_start(out_d[:, h * TILES + t, :], fin[:, t, :]).then_inc(S["outd"], 16)
            sp.wait_ge(S["outd"], 16 * HALVES * TILES)

        @block.gpsimd
        def _(pool):
            g = nc.gpsimd
            g.memset(ident[:], 0.0).then_inc(S["zeroed"], 1)
            g.memset(avg6[:], 1.0 / GN_SIZE).then_inc(S["zeroed"], 1)
            g.memset(pmask[:], 1.0).then_inc(S["zeroed"], 1)
            g.memset(band[:], 1.0).then_inc(S["zeroed"], 1)
            g.memset(spread[:], 0.0).then_inc(S["zeroed"], 1)
            g.memset(dmatch[:], 0.0).then_inc(S["zeroed"], 1)
            g.memset(tri[:], 1.0).then_inc(S["zeroed"], 1)
            pool.wait_ge(S["zeroed"], 7)
            g.affine_select(out=ident[:], in_=ident[:], pattern=[[-1, P]], compare_op=ALU.not_equal, fill=1.0,
                            base=0, channel_multiplier=1).then_inc(S["ident"], 1)
            avg = avg6[:].rearrange("p (g e) -> p g e", e=GN_SIZE)
            groups = CK // GN_SIZE
            at = NS * (DI - GRP)
            g.affine_select(out=avg, in_=avg, pattern=[[-GN_SIZE, groups], [0, GN_SIZE]], compare_op=ALU.is_ge,
                            fill=0.0, base=0, channel_multiplier=1).then_inc(S["const"], 1)
            g.affine_select(out=pmask[:], in_=pmask[:], pattern=[[-HD, HPC], [0, FEAT]], compare_op=ALU.is_ge,
                            fill=0.0, base=0, channel_multiplier=1).then_inc(S["const"], 1)
            g.affine_select(out=band[:], in_=band[:], pattern=[[-NS, 2 * DI - GRP]], compare_op=ALU.is_ge,
                            fill=0.0, base=at, channel_multiplier=1).then_inc(S["const"], 1)
            pool.wait_ge(S["const"], 3)
            g.affine_select(out=avg, in_=avg, pattern=[[GN_SIZE, groups], [0, GN_SIZE]], compare_op=ALU.is_ge,
                            fill=0.0, base=GN_SIZE - 1, channel_multiplier=-1).then_inc(S["const"], 1)
            g.affine_select(out=pmask[:], in_=pmask[:], pattern=[[HD, HPC], [0, FEAT]], compare_op=ALU.is_ge,
                            fill=0.0, base=HD - 1, channel_multiplier=-1).then_inc(S["const"], 1)
            g.affine_select(out=band[:], in_=band[:], pattern=[[NS, 2 * DI - GRP]], compare_op=ALU.is_ge,
                            fill=0.0, base=NS - 1 - at, channel_multiplier=-1).then_inc(S["const"], 1)
            g.memset(neg_half[:], -0.5).then_inc(S["const"], 1)
            g.memset(xpad[:], 0.0).then_inc(S["const"], 1)

            def inv_sqrt(dst, src, ready, count, done):
                pool.wait_ge(S[ready], count)
                g.tensor_tensor(dst, src, neg_half[0:dst.shape[0], 0:dst.shape[1]], ALU.pow).then_inc(S[done], 1)

            pool.wait_ge(S["ident"], 1)
            pool.wait_ge(S["w_small"], 64)
            for i in range(9):
                g.tensor_scalar(taps[:, i, :], ident[0:DI, 0:DI], cw[:, i:i + 1], None, ALU.mult).then_inc(S["taps"], 1)
            pool.wait_ge(S["const"], 8)
            inv_sqrt(grs[:], gve[:], "gn_eps", 1, "gn_rsqrt")
            sel_s = spread[:].rearrange("p q (c n) -> p q c n", n=NS)
            for part in range(3):
                g.affine_select(out=sel_s, in_=sel_s, pattern=[[-GRP, PER_CHUNK], [-1, GRP], [0, NS]],
                                compare_op=ALU.not_equal, fill=1.0, base=-CHUNK * part,
                                channel_multiplier=1).then_inc(S["const2"], 1)
                pool.wait_ge(S["const2"], part + 1)
            g.affine_select(out=tri[:], in_=tri[:], pattern=[[1, HEADS], [-1, HEADS]], compare_op=ALU.is_gt,
                            fill=0.0, base=0, channel_multiplier=0).then_inc(S["const2"], 1)
            for i in range(HPC):
                g.affine_select(out=dmatch[:, 0:HD], in_=dmatch[:, 0:HD], pattern=[[-1, HD]], compare_op=ALU.not_equal,
                                fill=1.0, base=-HD * i, channel_multiplier=1).then_inc(S["const2"], 1)
                pool.wait_ge(S["const2"], 5 + i)
            for j in range(TOPK):
                g.memset(slot_no[:, j:j + 1], float(j)).then_inc(S["const2"], 1)

            for h in range(HALVES):
                pool.wait_ge(freed(f"cv{h}"), ring[f"cv{h}"] // RING + 1)
                grid = xs[:, h, 0, :].rearrange("p (b y x) -> p b x y", b=IMG, x=SIDE)
                rows = xs[:, h, 0, :].rearrange("p (b l) -> p b l", b=IMG)
                for b in range(IMG):
                    g.tensor_copy(xs[:, h, 1, b * L:(b + 1) * L].rearrange("p (x y) -> p x y", x=SIDE),
                                  grid[:, b, :, :]).then_inc(S["xs"], 1)
                g.tensor_copy(xs[:, h, 2, :].rearrange("p (b l) -> p b l", b=IMG), rows[:, :, ::-1]).then_inc(S["xs"], 1)
                for b in range(IMG):
                    g.tensor_copy(xs[:, h, 3, b * L:(b + 1) * L].rearrange("p (x y) -> p x y", x=SIDE),
                                  grid[:, b, ::-1, ::-1]).then_inc(S["xs"], 1)

            def series(n):
                pool.wait_ge(S["sp_exp"], n + 1)
                g.tensor_scalar(sps[:], spe[:], -0.5, 1.0, ALU.mult, ALU.add).then_inc(S["sp_t"], 1)
                if n > 0:
                    pool.wait_ge(S["sp_max"], n)
                pool.wait_ge(S["sp_t"], n + 1)
                g.tensor_tensor(sps[:], sps[:], spe[:], ALU.mult).then_inc(S["sp_s"], 1)

            def left_of_hi(n):
                pool.wait_ge(S["hi"], n + 1)
                g.tensor_tensor(step2[:], step2[:], hi[:], ALU.subtract).then_inc(S["rest"], 1)

            def left_of_mid(n):
                pool.wait_ge(S["mid"], n + 1)
                g.tensor_tensor(lo[:], step2[:], mid[:], ALU.subtract).then_inc(S["lo"], 1)

            def weigh(n, k, g12):
                pool.wait_ge(S["state"], n + 1)
                if n >= SLOTS:
                    pool.wait_ge(S["y_mm"], n - SLOTS + 1)
                g.tensor_tensor(outp[:, g12 % SLOTS, :], state[:, g12 % SLOTS, :], c_rep[:, k, :],
                                ALU.mult).then_inc(S["outp"], 1)

            for k in range(DIRS):
                series(k)
                left_of_hi(k)
                left_of_mid(k)
            taken(pool, "C00", DIRS - 1)
            for g12 in range(UNITS):
                weigh(g12, 0, g12)
            for k in range(1, DIRS):
                for g12 in range(UNITS):
                    weigh(UNITS * k + g12, k, g12)
                    if g12 == 3:
                        series(DIRS + k - 1)
                    if g12 == 7:
                        left_of_hi(DIRS + k - 1)
                    if g12 == 10:
                        left_of_mid(DIRS + k - 1)
            for k in range(DIRS):
                taken(pool, "C10", k)
                for g12 in range(UNITS):
                    weigh(UNITS * (DIRS + k) + g12, k, g12)
                    if k == 0 and g12 == 3:
                        series(2 * DIRS - 1)
                    if k == 0 and g12 == 7:
                        left_of_hi(2 * DIRS - 1)
                    if k == 0 and g12 == 10:
                        left_of_mid(2 * DIRS - 1)
            for h in range(HALVES):
                inv_sqrt(rs[:, 0, :], mv[:, 0, :, 1], "eps_y", h + 1, "rsqrt_y")
                inv_sqrt(rs[:, 1, :], mv[:, 1, :, 1], "eps_t", h + 1, "rsqrt_t")
                inv_sqrt(rs[:, 2, :], mv[:, 2, :, 1], "eps_u", h + 1, "rsqrt_u")
                taken(pool, f"cr{h}")
                for b in range(IMG):
                    for i in range(2):
                        for u, w in ((0, 1), (1, 2)):
                            g.tensor_scalar(hot[:, u, i, b, :], slot_no[:], col[:, 0, i, b:b + 1], col[:, w, i, b:b + 1],
                                            ALU.is_equal, ALU.mult).then_inc(S["hot"], 1)
                pool.wait_ge(S["hot"], 8 * (h + 1))
                if h:
                    fetched(pool, f"wv{h - 1}{IMG - 1}")
                for b in range(IMG):
                    for i in range(2):
                        g.tensor_tensor(sel_m[:, b, i, :, :], dmatch[:].unsqueeze(1).to_broadcast([CK, TOPK, 2 * HD]),
                                        hot[:, 0, i, b, :].unsqueeze(2).to_broadcast([CK, TOPK, 2 * HD]), ALU.mult).then_inc(S["sel"], 1)
                        g.tensor_tensor(sel_u[:, b, i, :, :], dmatch[:, 0:HD].unsqueeze(1).to_broadcast([CK, TOPK, HD]),
                                        hot[:, 1, i, b, :].unsqueeze(2).to_broadcast([CK, TOPK, HD]), ALU.mult).then_inc(S["sel"], 1)
                inv_sqrt(rs[:, 3, :], mv[:, 3, :, 1], "eps_r", h + 1, "rsqrt_r")

        @block.scalar
        def _(act):
            a = nc.scalar

            def evac(name, *copies):
                fetched(act, name)
                for dst, src in copies:
                    ins = a.copy(dst, src)
                ins.then_inc(freed(name), 1)

            evac("w_in", (inT[:].rearrange("p a b -> p (a b)"), bank("w_in")[0:CK, 0:2 * CH]))
            act.wait_ge(S["gn_bias"], 1)
            for h in range(HALVES):
                for c in range(2):
                    for b in range(IMG):
                        s = c * IMAGES + h * IMG + b
                        a.activation(xnT[:, c, h * TOK + b * L:h * TOK + (b + 1) * L],
                                     gn_banks[2 * h + c][0:CK, b * L:(b + 1) * L],
                                     ACT.Identity, bias=gbi[:, s:s + 1], scale=grs[:, s:s + 1]).then_inc(S["xn"], 1)
            src = bank("w_xp")[0:DI, 0:DIRS * XROWS].rearrange("p (k r) -> p k r", k=DIRS)
            evac("w_xp", *[(pre_w[:, k, DI + i * P:DI + (i + 1) * P].rearrange("p (c n) -> p c n", n=NS),
                            src[:, k, RANK + NS * i:RANK + NS * (i + 1)].unsqueeze(1).to_broadcast([DI, GRP, NS]))
                           for i in range(2) for k in range(DIRS)])
            evac("w_dt", (dtT[:].rearrange("p a b -> p (a b)"), bank("w_dt")[0:RANK, 0:DIRS * DI]))
            evac("w_fold", (pre_w[:, :, 0:DI], bank("w_fold")[0:DI, 0:DIRS * DI].rearrange("p (k c) -> p k c", k=DIRS)))
            taken(act, "w_alog")
            a.activation(a_neg[:], a_log[:], ACT.Exp).then_inc(S["a_exp"], 1)

            act.wait_ge(S["const"], 8)
            act.wait_ge(S["small"], 2)
            for h in range(HALVES):
                if h:
                    fetched(act, f"cv{h - 1}")
                evac(f"xh{h}", *[(xpad[:, b, 1:SIDE + 1, 1:SIDE + 1],
                                  bank(f"xh{h}")[0:DI, b * L:(b + 1) * L].rearrange("p (y x) -> p y x", y=SIDE))
                                 for b in range(IMG)])
                evac(f"z{h}", (z[:, h, :, :], bank(f"z{h}")[:, 0:TILES * DI].rearrange("p (t c) -> p t c", t=TILES)))
                if h:
                    taken(act, f"cv{h - 1}")
                fetched(act, f"cv{h}")
                a.activation(sg[:], bank(f"cv{h}")[0:DI, :], ACT.Exp, bias=cb[:, 1:2], scale=-1.0).then_inc(S["conv_e"], 1)

            evac("w_out", (outT[:], bank("w_out")[0:DI, 0:CH]))
            for i in range(2):
                for rc in range(2):
                    for c in range(2):
                        rows, n, name = CK + c, HPC * FEAT, f"w_qk{i}{rc}{c}"
                        dst = qw[0:rows, c, rc * n:(rc + 1) * n] if i == 0 else kvw[0:rows, c, rc, 0:n]
                        evac(name, (dst, bank(name)[0:rows, 0:n]))
            for name, dsts in (("w_v", [kvw[0:CK + c, c, :, HPC * FEAT:] for c in range(2)]),
                               ("w_proj", [pjT[0:CK + c, c, :].rearrange("p (o k) -> p o k", o=2) for c in range(2)])):
                srcs = bank(name)[:, 0:2 * CH].rearrange("p (c o k) -> p c o k", c=2, o=2)
                evac(name, *[(dsts[c], srcs[0:CK + c, c, :, :]) for c in range(2)])
            for i in range(3):
                name = f"w_f{i}"
                evac(name, (fT[:, i, :, 0:CH], bank(name)[0:CK, 0:2 * CH].rearrange("p (o k) -> p o k", o=2)))

            def pre_weights(n, k):
                if n > 0:
                    fetched(act, "C00", 3 * (n - 1))
                a.copy(cur_w[:], pre_w[:, k, :]).then_inc(S["cur"], 1)

            def pre_softplus(n):
                act.wait_ge(S["sp_in"], n + 1)
                if n > 0:
                    act.wait_ge(S["sp_s"], n)
                a.activation(spe[:], spl[:], ACT.Exp).then_inc(S["sp_exp"], 1)
                act.wait_ge(S["sp_exp"], n + 1)
                a.activation(spl[:], spe[:], ACT.Ln, bias=1.0).then_inc(S["sp_ln"], 1)

            def pre_bc(h, k, used):
                for name, dst, gone in ((f"B{h}0", b_rep, "drive"), (f"C{h}0", c_rep, "outp")):
                    fetched(act, name, 3 * k)
                    if used is not None:
                        act.wait_ge(S[gone], used)
                    a.copy(dst[:, k, :], bank(name)[:, :]).then_inc(freed(name), 1)

            def pre_hi(n):
                act.wait_ge(S["step"], n + 1)
                if n > 0:
                    act.wait_ge(S["stack"], 16 * 9 * n)
                a.copy(hi[:], step2[:]).then_inc(S["hi"], 1)

            def pre_mid(n):
                act.wait_ge(S["rest"], n + 1)
                a.copy(mid[:], step2[:]).then_inc(S["mid"], 1)

            def expo(n, k, g12):
                act.wait_ge(S["bc_step"], n + 1)
                if n >= SLOTS:
                    act.wait_ge(S["state"], n - SLOTS + 1)
                a.activation(decay[:, g12 % SLOTS, :, 1:L],
                             step_bc[g12 % 2][:, :].rearrange("p (b l) -> p b l", b=IMG)[:, :, 1:L],
                             ACT.Exp, scale=a_neg[:, k * UNITS + g12:k * UNITS + g12 + 1]).then_inc(S["decay"], 1)

            def keep_y(n, k):
                act.wait_ge(S["y_mm"], UNITS * (n + 1))
                a.copy(y_dir[:, k, :], y_acc[0:DI, :]).then_inc(S["y_ev"], 1)

            def between(n, k, g12):
                if g12 == 0:
                    pre_weights(n, k)
                if g12 == 4:
                    pre_bc(1, k, UNITS * (k + 1))
                    pre_softplus(n)
                if g12 == 7:
                    pre_hi(n)
                if g12 == 9:
                    pre_mid(n)

            for k in range(DIRS):
                pre_weights(k, k)
                pre_softplus(k)
                pre_bc(0, k, None)
                pre_hi(k)
                pre_mid(k)
            act.wait_ge(S["neg_a"], 1)
            act.wait_ge(S["ones"], ONES)
            for g12 in range(UNITS):
                expo(g12, 0, g12)
            for k in range(1, DIRS):
                for g12 in range(UNITS):
                    expo(UNITS * k + g12, k, g12)
                    if g12 == 3:
                        keep_y(k - 1, k - 1)
                    between(DIRS + k - 1, k - 1, g12)
            for k in range(DIRS):
                for g12 in range(UNITS):
                    expo(UNITS * (DIRS + k) + g12, k, g12)
                    if g12 == 3:
                        if k == 1:
                            act.wait_ge(S["y_sum"], 1)
                        keep_y(DIRS + k - 1, (k - 1) % DIRS)
                    if k == 0:
                        between(2 * DIRS - 1, DIRS - 1, g12)
            keep_y(2 * DIRS - 1, DIRS - 1)

            for h in range(HALVES):
                if h:
                    act.wait_ge(S["gate"], h)
                a.activation(ze[:], z[:, h, :, :], ACT.Exp, scale=-1.0).then_inc(S["gate_e"], 1)
                evac(f"gT{h}", (gT[:], bank(f"gT{h}")[0:DI, :]))
                for c in range(2):
                    evac(f"tT{h}{c}", (tT[0:CK, c, :], bank(f"tT{h}{c}")[0:CK, :]))
                for c in range(2):
                    evac(f"aT{h}{c}", (aT[0:CK, c, :], bank(f"aT{h}{c}")[0:CK, :]))
                for c in range(2):
                    evac(f"hT{h}{c}", (hT[0:CK, c, :], bank(f"hT{h}{c}")[0:CK, :]))
                for b in range(IMG):
                    n = h * IMG + b
                    if n:
                        fetched(act, f"fo{(n - 1) // IMG}{(n - 1) % IMG}")
                    for i, w in enumerate("qk"):
                        src = bank(f"w{w}{h}{b}")[:, 0:2 * CH].rearrange("p (c k) -> p c k", c=2)
                        evac(f"w{w}{h}{b}", (wsel[0:CK, i, 0, :], src[0:CK, 0, :]), (wsel[0:CK + 1, i, 1, :], src[0:CK + 1, 1, :]))
                    src = bank(f"wv{h}{b}")
                    if n == 0:
                        act.wait_ge(S["w_bo"], 16)
                    evac(f"wv{h}{b}", (wsv[0:CK, 0, :], src[0:CK, 0:CK]), (wsv[0:CK + 1, 1, :], src[0:CK + 1, CK:2 * CK]),
                         (wos[0:CK, :], src[0:CK, CH:2 * CH]))
                    for w, dst in (("q", fq), ("k", fk)):
                        src = bank(f"f{w}{h}{b}")
                        evac(f"f{w}{h}{b}", (dst[:, 0, :], src[:, 0:L]), (dst[0:64, 1, :], src[0:64, L:2 * L]))
                    evac(f"fv{h}{b}", (fv[:].rearrange("p a b -> p (a b)"), bank(f"fv{h}{b}")[:, 0:2 * CK]))
                    for j in range(TOPK):
                        m = n * TOPK + j
                        name = f"s{h}{b}{j}"
                        act.wait_ge(S["prob_bias"], m + 1)
                        if m >= 2:
                            fetched(act, f"pt{(m - 2) // (TOPK * IMG)}{(m - 2) // TOPK % IMG}{(m - 2) % TOPK}")
                            act.wait_ge(S["prob_rec"], m - 1)
                        for q in range(2):
                            ins = a.activation(prob[:, m % 2, q, :], bank(name)[:, q * L:(q + 1) * L], ACT.Exp,
                                               bias=nmaxs[:, m % 2, q:q + 1], scale=HD ** -0.5,
                                               accum_out=psum_row[:, m % 2, q:q + 1])
                            ins.then_inc(S["prob"] if q == 0 else freed(name), 1)

        @block.vector
        def _(dve):
            v = nc.vector

            v.memset(decay[:], 0.0).then_inc(S["ones"], 1)
            v.memset(tT[CK:CK + 1, :, :], 1.0).then_inc(S["ones"], 1)
            v.memset(cT[CK:CK + 1, :], 1.0).then_inc(S["ones"], 1)
            v.memset(v1[:, :, :, HD:HD + 1], 1.0).then_inc(S["ones"], 1)
            v.memset(cbd[:], 0.0).then_inc(S["ones"], 1)

            for i in range(4):
                h, c = i // 2, i % 2
                dve.wait_ge(S["gn_turned"], i + 1)
                for b in range(IMG):
                    v.bn_stats(gst[:, c * IMAGES + h * IMG + b, :], gn_banks[i][0:CK, b * L:(b + 1) * L]).then_inc(S["gn_stats"], 1)
            dve.wait_ge(S["gn_stats"], 8)
            for s in range(8):
                v.bn_aggr(gmv[:, s, :], gst[:, s, :]).then_inc(S["gn_stats"], 1)
            fetched(dve, "gm")
            dve.wait_ge(S["gn_stats"], 16)
            v.tensor_copy(gmean[:], bank("gm")[0:CK, 0:8]).then_inc(freed("gm"), 1)
            taken(dve, "gm")
            v.tensor_tensor(gdv[:], gmv[:, :, 0], gmean[:], ALU.subtract).then_inc(S["gn_dev"], 1)
            dve.wait_ge(S["gn_dev"], 1)
            v.tensor_tensor(gsq[:], gdv[:], gdv[:], ALU.mult).then_inc(S["gn_dev"], 1)
            dve.wait_ge(S["gn_dev"], 2)
            v.tensor_tensor(gva[:], gsq[:], gmv[:, :, 1], ALU.add).then_inc(S["gn_var"], 1)
            fetched(dve, "gv")
            v.tensor_scalar(gve[:], bank("gv")[0:CK, 0:8], 1e-5, None, ALU.add).then_inc(freed("gv"), 1)
            taken(dve, "gv")
            v.tensor_scalar(gmean[:], gmean[:], -1.0, None, ALU.mult).then_inc(S["gn_eps"], 1)
            dve.wait_ge(S["gn_rsqrt"], 1)
            v.tensor_tensor(gbi[:], gmean[:], grs[:], ALU.mult).then_inc(S["gn_bias"], 1)

            dve.wait_ge(S["w_small"], 64)
            v.tensor_scalar(cb[:, 1:2], cb[:, 0:1], -1.0, None, ALU.mult).then_inc(S["small"], 1)
            v.reduce_sum(dsum[:], dsk[:], AX_X).then_inc(S["small"], 1)
            fetched(dve, "w_alog")
            v.tensor_scalar(a_log[:], bank("w_alog")[:, 0:DIRS * UNITS], LOG_MAX, None, ALU.min).then_inc(freed("w_alog"), 1)
            dve.wait_ge(S["a_exp"], 1)
            v.tensor_scalar(a_neg[:], a_neg[:], -1.0, None, ALU.mult).then_inc(S["neg_a"], 1)

            for h in range(HALVES):
                dve.wait_ge(S["conv_e"], h + 1)
                v.tensor_scalar(sg[:], sg[:], 1.0, None, ALU.add).then_inc(S["conv_s"], 1)
                dve.wait_ge(S["conv_s"], 2 * h + 1)
                v.reciprocal(sg[:], sg[:]).then_inc(S["conv_s"], 1)
                dve.wait_ge(S["conv_s"], 2 * h + 2)
                v.scalar_tensor_tensor(xs[:, h, 0, :], bank(f"cv{h}")[0:DI, :], cb[:, 0:1], sg[:],
                                       ALU.add, ALU.mult).then_inc(freed(f"cv{h}"), 1)
                taken(dve, f"cv{h}")

            dve.wait_ge(S["w_qkv"], 48)
            dve.wait_ge(S["ident"], 1)
            v.tensor_copy(prep[:], proj[:].unsqueeze(1).to_broadcast([FEAT, HPC, HD])).then_inc(S["repl"], 1)
            v.tensor_copy(irep[:], ident[0:FEAT, 0:FEAT].unsqueeze(1).to_broadcast([FEAT, HPC, FEAT])).then_inc(S["repl"], 1)
            fetched(dve, "w_pbd")
            dve.wait_ge(S["const"], 8)
            v.scalar_tensor_tensor(pbd[:], bank("w_pbd")[0:CK, 0:HPC * FEAT], float(HD) ** -0.25,
                                   pmask[:].rearrange("p a b -> p (a b)"), ALU.mult, ALU.mult).then_inc(freed("w_pbd"), 1)

            def pre_clip(n, h, k):
                fetched(dve, f"d{h}0", 3 * k)
                v.tensor_scalar(spl[:], bank(f"d{h}0")[0:DI, :], dtb[:, k:k + 1], SOFTPLUS_LINEAR,
                                ALU.add, ALU.min).then_inc(S["sp_in"], 1)

            def pre_step(n, h, k):
                dve.wait_ge(S["sp_ln"], n + 1)
                v.scalar_tensor_tensor(spl[:], spe[:], SERIES_BELOW, spl[:], ALU.is_ge, ALU.mult).then_inc(S["sp_l"], 1)
                if n > 0:
                    dve.wait_ge(S["lo"], n)
                dve.wait_ge(S["sp_l"], n + 1)
                v.scalar_tensor_tensor(spl[:], bank(f"d{h}0")[0:DI, :], dtb[:, k:k + 1], spl[:],
                                       ALU.add, ALU.max).then_inc(freed(f"d{h}0"), 1)
                taken(dve, f"d{h}0", k)
                dve.wait_ge(S["sp_s"], n + 1)
                v.tensor_tensor(step2[:, 0, :], spl[:], sps[:], ALU.max).then_inc(S["sp_max"], 1)
                dve.wait_ge(S["sp_max"], n + 1)
                v.tensor_tensor(step2[:, 1, :], step2[:, 0, :], xs[:, h, k, :], ALU.mult).then_inc(S["step"], 1)

            def drive_of(n, k, g12):
                if n >= SLOTS:
                    dve.wait_ge(S["state"], n - SLOTS + 1)
                dve.wait_ge(S["bc_inp"], n + 1)
                v.tensor_tensor(drive[:, g12 % SLOTS, :], b_rep[:, k, :], inp_bc[g12 % 2][:, :],
                                ALU.mult).then_inc(S["drive"], 1)

            def scan(n, g12):
                dve.wait_ge(S["drive"], n + 1)
                dve.wait_ge(S["decay"], n + 1)
                if n >= SLOTS:
                    dve.wait_ge(S["outp"], n - SLOTS + 1)
                v.tensor_tensor_scan(state[:, g12 % SLOTS, :], decay[:, g12 % SLOTS, :, :].rearrange("p b l -> p (b l)"),
                                     drive[:, g12 % SLOTS, :], 0.0, ALU.mult, ALU.add).then_inc(S["state"], 1)

            def between(n, k, g12):
                if g12 == 2:
                    pre_clip(n, 1, k)
                if g12 == 5:
                    pre_step(n, 1, k)

            def merge_y(h):
                dve.wait_ge(S["y_ev"], DIRS * (h + 1))
                turned = y_sum[:, h, :].rearrange("p (b y x) -> p b x y", b=IMG, x=SIDE)
                v.scalar_tensor_tensor(y_sum[:, h, :], xs[:, h, 0, :], dsum[:, 0:1], y_dir[:, 0, :],
                                       ALU.mult, ALU.add).then_inc(S["y_part"], 1)
                dve.wait_ge(S["y_part"], 5 * h + 1)
                for b in range(IMG):
                    src = y_dir[:, 1, b * L:(b + 1) * L].rearrange("p (x y) -> p x y", x=SIDE)
                    v.tensor_tensor(turned[:, b, :, :], turned[:, b, :, :], src, ALU.add).then_inc(S["y_part"], 1)
                dve.wait_ge(S["y_part"], 5 * h + 3)
                for b in range(IMG):
                    src = y_dir[:, 3, b * L:(b + 1) * L].rearrange("p (x y) -> p x y", x=SIDE)[:, ::-1, ::-1]
                    v.tensor_tensor(turned[:, b, :, :], turned[:, b, :, :], src, ALU.add).then_inc(S["y_part"], 1)
                dve.wait_ge(S["y_part"], 5 * h + 5)
                rows = y_sum[:, h, :].rearrange("p (b l) -> p b l", b=IMG)
                v.tensor_tensor(rows, rows, y_dir[:, 2, :].rearrange("p (b l) -> p b l", b=IMG)[:, :, ::-1],
                                ALU.add).then_inc(S["y_sum"], 1)

            dve.wait_ge(S["xs"], 5)
            for k in range(DIRS):
                pre_clip(k, 0, k)
                pre_step(k, 0, k)
            taken(dve, "B00", DIRS - 1)
            for g12 in range(UNITS):
                drive_of(g12, 0, g12)
                if g12:
                    scan(g12 - 1, g12 - 1)
            dve.wait_ge(S["xs"], 10)
            for k in range(1, DIRS):
                for g12 in range(UNITS):
                    n = UNITS * k + g12
                    drive_of(n, k, g12)
                    scan(n - 1, (g12 - 1) % UNITS)
                    between(DIRS + k - 1, k - 1, g12)
            for k in range(DIRS):
                taken(dve, "B10", k)
                for g12 in range(UNITS):
                    n = UNITS * (DIRS + k) + g12
                    drive_of(n, k, g12)
                    scan(n - 1, (g12 - 1) % UNITS)
                    if k == 0:
                        between(2 * DIRS - 1, DIRS - 1, g12)
                    if k == 0 and g12 == 8:
                        merge_y(0)
            scan(2 * DIRS * UNITS - 1, UNITS - 1)
            merge_y(1)

            def normed(h, i, dst, src_of, tag, eps):
                for t in range(TILES):
                    v.bn_stats(mst[:, i, t, :], src_of(t)).then_inc(S["stat_" + tag], 1)
                dve.wait_ge(S["stat_" + tag], TILES * (h + 1))
                for t in range(TILES):
                    v.bn_aggr(mv[:, i, t, :], mst[:, i, t, :]).then_inc(S["agg_" + tag], 1)
                dve.wait_ge(S["agg_" + tag], TILES * (h + 1))
                v.tensor_scalar(mv[:, i, :, 1], mv[:, i, :, 1], eps, None, ALU.add).then_inc(S["eps_" + tag], 1)
                dve.wait_ge(S["rsqrt_" + tag], h + 1)
                for t in range(TILES):
                    v.tensor_scalar(dst[:, t, :], src_of(t), mv[:, i, t, 0:1], rs[:, i, t:t + 1],
                                    ALU.subtract, ALU.mult).then_inc(S["norm_" + tag], 1)

            for h in range(HALVES):
                tk = x_tok[:, h * TILES:(h + 1) * TILES, :]
                dve.wait_ge(S["gate_e"], h + 1)
                v.tensor_scalar(ze[:], ze[:], 1.0, None, ALU.add).then_inc(S["gated"], 1)
                dve.wait_ge(S["gated"], 4 * h + 1)
                v.reciprocal(ze[:], ze[:]).then_inc(S["gated"], 1)
                dve.wait_ge(S["gated"], 4 * h + 2)
                v.tensor_tensor(ze[:], ze[:], z[:, h, :, :], ALU.mult).then_inc(S["gated"], 1)
                fetched(dve, f"yT{h}")
                normed(h, 0, yn, lambda t: bank(f"yT{h}")[:, t * DI:(t + 1) * DI], "y", 1e-5)
                dve.wait_ge(S["norm_y"], TILES * (h + 1))
                if h == 0:
                    dve.wait_ge(S["w_gb"], 64)
                v.tensor_tensor(yn[:], yn[:], gb[:, 0, 0:DI].unsqueeze(1).to_broadcast([P, TILES, DI]), ALU.mult).then_inc(freed(f"yT{h}"), 1)
                taken(dve, f"yT{h}")
                v.tensor_tensor(yn[:], yn[:], gb[:, 1, 0:DI].unsqueeze(1).to_broadcast([P, TILES, DI]), ALU.add).then_inc(S["gated"], 1)
                dve.wait_ge(S["gated"], 4 * h + 4)
                v.tensor_tensor(yn[:], yn[:], ze[:], ALU.mult).then_inc(S["gate"], 1)
                for u in range(2):
                    name = f"o{h}{u}"
                    fetched(dve, name)
                    v.tensor_tensor(tk[:, 2 * u:2 * u + 2, :], tk[:, 2 * u:2 * u + 2, :],
                                    bank(name)[:, 0:2 * CH].rearrange("p (t c) -> p t c", t=2), ALU.add).then_inc(freed(name), 1)
                    taken(dve, name)
                normed(h, 1, tn, lambda t: tk[:, t, :], "t", 1e-5)
                for i in range(PAIRS):
                    name = f"q{h}{i}"
                    fetched(dve, name)
                    v.tensor_scalar(qp[:, i, :], bank(name)[:, :], KERNEL_EPS, KERNEL_EPS, ALU.add, ALU.max).then_inc(freed(name), 1)
                n = HPC * FEAT
                for t in range(TILES):
                    for j in range(2):
                        name = f"kv{h}{t}{j}"
                        fetched(dve, name)
                        v.tensor_scalar(kp[:, t, j * n:(j + 1) * n], bank(name)[:, 0:n], KERNEL_EPS, KERNEL_EPS,
                                        ALU.add, ALU.max).then_inc(S["key"], 1)
                        v.tensor_copy(v1[:, t, j * HPC:(j + 1) * HPC, 0:HD],
                                      bank(name)[:, n:n + CK].rearrange("p (h d) -> p h d", d=HD)).then_inc(freed(name), 1)
                for b in range(IMG):
                    name = f"cx{h}{b}"
                    fetched(dve, name)
                    src = bank(name)[:, 0:PAIRS * 2 * (HD + 1)].rearrange("p (i d) -> p i d", i=PAIRS)
                    v.tensor_copy(cbd[0:FEAT, b, :, 0:HD + 1], src[0:FEAT, :, 0:HD + 1]).then_inc(S["ctx_lo"], 1)
                    v.tensor_copy(cbd[FEAT:P, b, :, HD + 1:], src[FEAT:P, :, HD + 1:]).then_inc(freed(name), 1)
                for b in range(IMG):
                    name = f"at{h}{b}"
                    fetched(dve, name)
                    src = bank(name)[:, 0:2 * HEADS * (HD + 1)].rearrange("p (t h d) -> p t h d", t=2, h=HEADS)
                    for t in range(2):
                        v.reciprocal(arec[:, 2 * b + t, :].unsqueeze(2), src[:, t, :, HD:HD + 1]).then_inc(S["a_rec"], 1)
                    dve.wait_ge(S["a_rec"], 2 * (h * IMG + b + 1))
                    for t in range(2):
                        v.tensor_tensor(ao[:, 2 * b + t, :].rearrange("p (h d) -> p h d", d=HD), src[:, t, :, 0:HD],
                                        arec[:, 2 * b + t, :].unsqueeze(2).to_broadcast([P, HEADS, HD]),
                                        ALU.mult).then_inc(S["att"] if t == 0 else freed(name), 1)
                for u in range(2):
                    name = f"p{h}{u}"
                    fetched(dve, name)
                    v.tensor_tensor(tk[:, 2 * u:2 * u + 2, :], tk[:, 2 * u:2 * u + 2, :],
                                    bank(name)[:, 0:2 * CH].rearrange("p (t c) -> p t c", t=2), ALU.add).then_inc(freed(name), 1)
                    taken(dve, name)
                normed(h, 2, hn, lambda t: tk[:, t, :], "u", 1e-5)
                for c in range(2):
                    taken(dve, f"hT{h}{c}")
                v.reduce_sum(rin[:].rearrange("p c b -> p (c b)"), hT[:].rearrange("p c (b l) -> p (c b) l", b=IMG), AX_X).then_inc(S["router_in"], 1)
                fetched(dve, f"lg{h}")
                v.tensor_scalar(lg[:], bank(f"lg{h}")[0:IMG, 0:HEADS], 1.0 / L, None, ALU.mult).then_inc(freed(f"lg{h}"), 1)
                taken(dve, f"lg{h}")
                li = lg[:].unsqueeze(2).to_broadcast([IMG, HEADS, HEADS])
                lj = lg[:].unsqueeze(1).to_broadcast([IMG, HEADS, HEADS])
                v.tensor_tensor(eq[:], lj, li, ALU.is_equal).then_inc(S["logit_eq"], 1)
                v.tensor_tensor(gt[:], lj, li, ALU.is_gt).then_inc(S["rank"], 1)
                dve.wait_ge(S["logit_eq"], h + 1)
                v.tensor_tensor(eqt[:], eq[:], tri[:], ALU.mult).then_inc(S["rank"], 1)
                dve.wait_ge(S["rank"], 5 * h + 2)
                v.tensor_tensor(eq[:], gt[:], eqt[:], ALU.add).then_inc(S["rank"], 1)
                dve.wait_ge(S["rank"], 5 * h + 3)
                v.reduce_sum(rank[:], eq[:], AX_X).then_inc(S["rank"], 1)
                dve.wait_ge(S["rank"], 5 * h + 4)
                v.tensor_scalar(val[:, 2, :], rank[:], float(TOPK), None, ALU.is_lt).then_inc(S["rank"], 1)
                dve.wait_ge(S["rank"], 5 * h + 5)
                v.tensor_tensor(gt[:], tri[:], val[:, 2, :].unsqueeze(1).to_broadcast([IMG, HEADS, HEADS]), ALU.mult).then_inc(S["slot_of"], 1)
                v.tensor_tensor(msum[:], val[:, 2, :], lg[:], ALU.add).then_inc(S["slot_of"], 1)
                dve.wait_ge(S["slot_of"], 2 * (h + 1))
                v.reduce_sum(val[:, 0, :], gt[:], AX_X).then_inc(S["vals"], 1)
                v.tensor_tensor(val[:, 1, :], msum[:], lg[:], ALU.subtract).then_inc(S["vals"], 1)
                dve.wait_ge(S["vals"], 2 * (h + 1))
                v.tensor_copy(valr[:], val[:].rearrange("p a b -> p (a b)").unsqueeze(2).to_broadcast([IMG, 3 * HEADS, HD])).then_inc(S["val_rows"], 1)
                fetched(dve, f"cr{h}")
                if h:
                    dve.wait_ge(S["hot"], 8 * h)
                v.tensor_copy(col[:].rearrange("p a b c -> p (a b c)"), bank(f"cr{h}")[0:CK, 0:12]).then_inc(freed(f"cr{h}"), 1)
                for b in range(IMG):
                    n = h * IMG + b

                    def row_max(j):
                        m = n * TOPK + j
                        name = f"s{h}{b}{j}"
                        fetched(dve, name)
                        v.tensor_reduce(nmax[:, m % 2, :], bank(name)[:, :].rearrange("p (q k) -> p q k", q=2), AX_X, ALU.max).then_inc(S["prob_max"], 1)
                        dve.wait_ge(S["prob_max"], m + 1)
                        if m >= 2:
                            dve.wait_ge(S["prob"], m - 1)
                        v.tensor_scalar(nmaxs[:, m % 2, :], nmax[:, m % 2, :], -(HD ** -0.5), None, ALU.mult).then_inc(S["prob_bias"], 1)

                    def turned(j):
                        m = n * TOPK + j
                        name = f"pt{h}{b}{j}"
                        fetched(dve, name)
                        if m >= 2:
                            fetched(dve, f"pv{(m - 2) // (TOPK * IMG)}{(m - 2) // TOPK % IMG}{(m - 2) % TOPK}")
                        v.tensor_copy(probT[:, m % 2, :, :].rearrange("p a b -> p (a b)"), bank(name)[:, :]).then_inc(freed(name), 1)
                        taken(dve, f"s{h}{b}{j}")
                        v.reciprocal(prec[:, m % 2, :], psum_row[:, m % 2, :]).then_inc(S["prob_rec"], 1)

                    def weighted(j):
                        m = n * TOPK + j
                        name = f"pv{h}{b}{j}"
                        fetched(dve, name)
                        dve.wait_ge(S["prob_rec"], m + 1)
                        v.tensor_tensor(cx[:, :, j * HD:(j + 1) * HD], bank(name)[:, 0:2 * HD].rearrange("p (q d) -> p q d", q=2),
                                        prec[:, m % 2, :].unsqueeze(2).to_broadcast([P, 2, HD]), ALU.mult).then_inc(freed(name), 1)

                    for j in range(TOPK + 2):
                        if j < TOPK:
                            row_max(j)
                        if j > 1:
                            weighted(j - 2)
                        if 0 < j <= TOPK:
                            turned(j - 1)
                    name = f"cT{h}{b}"
                    fetched(dve, name)
                    v.tensor_copy(cT[0:CK, :], bank(name)[0:CK, 0:L]).then_inc(freed(name), 1)
                    name = f"fo{h}{b}"
                    fetched(dve, name)
                    v.tensor_tensor(res[:, 2 * b:2 * b + 2, :], hn[:, 2 * b:2 * b + 2, :],
                                    bank(name)[:, 0:2 * CH].rearrange("p (t c) -> p t c", t=2), ALU.add).then_inc(freed(name), 1)
                    taken(dve, name)
                normed(h, 3, tn, lambda t: res[:, t, :], "r", 1e-12)
                dve.wait_ge(S["norm_r"], TILES * (h + 1))
                v.tensor_tensor(tn[:], tn[:], gb[:, 2, :].unsqueeze(1).to_broadcast([P, TILES, CH]), ALU.mult).then_inc(S["affine"], 1)
                dve.wait_ge(S["affine"], 2 * h + 1)
                v.tensor_tensor(tn[:], tn[:], gb[:, 3, :].unsqueeze(1).to_broadcast([P, TILES, CH]), ALU.add).then_inc(S["affine"], 1)
                dve.wait_ge(S["affine"], 2 * h + 2)
                if h:
                    dve.wait_ge(S["outd"], 16 * TILES * h)
                for t in range(TILES):
                    v.tensor_tensor(fin[:, t, :], tn[:, t, :], tk[:, t, :], ALU.add).then_inc(S["fin"], 1)

        @block.tensor
        def _(pe):
            t_ = nc.tensor
            idn = ident[:]

            def begin(name, more=0):
                reuse(pe, name, more)
                return bank(name)

            def done(ins):
                ins.then_inc(S["filled"], 1)

            pe.wait_ge(S["ident"], 1)
            for i in range(4):
                h, c = i // 2, i % 2
                if c == 0:
                    pe.wait_ge(S["x"][h], 16)
                for t in range(TILES):
                    ins = t_.transpose(gn_banks[i][0:CK, t * P:(t + 1) * P], x_tok[:, h * TILES + t, c * CK:(c + 1) * CK], idn)
                ins.then_inc(S["gn_turned"], 1)

            b_ = begin("w_in")
            pe.wait_ge(S["w_in"], 32)
            for ic in range(2):
                for oc in range(2):
                    ins = t_.transpose(b_[0:CK, (2 * ic + oc) * CK:(2 * ic + oc + 1) * CK], inw[:, oc, ic * CK:(ic + 1) * CK], ident[0:DI, 0:DI])
            done(ins)
            b_ = begin("gm")
            pe.wait_ge(S["const"], 8)
            pe.wait_ge(S["gn_stats"], 16)
            done(t_.matmul(b_[0:CK, 0:8], avg6[:], gmv[:, :, 0], start=True, stop=True))
            b_ = begin("gv")
            pe.wait_ge(S["gn_var"], 1)
            done(t_.matmul(b_[0:CK, 0:8], avg6[:], gva[:], start=True, stop=True))
            b_ = begin("w_xp")
            pe.wait_ge(S["w_xp"], 32)
            for k in range(DIRS):
                ins = t_.transpose(b_[0:DI, k * XROWS:(k + 1) * XROWS], xpw[:, k, :], ident[0:XROWS, 0:XROWS])
            done(ins)
            b_ = begin("w_dt")
            for k in range(DIRS):
                ins = t_.transpose(b_[0:RANK, k * DI:(k + 1) * DI], dtw[:, k, :], ident[0:DI, 0:DI])
            done(ins)
            b_ = begin("w_fold")
            taken(pe, "w_dt")
            for k in range(DIRS):
                ins = t_.matmul(b_[0:DI, k * DI:(k + 1) * DI], xpw[0:RANK, k, :], dtT[:, k, :], start=True, stop=True)
            done(ins)
            b_ = begin("w_alog")
            pe.wait_ge(S["w_alog"], 16)
            done(t_.transpose(b_[:, 0:DIRS * UNITS], alog[:], ident[0:DIRS * UNITS, 0:DIRS * UNITS]))

            taken(pe, "w_in")
            for h in range(HALVES):
                b_ = begin(f"xh{h}")
                pe.wait_ge(S["xn"], 4 * (h + 1))
                for c in range(2):
                    ins = t_.matmul(b_[0:DI, :], inT[:, c, 0:DI], xnT[:, c, h * TOK:(h + 1) * TOK], start=(c == 0), stop=(c == 1))
                done(ins)
                b_ = begin(f"z{h}")
                for t in range(TILES):
                    for c in range(2):
                        at = h * TOK + t * P
                        ins = t_.matmul(b_[:, t * DI:(t + 1) * DI], xnT[:, c, at:at + P], inT[:, c, DI:2 * DI],
                                        start=(c == 0), stop=(c == 1))
                done(ins)
                b_ = begin(f"cv{h}")
                pe.wait_ge(S["taps"], 9)
                taken(pe, f"xh{h}")
                for b in range(IMG):
                    for i in range(9):
                        ins = t_.matmul(b_[0:DI, b * L:(b + 1) * L], taps[:, i, :],
                                        xpad[:, b, i // 3:i // 3 + SIDE, i % 3:i % 3 + SIDE], start=(i == 0), stop=(i == 8))
                done(ins)

            b_ = begin("w_out")
            for o in range(2):
                ins = t_.transpose(b_[0:DI, o * CK:(o + 1) * CK], opw[:, o, :], ident[0:CK, 0:CK])
            done(ins)
            b_ = begin("w_pbd")
            pe.wait_ge(S["repl"], 2)
            done(t_.matmul(b_[0:CK, 0:HPC * FEAT], prep[:].rearrange("p a b -> p (a b)"), irep[:].rearrange("p a b -> p (a b)"),
                           start=True, stop=True))
            taken(pe, "w_pbd")
            for i in range(2):
                for rc in range(2):
                    for c in range(2):
                        b_ = begin(f"w_qk{i}{rc}{c}")
                        done(t_.matmul(b_[0:CK + c, 0:HPC * FEAT], qkvw[:, 2 * i + rc, c * CK:(c + 1) * CK + c], pbd[:],
                                       start=True, stop=True))
            for name, w, base, s, cnt in (("w_v", qkvw, 4, "w_qkv", 48), ("w_proj", pjw, 0, "w_proj", 32)):
                b_ = begin(name)
                pe.wait_ge(S[s], cnt)
                for c in range(2):
                    for o in range(2):
                        ins = t_.transpose(b_[0:CK + c, (2 * c + o) * CK:(2 * c + o + 1) * CK],
                                           w[:, base + o, c * CK:(c + 1) * CK + c], ident[0:CK, 0:CK])
                done(ins)
            pe.wait_ge(S["w_ffn"], 96)
            for i in range(3):
                b_ = begin(f"w_f{i}")
                for oc in range(2):
                    for ic in range(2):
                        ins = t_.transpose(b_[0:CK, (2 * oc + ic) * CK:(2 * oc + ic + 1) * CK],
                                           fw[:, i, ic, oc * CK:(oc + 1) * CK], ident[0:CK, 0:CK])
                done(ins)

            def pre(n, h, k):
                pe.wait_ge(S["cur"], n + 1)
                for name, at, m in ((f"d{h}0", 0, DI), (f"B{h}0", DI, P), (f"C{h}0", DI + P, P)):
                    b_ = begin(name, k)
                    done(t_.matmul(b_[0:m, :], cur_w[:, at:at + m], xs[:, h, k, :], start=True, stop=True))

            def spread_out(n, k, g12):
                j, q = g12 // PER_CHUNK, g12 % PER_CHUNK
                if n >= 2:
                    pe.wait_ge(S["decay"], n - 1)
                t_.matmul(step_bc[g12 % 2][:, :], spread[:, q, :], stack[:, k, j, 0:TOK], start=True, stop=True
                          ).then_inc(S["bc_step"], 1)
                if n >= 2:
                    pe.wait_ge(S["drive"], n - 1)
                t_.matmul(inp_bc[g12 % 2][:, :], spread[:, q, :], stack[:, k, j, TOK:2 * TOK], start=True, stop=True
                          ).then_inc(S["bc_inp"], 1)

            def sum_states(n, kk, g12):
                pe.wait_ge(S["outp"], n + 1)
                if g12 == 0 and kk > 0:
                    pe.wait_ge(S["y_ev"], kk)
                at = DI - GRP - GRP * g12
                t_.matmul(y_acc[0:DI, :], band[:, at:at + DI], outp[:, g12 % SLOTS, :],
                          start=(g12 == 0), stop=(g12 == UNITS - 1)).then_inc(S["y_mm"], 1)

            pe.wait_ge(S["xs"], 5)
            for k in range(DIRS):
                pre(k, 0, k)
            pe.wait_ge(S["const2"], CONST2)
            pe.wait_ge(S["ones"], ONES)
            pe.wait_ge(S["xn"], 8)
            pe.wait_ge(S["stack"], 16 * 9 * DIRS)
            for g12 in range(UNITS):
                spread_out(g12, 0, g12)
                if g12 >= Y_LAG:
                    sum_states(g12 - Y_LAG, 0, g12 - Y_LAG)
            pe.wait_ge(S["xs"], 10)
            for k in range(1, DIRS):
                for g12 in range(UNITS):
                    n = UNITS * k + g12
                    spread_out(n, k, g12)
                    sum_states(n - Y_LAG, k, (g12 - Y_LAG) % UNITS)
                    if g12 == 1:
                        pre(DIRS + k - 1, 1, k - 1)
            for k in range(DIRS):
                pe.wait_ge(S["stack"], 16 * 9 * (DIRS + k + 1))
                for g12 in range(UNITS):
                    n = UNITS * (DIRS + k) + g12
                    spread_out(n, k, g12)
                    sum_states(n - Y_LAG, DIRS + k, (g12 - Y_LAG) % UNITS)
                    if k == 0 and g12 == 1:
                        pre(2 * DIRS - 1, 1, DIRS - 1)
            for g12 in range(UNITS - Y_LAG, UNITS):
                sum_states(UNITS * (2 * DIRS - 1) + g12, 2 * DIRS - 1, g12)

            for h in range(HALVES):
                b_ = begin(f"yT{h}")
                pe.wait_ge(S["y_sum"], h + 1)
                for t in range(TILES):
                    ins = t_.transpose(b_[:, t * DI:(t + 1) * DI], y_sum[:, h, t * P:(t + 1) * P], ident[0:DI, 0:DI])
                done(ins)
                b_ = begin(f"gT{h}")
                pe.wait_ge(S["gate"], h + 1)
                for t in range(TILES):
                    ins = t_.transpose(b_[0:DI, t * P:(t + 1) * P], yn[:, t, :], idn)
                done(ins)
                for u in range(2):
                    b_ = begin(f"o{h}{u}")
                    taken(pe, f"gT{h}")
                    for t in range(2):
                        at = (2 * u + t) * P
                        ins = t_.matmul(b_[:, t * CH:(t + 1) * CH], gT[:, at:at + P], outT[:], start=True, stop=True)
                    done(ins)

                def turn(name, src, ready, count):
                    for c in range(2):
                        b_ = begin(f"{name}{h}{c}")
                        pe.wait_ge(ready, count)
                        for t in range(TILES):
                            ins = t_.transpose(b_[0:CK, t * P:(t + 1) * P], src[:, t, c * CK:(c + 1) * CK], idn)
                        done(ins)
                    for c in range(2):
                        taken(pe, f"{name}{h}{c}")

                turn("tT", tn, S["norm_t"], TILES * (h + 1))
                for i in range(PAIRS):
                    b_ = begin(f"q{h}{i}")
                    for c in range(2):
                        ins = t_.matmul(b_[:, :], qw[0:CK + c, c, i * P:(i + 1) * P], tT[0:CK + c, c, :], start=(c == 0), stop=(c == 1))
                    done(ins)
                n = HPC * FEAT + CK
                for t in range(TILES):
                    for j in range(2):
                        b_ = begin(f"kv{h}{t}{j}")
                        for c in range(2):
                            ins = t_.matmul(b_[:, 0:n], tT[0:CK + c, c, t * P:(t + 1) * P], kvw[0:CK + c, c, j, :],
                                            start=(c == 0), stop=(c == 1))
                        done(ins)
                w = 2 * (HD + 1)
                for b in range(IMG):
                    b_ = begin(f"cx{h}{b}")
                    taken(pe, f"kv{h}{2 * b + 1}0")
                    taken(pe, f"kv{h}{2 * b + 1}1")
                    for i in range(PAIRS):
                        for t in range(2):
                            ins = t_.matmul(b_[:, i * w:(i + 1) * w], kp[:, 2 * b + t, i * P:(i + 1) * P],
                                            v1[:, 2 * b + t, 2 * i:2 * i + 2, :].rearrange("p h d -> p (h d)"),
                                            start=(t == 0), stop=(t == 1))
                    done(ins)
                for b in range(IMG):
                    b_ = begin(f"at{h}{b}")
                    taken(pe, f"cx{h}{b}")
                    for t in range(2):
                        for i in range(PAIRS):
                            at = (t * PAIRS + i) * w
                            ins = t_.matmul(b_[:, at:at + w], qp[:, i, (2 * b + t) * P:(2 * b + t + 1) * P], cbd[:, b, i, :],
                                            start=True, stop=True)
                    done(ins)
                for b in range(IMG):
                    taken(pe, f"at{h}{b}")
                turn("aT", ao, S["att"], IMG * (h + 1))
                for u in range(2):
                    b_ = begin(f"p{h}{u}")
                    for t in range(2):
                        at = (2 * u + t) * P
                        for c in range(2):
                            ins = t_.matmul(b_[:, t * CH:(t + 1) * CH], aT[0:CK + c, c, at:at + P], pjT[0:CK + c, c, :],
                                            start=(c == 0), stop=(c == 1))
                    done(ins)
                turn("hT", hn, S["norm_u"], TILES * (h + 1))
                b_ = begin(f"lg{h}")
                pe.wait_ge(S["router_in"], h + 1)
                pe.wait_ge(S["w_wo"], 48)
                for c in range(2):
                    ins = t_.matmul(b_[0:IMG, 0:HEADS], rin[0:CK + c, c, :], wr[0:CK + c, c, :], start=(c == 0), stop=(c == 1))
                done(ins)
                b_ = begin(f"cr{h}")
                pe.wait_ge(S["val_rows"], h + 1)
                for u in range(3):
                    for i in range(2):
                        at = (2 * u + i) * IMG
                        rep = valr[:, u * HEADS + i * HPC:u * HEADS + (i + 1) * HPC, :].rearrange("p a b -> p (a b)")
                        ins = t_.matmul(b_[0:CK, at:at + IMG], rep, ident[0:IMG, 0:IMG], start=True, stop=True)
                done(ins)
                for b in range(IMG):
                    n = h * IMG + b
                    pe.wait_ge(S["sel"], 8 * (h + 1))
                    for wi, w in enumerate("qk"):
                        b_ = begin(f"w{w}{h}{b}")
                        for c in range(2):
                            for o in range(2):
                                ins = t_.matmul(b_[0:CK + c, c * CH:(c + 1) * CH], fT[:, wi, o, c * CK:(c + 1) * CK + c],
                                                sel_m[:, b, o, :, :].rearrange("p a b -> p (a b)"), start=(o == 0), stop=(o == 1))
                        done(ins)
                    b_ = begin(f"wv{h}{b}")
                    for c in range(2):
                        for o in range(2):
                            t_.matmul(b_[0:CK + c, c * CK:(c + 1) * CK], fT[:, 2, o, c * CK:(c + 1) * CK + c],
                                      sel_m[:, b, o, :, 0:HD], start=(o == 0), stop=(o == 1))
                    for o in range(2):
                        ins = t_.matmul(b_[0:CK, CH:2 * CH], sel_u[:, b, o, :, :].rearrange("p a b -> p (a b)"), wo[:, o, :],
                                        start=(o == 0), stop=(o == 1))
                    done(ins)
                    for wi, w in enumerate("qk"):
                        b_ = begin(f"f{w}{h}{b}")
                        taken(pe, f"w{w}{h}{b}")
                        for lo_, m, at in ((0, P, 0), (P, 64, L)):
                            for c in range(2):
                                ins = t_.matmul(b_[0:m, at:at + L], wsel[0:CK + c, wi, c, lo_:lo_ + m],
                                                hT[0:CK + c, c, b * L:(b + 1) * L], start=(c == 0), stop=(c == 1))
                        done(ins)
                    b_ = begin(f"fv{h}{b}")
                    taken(pe, f"wv{h}{b}")
                    for t in range(2):
                        for c in range(2):
                            ins = t_.matmul(b_[:, t * CK:(t + 1) * CK], hT[0:CK + c, c, b * L + t * P:b * L + (t + 1) * P],
                                            wsv[0:CK + c, c, :], start=(c == 0), stop=(c == 1))
                    done(ins)
                    for w in "qkv":
                        taken(pe, f"f{w}{h}{b}")

                    def scores(j):
                        b_ = begin(f"s{h}{b}{j}")
                        r0, ch = 2 * HD * (j % 4), j // 4
                        for q in range(2):
                            ins = t_.matmul(b_[:, q * L:(q + 1) * L], fq[r0:r0 + HD, ch, q * P:(q + 1) * P], fk[r0:r0 + HD, ch, :],
                                            start=True, stop=True)
                        done(ins)

                    def turn_probs(j):
                        m = n * TOPK + j
                        b_ = begin(f"pt{h}{b}{j}")
                        taken(pe, f"s{h}{b}{j}")
                        for kt in range(2):
                            for q in range(2):
                                ins = t_.transpose(b_[:, (2 * kt + q) * P:(2 * kt + q + 1) * P], prob[:, m % 2, q, kt * P:(kt + 1) * P], idn)
                        done(ins)

                    def weigh_values(j):
                        m = n * TOPK + j
                        b_ = begin(f"pv{h}{b}{j}")
                        taken(pe, f"pt{h}{b}{j}")
                        for q in range(2):
                            for kt in range(2):
                                ins = t_.matmul(b_[:, q * HD:(q + 1) * HD], probT[:, m % 2, kt, q * P:(q + 1) * P],
                                                fv[:, kt, j * HD:(j + 1) * HD], start=(kt == 0), stop=(kt == 1))
                        done(ins)

                    for j in range(TOPK + 2):
                        if j < TOPK:
                            scores(j)
                        if 0 < j <= TOPK:
                            turn_probs(j - 1)
                        if j > 1:
                            weigh_values(j - 2)
                    b_ = begin(f"cT{h}{b}")
                    for j in (TOPK - 3, TOPK - 2, TOPK - 1):
                        taken(pe, f"pv{h}{b}{j}")
                    for q in range(2):
                        ins = t_.transpose(b_[0:CK, q * P:(q + 1) * P], cx[:, q, :], idn)
                    done(ins)
                    b_ = begin(f"fo{h}{b}")
                    taken(pe, f"cT{h}{b}")
                    for q in range(2):
                        ins = t_.matmul(b_[:, q * CH:(q + 1) * CH], cT[:, q * P:(q + 1) * P], wos[:], start=True, stop=True)
                    done(ins)


_INS = ["x"] + ["L0_conv_" + n for n in ("in_proj_w", "conv_w", "conv_b", "x_proj_w", "dt_projs_w", "dt_projs_b", "A_logs",
                                         "Ds", "out_norm_g", "out_norm_b", "out_proj_w")]
_INS += ["L1_attn_" + n for n in ("w_qkv", "b_qkv", "w_proj", "b_proj", "projection")]
_INS += ["L1_ffn_" + n for n in ("Wq", "bq", "Wk", "bk", "Wv", "bv", "Wr", "br", "Wo", "bo", "ln_g", "ln_b")]
_OUTS = [((4, 16, 16, 192), "float32")]


def kernel(**inputs):
    import numpy as _np
    import concourse.bacc as _bacc
    from concourse import mybir as _mybir
    from concourse.bass_utils import run_bass_kernel_spmd as _run

    nc = _bacc.Bacc("TRN2", target_bir_lowering=False, num_devices=1)
    arrays, args = {}, []
    for name in _INS:
        a = _np.ascontiguousarray(inputs[name])
        arrays[f"in_{name}_dram"] = a
        args.append(nc.dram_tensor(f"in_{name}_dram", a.shape, _mybir.dt.from_np(a.dtype), kind="ExternalInput").ap())
    for i, (shape, dtype) in enumerate(_OUTS):
        dt = _mybir.dt.from_np(_np.dtype(dtype))
        args.append(nc.dram_tensor(f"out_{i}_dram", shape, dt, kind="ExternalOutput").ap())
    hybrid_kernel(nc, *args)
    r = _run(nc, [arrays], core_ids=[0])
    got = tuple(r.results[0][f"out_{i}_dram"] for i in range(len(_OUTS)))
    return got[0]
```

```python
from contextlib import ExitStack

import concourse.bass as bass
from concourse import mybir

F32 = mybir.dt.float32
BF16 = mybir.dt.bfloat16
ALU = mybir.AluOpType
ACT = mybir.ActivationFunctionType
AX_X = mybir.AxisListType.X

P = 128
IMAGES, SIDE, CH = 4, 16, 192
L = SIDE * SIDE
HALVES = 2
IMG = IMAGES // HALVES
TOK = IMG * L
TILES = TOK // P
CK = CH // 2
DI, NS, RANK, DIRS = 96, 16, 12, 4
GRP = P // NS
UNITS = DI // GRP
CHUNK = 32
CHUNKS = DI // CHUNK
PER_CHUNK = CHUNK // GRP
XROWS = RANK + 2 * NS
GN_SIZE = CH // 32
HEADS, HD, FEAT, TOPK = 12, 16, 64, 6
HPC = CK // HD
PAIRS = HEADS // 2
KERNEL_EPS = 0.001
RING = 3
SLOTS = 3
Y_LAG = 3
SOFTPLUS_LINEAR = 40.0
SERIES_BELOW = 0.0025
PRE_STEP_MM, PRE_CLIP, PRE_STEP, PRE_B, PRE_C, PRE_HI, PRE_MID, PRE_LO = 0, 1, 2, 2, 3, 3, 4, 4
LOG_MAX = 82.0

CONST2 = 3 + 1 + HPC + TOPK
ONES = 6
ACC_ROWS = IMG * (SIDE + 2) - 2
SCANS = HALVES * DIRS
SLOT_COUNT = SCANS * UNITS
FINAL_RING = 8

ATTN_STEPS = (["yT", "yn", "gT", "o", "tn", "tT", "q0", "q1", "q2", "kv00", "kv01", "kv10", "kv11", "cx", "at", "aT",
               "p", "un", "hT", "lg", "cr"])
FFN_STEPS = ["wq", "wk", "wv", "fq", "fk", "fv"] + [f"h{j}" for j in range(TOPK + 2)] + ["cT", "fo", "rn"]
WEIGHT_STEPS = (["w_out", "w_pbd"] + [f"w_qk{i}{rc}{c}" for i in range(2) for rc in range(2) for c in range(2)]
                + ["w_v", "w_proj", "w_f0", "w_f1", "w_f2"])
NO_PRODUCT = {"yn", "tn", "un", "rn", "conv0", "conv1", "silu"}


def side_work():
    beside = [[] for _ in range(SLOT_COUNT)]
    for at, step in ((1, "xh"), (3, "conv0"), (4, "conv1"), (6, "silu"), (8, "z")):
        beside[at].append((step, 1))
    for i, step in enumerate(WEIGHT_STEPS):
        beside[12 + 2 * i].append((step, 0))
    order = [(step, n) for step in ATTN_STEPS for n in (0, 1)] + [(step, n) for n in (0, 1) for step in FFN_STEPS]
    first = DIRS * UNITS + 5
    slots, total = SLOT_COUNT - first, len(order)
    for u in range(first, SLOT_COUNT):
        due = -(-total * (u + 1 - first) // slots)
        while order and total - len(order) < due:
            if u % UNITS == PRE_CLIP and sum(len(products(*item)) for item in beside[u] + order[:1]) > RING - 1:
                break
            beside[u].append(order.pop(0))
    assert not order
    rest = [(step, n) for step in ATTN_STEPS + FFN_STEPS for n in (2, 3)]
    return beside, rest


def products(step, n):
    if step in NO_PRODUCT:
        return []
    if step in WEIGHT_STEPS:
        return [step]
    if step[0] == "h" and step[1:].isdigit():
        j = int(step[1:])
        return [f"s{n}{j}"] * (j < TOPK) + [f"pt{n}{j - 1}"] * (0 < j <= TOPK) + [f"pv{n}{j - 2}"] * (j > 1)
    return [f"{step}_{n}"]


def pre_at(u):
    return u // UNITS + 1, u % UNITS


def ring_plan():
    beside, rest = side_work()
    names = ["w_in", "w_xp", "w_dt", "w_fold", "w_alog", "gm", "gv", "xh_0", "z_0", "d0", "B0", "C0"]
    for u in range(SLOT_COUNT):
        n, g12 = pre_at(u)
        for item in beside[u]:
            names += products(*item)
        if n < SCANS:
            names += [f"d{n}"] * (g12 == PRE_STEP_MM) + [f"B{n}"] * (g12 == PRE_B) + [f"C{n}"] * (g12 == PRE_C)
    early = len(names)
    for item in rest:
        names += products(*item)
    plan, held = {}, [0] * FINAL_RING
    for i, name in enumerate(names):
        at = i % RING if i < early else (i - early) % FINAL_RING
        plan[name] = (i, at, held[at])
        held[at] += 1
    return plan


def hybrid_kernel(nc, x, in_proj_w, conv_w, conv_b, x_proj_w, dt_w, dt_b, A_logs, Ds, norm_g, norm_b, out_proj_w,
                  w_qkv, b_qkv, w_proj, b_proj, projection, Wq, bq, Wk, bk, Wv, bv, Wr, br, Wo, bo, ln_g, ln_b, out):
    ring = ring_plan()
    x_d = x.rearrange("b h w c -> (b h w) c").rearrange("(t p) c -> p t c", p=P)
    out_d = out.rearrange("b h w c -> (b h w) c").rearrange("(t p) c -> p t c", p=P)

    with ExitStack() as ctx:
        ctx.enter_context(nc.allow_non_contiguous_dma(reason="small parameter vectors"))

        def sb(name, shape, dt=F32):
            return ctx.enter_context(nc.sbuf_tensor(name, shape, dt))

        def shared(name, *tenants):
            def words(shape, dt):
                n = 1
                for d in shape[1:]:
                    n *= d
                return n * (2 if dt == BF16 else 4) // 4
            room = sb(name, [P, max(sum(words(*t) for t in tenant) for tenant in tenants)])
            views = []
            for tenant in tenants:
                at = 0
                for shape, dt in tenant:
                    ap = room[0:shape[0], at:at + words(shape, dt)]
                    at += words(shape, dt)
                    if dt == BF16:
                        ap = ap.bitcast(BF16)
                    dims = "abcde"[:len(shape) - 1]
                    if len(dims) > 1:
                        ap = ap.rearrange(f"p ({' '.join(dims)}) -> p {' '.join(dims)}",
                                          **{d: shape[1 + i] for i, d in enumerate(dims)})
                    views.append(ap)
            return views

        def sem(name):
            return ctx.enter_context(nc.semaphore(name))

        step_bc = [ctx.enter_context(nc.psum_tensor(f"step_bc{i}", [P, TOK], F32)) for i in range(2)]
        inp_bc = [ctx.enter_context(nc.psum_tensor(f"inp_bc{i}", [P, TOK], F32)) for i in range(2)]
        y_acc = ctx.enter_context(nc.psum_tensor("y_acc", [P, TOK], F32))
        banks = [ctx.enter_context(nc.psum_tensor(f"ring{i}", [P, TOK], F32)) for i in range(RING)]
        banks += step_bc + inp_bc + [y_acc]

        def bank(name):
            return banks[ring[name][1]]

        x_tok = sb("x_tok", [P, HALVES * TILES, CH])
        opw = sb("opw", [CK, 2, DI])
        cw = sb("cw", [DI, 9])
        cb = sb("cb", [DI, 2])
        dtb = sb("dtb", [DI, DIRS])
        dsk = sb("dsk", [DI, DIRS])
        gb = sb("gb", [P, 4, CH])
        proj = sb("proj", [FEAT, HD])
        wr = sb("wr", [CK + 1, 2, HEADS])
        wo = sb("wo", [CK, 2, CH])
        ident = sb("ident", [P, P])
        avg6 = sb("avg6", [CK, CK])
        band = sb("band", [P, 2 * DI - GRP])
        spread = sb("spread", [DI, PER_CHUNK, P], BF16)
        dmatch = sb("dmatch", [CK, 2 * HD])
        tri = sb("tri", [1, HEADS, HEADS])
        slot_no = sb("slot_no", [CK, TOPK])
        neg_half = sb("neg_half", [P, 8])
        xpT = sb("xpT", [DI, DIRS, XROWS])
        a_log = sb("a_log", [P, DIRS * UNITS])
        a_neg = sb("a_neg", [P, DIRS * UNITS])
        outT = sb("outT", [DI, CH])
        dsum = sb("dsum", [DI, 1])
        qw = sb("qw", [CK + 1, 2, HEADS * FEAT])
        kvw = sb("kvw", [CK + 1, 2, 2, HPC * FEAT + CK])
        pjT = sb("pjT", [CK + 1, 2, CH])
        fT = sb("fT", [CK, 3, 2, CH + 1])
        qkvw, pjw, fw, kp = shared("room_a", [([CK, 6, CH + 1], F32), ([CK, 2, CH + 1], F32), ([CK, 3, 2, CH], F32)],
                                   [([P, TILES, HEADS * FEAT], F32)])
        xnT, irep, prep, pmask, qp, gt, eq, eqt, valr = shared(
            "room_b", [([CK, 2, HALVES * TOK], F32), ([FEAT, HPC, FEAT], F32), ([FEAT, HPC, HD], F32), ([CK, HPC, FEAT], F32)],
            [([P, PAIRS, TOK], F32)], [([1, HEADS, HEADS], F32)] * 3 + [([1, IMG, 3 * HEADS, HD], F32)])
        acc, hn = shared("room_e", [([DI, ACC_ROWS, SIDE], F32)], [([P, TILES, CH], F32)])
        inT, dtT, yn = shared("room_f", [([CK, 2, CH], F32), ([RANK, DIRS, DI], F32)], [([P, TILES, DI], F32)])
        inw, xpw, dtw, alog, ze, tn = shared("room_h", [([DI, 2, CH], F32), ([XROWS, DIRS, DI], F32), ([DI, DIRS, RANK], F32),
                                                        ([DIRS * UNITS, P], F32)], [([P, TILES, DI], F32)],
                                             [([P, TILES, CH], F32)])
        sg, gT = shared("room_i", [([DI, TOK], F32)], [([DI, TOK], F32)])
        prob = [sb("prob", [P, 2, 2, L])]
        probT = [sb("probT", [P, 2, 2, L])]
        fq = [sb("fq", [P, 2, L])]
        fk = [sb("fk", [P, 2, L])]
        fv = [sb("fv", [P, 2, CK])]
        wsel = [sb("wsel", [CK + 1, 2, 2, TOPK * 2 * HD])]
        wsv = [sb("wsv", [CK + 1, 2, CK])]
        cx = [sb("cx", [P, 2, CK])]
        wos = [sb("wos", [CK + 1, CH])]
        pbd, cT_ = shared("room_j", [([CK, HPC * FEAT], F32)], [([CK + 1, L], F32)])
        cT = [cT_]
        stack, *second = shared("room_s", [([DI, 2, CHUNKS, 2 * TOK], BF16)],
                                [([P, 2, 2, L], F32), ([P, 2, 2, L], F32), ([P, 2, L], F32), ([P, 2, L], F32)])
        for bufs, view in zip((prob, probT, fq, fk), second):
            bufs.append(view)
        b_rep, c_rep, *second = shared("room_r", [([P, 2, TOK], F32), ([P, 2, TOK], F32)],
                                       [([CK + 1, 2, 2, TOPK * 2 * HD], F32), ([CK + 1, 2, CK], F32), ([P, 2, CK], F32),
                                        ([P, 2, CK], F32), ([CK + 1, L], F32), ([CK + 1, CH], F32)])
        for bufs, view in zip((wsel, wsv, cx, fv, cT, wos), second):
            bufs.append(view)
        pre_w = sb("pre_w", [DI, DIRS, DI + 2 * P])
        spl = sb("spl", [DI, TOK])
        spe = sb("spe", [DI, TOK])
        sps = sb("sps", [DI, TOK])
        step2 = sb("step2", [DI, 2, TOK])
        hi = sb("hi", [DI, 2, TOK], BF16)
        mid = sb("mid", [DI, 2, TOK], BF16)
        lo = sb("lo", [DI, 2, TOK], BF16)
        sel_m = sb("sel_m", [CK, IMG, 2, TOPK, 2 * HD])
        sel_u = sb("sel_u", [CK, IMG, 2, TOPK, HD])
        (xs_room,) = shared("room_g", [([P, HALVES, DIRS, TOK], F32)])
        xs = xs_room[0:DI]
        later = xs_room[:, 0, 1:DIRS, :].rearrange("p k t -> p (k t)")
        n = TILES * CH
        ao = res = later[:, 0:n].rearrange("p (t c) -> p t c", t=TILES)
        fin = later[:, n:2 * n].rearrange("p (t c) -> p t c", t=TILES)
        conv_out = [acc[:, b * (SIDE + 2):b * (SIDE + 2) + SIDE, :].rearrange("p y x -> p (y x)") for b in range(IMG)]
        gst = sb("gst", [CK, 2 * IMAGES, 6])
        gmv = sb("gmv", [CK, 2 * IMAGES, 2])
        gdv = sb("gdv", [CK, 2 * IMAGES])
        gmean = sb("gmean", [CK, 2 * IMAGES])
        gva = sb("gva", [CK, 2 * IMAGES])
        gve = sb("gve", [CK, 2 * IMAGES])
        gsq = sb("gsq", [CK, 2 * IMAGES])
        grs = sb("grs", [CK, 2 * IMAGES])
        gbi = sb("gbi", [CK, 2 * IMAGES])
        xpad = sb("xpad", [DI, IMG, SIDE + 2, SIDE + 2])
        z = sb("z", [P, HALVES, TILES, DI])
        decay = sb("decay", [P, SLOTS, IMG, L])
        drive = sb("drive", [P, SLOTS, TOK])
        state = sb("state", [P, SLOTS, TOK])
        outp = sb("outp", [P, SLOTS, TOK])
        y_dir = sb("y_dir", [DI, DIRS, TOK])
        y_sum = sb("y_sum", [DI, HALVES, TOK])
        mst = sb("mst", [P, 4, TILES, 6])
        mv = sb("mv", [P, 4, TILES, 2])
        rs = sb("rs", [P, 4, TILES])
        tT = sb("tT", [CK + 1, 2, TOK])
        aT = hT = tT
        v1 = sb("v1", [P, TILES, HEADS, HD + 1])
        cbd = sb("cbd", [P, IMG, PAIRS, 2 * (HD + 1)])
        arec = sb("arec", [P, TILES, HEADS])
        rin = sb("rin", [CK + 1, 2, IMG])
        lg = sb("lg", [1, IMG, HEADS])
        rank = sb("rank", [1, IMG, HEADS])
        val = sb("val", [1, IMG, 3, HEADS])
        msum = sb("msum", [1, IMG, HEADS])
        col = sb("col", [CK, 3, 2, IMG])
        hot = sb("hot", [CK, 2, 2, IMG, TOPK])
        nmax = [sb(f"nmax{i}", [P, 2, 2]) for i in range(2)]
        nmaxs = [sb(f"nmaxs{i}", [P, 2, 2]) for i in range(2)]
        psum_row = [sb(f"psum_row{i}", [P, 2, 2]) for i in range(2)]
        prec = [sb(f"prec{i}", [P, 2, 2]) for i in range(2)]

        gn_banks = [step_bc[0], step_bc[1], inp_bc[0], inp_bc[1]]
        S = {n: sem("s_" + n) for n in (
            "w_in w_xp w_alog w_small w_gb w_qkv w_proj w_ffn w_wo w_bo zeroed const const2 ones ident filled repl small neg_a "
            "gn_turned gn_stats gn_dev gn_var gn_eps gn_rsqrt gn_bias xn padded z_kept gate_e gate_s conv conv_e xs0 xs "
            "a_exp sp_t sp_s sp_l sp_max sp_in sp_exp sp_ln step hi rest mid lo stack bc_step bc_inp decay drive state outp y_mm y_ev y_part y_sum "
            "stat_y agg_y eps_y rsqrt_y norm_y gate stat_t agg_t eps_t rsqrt_t norm_t key ctx_lo a_rec att "
            "stat_u agg_u eps_u rsqrt_u norm_u router_in logit_eq rank slot_of vals val_rows hot sel "
            "stat_r agg_r eps_r rsqrt_r norm_r wos_row fin"
        ).split()}
        S["outd"] = [sem(f"s_outd{b}") for b in range(IMG)]
        S["x"] = [sem(f"s_x{h}") for h in range(HALVES)]
        for n in ("prob_max", "prob_bias", "prob", "prob_rec"):
            S[n] = [sem(f"s_{n}{i}") for i in range(2)]
        free = [sem(f"s_free{i}") for i in range(FINAL_RING)]
        beside, rest = side_work()

        def fetched(eng, name):
            eng.wait_ge(S["filled"], ring[name][0] + 1)

        def reuse(eng, name):
            _, at, held = ring[name]
            if held:
                eng.wait_ge(free[at], held)

        def taken(eng, name):
            eng.wait_ge(freed(name), ring[name][2] + 1)

        def freed(name):
            return free[ring[name][1]]

        def of_set(n):
            return (0, n) if n < IMAGES - 1 else (1, 0)

        def key_count(n, step):
            return 2 * IMG * IMG * (n // IMG) + IMG * (2 * int(step[2]) + int(step[3])) + n % IMG + 1

        block = ctx.enter_context(nc.Block())

        @block.sync
        def _(sp):
            for h in range(HALVES):
                sp.dma_start(x_tok[:, h * TILES:(h + 1) * TILES, :], x_d[:, h * TILES:(h + 1) * TILES, :]).then_inc(S["x"][h], 16)
            sp.dma_start(inw[:], in_proj_w.rearrange("(o p) c -> p o c", p=DI)).then_inc(S["w_in"], 16)
            sp.dma_start(xpw[:], x_proj_w.rearrange("k r c -> r k c")).then_inc(S["w_xp"], 16)
            sp.dma_start(dtw[:], dt_w.rearrange("k c r -> c k r")).then_inc(S["w_xp"], 16)
            sp.dma_start(alog[:], A_logs.rearrange("(g c) n -> g (c n)", c=GRP)).then_inc(S["w_alog"], 16)
            sp.dma_start(cw[:], conv_w.rearrange("c a y x -> c (a y x)")).then_inc(S["w_small"], 16)
            sp.dma_start(cb[:, 0:1], conv_b.rearrange("(c a) -> c a", a=1)).then_inc(S["w_small"], 16)
            sp.dma_start(dtb[:], dt_b.rearrange("k c -> c k")).then_inc(S["w_small"], 16)
            sp.dma_start(dsk[:], Ds.rearrange("(k c) -> c k", c=DI)).then_inc(S["w_small"], 16)
            sp.dma_start(opw[:], out_proj_w.rearrange("(o p) c -> p o c", p=CK)).then_inc(S["w_in"], 16)
            for i, v in enumerate((norm_g, norm_b)):
                sp.dma_start(gb[:, i, 0:DI], v.rearrange("(a c) -> a c", a=1).to_broadcast([P, DI])).then_inc(S["w_gb"], 16)
            for i, v in enumerate((ln_g, ln_b)):
                sp.dma_start(gb[:, 2 + i, :], v.rearrange("(a c) -> a c", a=1).to_broadcast([P, CH])).then_inc(S["w_gb"], 16)
            sp.dma_start(qkvw[:, :, 0:CH], w_qkv.rearrange("(o p) c -> p o c", p=CK)).then_inc(S["w_qkv"], 16)
            sp.dma_start(qkvw[:, :, CH], b_qkv.rearrange("(o p) -> p o", p=CK)).then_inc(S["w_qkv"], 16)
            sp.dma_start(proj[:], projection).then_inc(S["w_qkv"], 16)
            sp.dma_start(pjw[:, :, 0:CH], w_proj.rearrange("(o p) c -> p o c", p=CK)).then_inc(S["w_proj"], 16)
            sp.dma_start(pjw[:, :, CH], b_proj.rearrange("(o p) -> p o", p=CK)).then_inc(S["w_proj"], 16)
            for i, (w, b) in enumerate(((Wq, bq), (Wk, bk), (Wv, bv))):
                sp.dma_start(fw[:, i, :, :], w.rearrange("(o p) c -> p o c", p=CK)).then_inc(S["w_ffn"], 16)
                sp.dma_start(fT[:, i, :, CH], b.rearrange("(o p) -> p o", p=CK)).then_inc(S["w_ffn"], 16)
            sp.dma_start(wr[0:CK, :, :], Wr.rearrange("(o p) c -> p o c", p=CK)).then_inc(S["w_wo"], 16)
            sp.dma_start(wr[CK:CK + 1, 1, :], br.rearrange("(a c) -> a c", a=1)).then_inc(S["w_wo"], 16)
            sp.dma_start(wo[:], Wo.rearrange("(o p) c -> p o c", p=CK)).then_inc(S["w_wo"], 16)
            sp.dma_start(wos[0][CK:CK + 1, :], bo.rearrange("(a c) -> a c", a=1)).then_inc(S["w_bo"], 16)

            for n in range(SCANS):
                if n >= 2:
                    sp.wait_ge(S["bc_inp"], UNITS * (n - 1))
                for part, (src, s) in enumerate(((hi, "hi"), (mid, "mid"), (lo, "lo"))):
                    sp.wait_ge(S[s], n + 1)
                    for j in range(CHUNKS):
                        sp.dma_start(stack[CHUNK * part:CHUNK * (part + 1), n % 2, j, :],
                                     src[CHUNK * j:CHUNK * (j + 1), :, :]).then_inc(S["stack"], 16)
            for n in range(IMAGES):
                h, b = n // IMG, n % IMG
                sp.wait_ge(S["fin"], n + 1)
                sp.dma_start(out_d[:, 2 * n:2 * n + 2, :], fin[:, 2 * b:2 * b + 2, :]).then_inc(S["outd"][b], 16)
            for b in range(IMG):
                sp.wait_ge(S["outd"][b], 16 * HALVES)

        @block.gpsimd
        def _(pool):
            g = nc.gpsimd
            g.memset(ident[:], 0.0).then_inc(S["zeroed"], 1)
            g.memset(avg6[:], 1.0 / GN_SIZE).then_inc(S["zeroed"], 1)
            g.memset(pmask[:], 1.0).then_inc(S["zeroed"], 1)
            g.memset(band[:], 1.0).then_inc(S["zeroed"], 1)
            g.memset(spread[:], 0.0).then_inc(S["zeroed"], 1)
            g.memset(dmatch[:], 0.0).then_inc(S["zeroed"], 1)
            g.memset(tri[:], 1.0).then_inc(S["zeroed"], 1)
            pool.wait_ge(S["zeroed"], 7)
            g.affine_select(out=ident[:], in_=ident[:], pattern=[[-1, P]], compare_op=ALU.not_equal, fill=1.0,
                            base=0, channel_multiplier=1).then_inc(S["ident"], 1)
            avg = avg6[:].rearrange("p (g e) -> p g e", e=GN_SIZE)
            groups = CK // GN_SIZE
            at = NS * (DI - GRP)
            g.affine_select(out=avg, in_=avg, pattern=[[-GN_SIZE, groups], [0, GN_SIZE]], compare_op=ALU.is_ge,
                            fill=0.0, base=0, channel_multiplier=1).then_inc(S["const"], 1)
            g.affine_select(out=pmask[:], in_=pmask[:], pattern=[[-HD, HPC], [0, FEAT]], compare_op=ALU.is_ge,
                            fill=0.0, base=0, channel_multiplier=1).then_inc(S["const"], 1)
            g.affine_select(out=band[:], in_=band[:], pattern=[[-NS, 2 * DI - GRP]], compare_op=ALU.is_ge,
                            fill=0.0, base=at, channel_multiplier=1).then_inc(S["const"], 1)
            pool.wait_ge(S["const"], 3)
            g.affine_select(out=avg, in_=avg, pattern=[[GN_SIZE, groups], [0, GN_SIZE]], compare_op=ALU.is_ge,
                            fill=0.0, base=GN_SIZE - 1, channel_multiplier=-1).then_inc(S["const"], 1)
            g.affine_select(out=pmask[:], in_=pmask[:], pattern=[[HD, HPC], [0, FEAT]], compare_op=ALU.is_ge,
                            fill=0.0, base=HD - 1, channel_multiplier=-1).then_inc(S["const"], 1)
            g.affine_select(out=band[:], in_=band[:], pattern=[[NS, 2 * DI - GRP]], compare_op=ALU.is_ge,
                            fill=0.0, base=NS - 1 - at, channel_multiplier=-1).then_inc(S["const"], 1)
            g.memset(neg_half[:], -0.5).then_inc(S["const"], 1)
            g.memset(xpad[:], 0.0).then_inc(S["const"], 1)

            def inv_sqrt(dst, src, ready, count, done):
                pool.wait_ge(S[ready], count)
                g.tensor_tensor(dst, src, neg_half[0:dst.shape[0], 0:dst.shape[1]], ALU.pow).then_inc(S[done], 1)

            pool.wait_ge(S["const"], 8)
            inv_sqrt(grs[:], gve[:], "gn_eps", 1, "gn_rsqrt")
            sel_s = spread[:].rearrange("p q (c n) -> p q c n", n=NS)
            for part in range(3):
                g.affine_select(out=sel_s, in_=sel_s, pattern=[[-GRP, PER_CHUNK], [-1, GRP], [0, NS]],
                                compare_op=ALU.not_equal, fill=1.0, base=-CHUNK * part,
                                channel_multiplier=1).then_inc(S["const2"], 1)
                pool.wait_ge(S["const2"], part + 1)
            g.affine_select(out=tri[:], in_=tri[:], pattern=[[1, HEADS], [-1, HEADS]], compare_op=ALU.is_gt,
                            fill=0.0, base=0, channel_multiplier=0).then_inc(S["const2"], 1)
            for i in range(HPC):
                g.affine_select(out=dmatch[:, 0:HD], in_=dmatch[:, 0:HD], pattern=[[-1, HD]], compare_op=ALU.not_equal,
                                fill=1.0, base=-HD * i, channel_multiplier=1).then_inc(S["const2"], 1)
                pool.wait_ge(S["const2"], 5 + i)
            for j in range(TOPK):
                g.memset(slot_no[:, j:j + 1], float(j)).then_inc(S["const2"], 1)

            def orders(h):
                pool.wait_ge(S["xs0"], IMG * (h + 1))
                grid = xs[:, h, 0, :].rearrange("p (b y x) -> p b x y", b=IMG, x=SIDE)
                rows = xs[:, h, 0, :].rearrange("p (b l) -> p b l", b=IMG)
                for b in range(IMG):
                    g.tensor_copy(xs[:, h, 1, b * L:(b + 1) * L].rearrange("p (x y) -> p x y", x=SIDE),
                                  grid[:, b, :, :]).then_inc(S["xs"], 1)
                g.tensor_copy(xs[:, h, 2, :].rearrange("p (b l) -> p b l", b=IMG), rows[:, :, ::-1]).then_inc(S["xs"], 1)
                for b in range(IMG):
                    g.tensor_copy(xs[:, h, 3, b * L:(b + 1) * L].rearrange("p (x y) -> p x y", x=SIDE),
                                  grid[:, b, ::-1, ::-1]).then_inc(S["xs"], 1)

            def series(n):
                pool.wait_ge(S["sp_exp"], n + 1)
                if n > 0:
                    pool.wait_ge(S["sp_max"], n)
                g.tensor_scalar(sps[:], spe[:], -0.5, 1.0, ALU.mult, ALU.add).then_inc(S["sp_t"], 1)
                pool.wait_ge(S["sp_t"], n + 1)
                g.tensor_tensor(sps[:], sps[:], spe[:], ALU.mult).then_inc(S["sp_s"], 1)

            def left_of_hi(n):
                pool.wait_ge(S["hi"], n + 1)
                g.tensor_tensor(step2[:], step2[:], hi[:], ALU.subtract).then_inc(S["rest"], 1)

            def left_of_mid(n):
                pool.wait_ge(S["mid"], n + 1)
                g.tensor_tensor(lo[:], step2[:], mid[:], ALU.subtract).then_inc(S["lo"], 1)

            def weigh(u):
                n, g12 = u // UNITS, u % UNITS
                if g12 == 0:
                    taken(pool, f"C{n}")
                pool.wait_ge(S["state"], u + 1)
                if u >= SLOTS:
                    pool.wait_ge(S["y_mm"], u - SLOTS + 1)
                g.tensor_tensor(outp[:, u % SLOTS, :], state[:, u % SLOTS, :], c_rep[:, n % 2, :],
                                ALU.mult).then_inc(S["outp"], 1)

            def side(step, n):
                h, b = n // IMG, n % IMG
                ts = slice(2 * b, 2 * b + 2)
                if step == "silu":
                    orders(n)
                for at, (tag, where) in enumerate((("y", "yT"), ("t", "o"), ("u", "p"), ("r", "fo"))):
                    if step == where:
                        inv_sqrt(rs[:, at, ts], mv[:, at, ts, 1], "eps_" + tag, n + 1, "rsqrt_" + tag)
                if step == "yn":
                    pool.wait_ge(S["norm_y"], 3 * (n + 1))
                    g.tensor_tensor(yn[:, ts, :], yn[:, ts, :], z[:, h, ts, :], ALU.mult).then_inc(S["gate"], 1)
                if step == "cr":
                    taken(pool, f"cr_{n}")
                    if n >= IMG:
                        pool.wait_ge(S["sel"], 4 * (n - 1))
                    for i in range(2):
                        for u, w in ((0, 1), (1, 2)):
                            g.tensor_scalar(hot[:, u, i, b, :], slot_no[:], col[:, 0, i, b:b + 1], col[:, w, i, b:b + 1],
                                            ALU.is_equal, ALU.mult).then_inc(S["hot"], 1)
                    pool.wait_ge(S["hot"], 4 * (n + 1))
                    if n >= IMG:
                        fetched(pool, f"wv_{n - IMG}")
                    for i in range(2):
                        g.tensor_tensor(sel_m[:, b, i, :, :], dmatch[:].unsqueeze(1).to_broadcast([CK, TOPK, 2 * HD]),
                                        hot[:, 0, i, b, :].unsqueeze(2).to_broadcast([CK, TOPK, 2 * HD]), ALU.mult).then_inc(S["sel"], 1)
                        g.tensor_tensor(sel_u[:, b, i, :, :], dmatch[:, 0:HD].unsqueeze(1).to_broadcast([CK, TOPK, HD]),
                                        hot[:, 1, i, b, :].unsqueeze(2).to_broadcast([CK, TOPK, HD]), ALU.mult).then_inc(S["sel"], 1)
                if step == "rn":
                    pool.wait_ge(S["norm_r"], 4 * (n + 1))
                    if n >= IMG:
                        pool.wait_ge(S["outd"][b], 16 * h)
                    g.tensor_tensor(fin[:, ts, :], tn[:, ts, :], x_tok[:, 2 * n:2 * n + 2, :], ALU.add).then_inc(S["fin"], 1)

            orders(0)
            series(0)
            left_of_hi(0)
            left_of_mid(0)
            for u in range(SLOT_COUNT):
                n, g12 = pre_at(u)
                if u > 0:
                    weigh(u - 1)
                if n < SCANS and g12 == PRE_CLIP:
                    series(n)
                if n < SCANS and g12 == PRE_HI:
                    left_of_hi(n)
                if n < SCANS and g12 == PRE_LO:
                    left_of_mid(n)
                for item in beside[u]:
                    side(*item)
            weigh(SLOT_COUNT - 1)
            for item in rest:
                side(*item)

        @block.scalar
        def _(act):
            a = nc.scalar

            def evac(name, *copies):
                fetched(act, name)
                for dst, src in copies:
                    ins = a.copy(dst, src)
                ins.then_inc(freed(name), 1)

            a.preload_act_table_set("natural_log_exp_and_others")
            evac("w_in", (inT[:].rearrange("p a b -> p (a b)"), bank("w_in")[0:CK, 0:2 * CH]))
            src = bank("w_xp")[0:DI, 0:DIRS * XROWS].rearrange("p (k r) -> p k r", k=DIRS)
            evac("w_xp", *[(pre_w[:, k, DI + i * P:DI + (i + 1) * P].rearrange("p (c n) -> p c n", n=NS),
                            src[:, k, RANK + NS * i:RANK + NS * (i + 1)].unsqueeze(1).to_broadcast([DI, GRP, NS]))
                           for i in range(2) for k in range(DIRS)])
            evac("w_dt", (dtT[:].rearrange("p a b -> p (a b)"), bank("w_dt")[0:RANK, 0:DIRS * DI]))
            evac("w_fold", (pre_w[:, :, 0:DI], bank("w_fold")[0:DI, 0:DIRS * DI].rearrange("p (k c) -> p k c", k=DIRS)))
            taken(act, "w_alog")
            a.activation(a_neg[:], a_log[:], ACT.Exp).then_inc(S["a_exp"], 1)
            act.wait_ge(S["gn_bias"], 1)

            def group_normed(h):
                for c in range(2):
                    for b in range(IMG):
                        s = c * IMAGES + h * IMG + b
                        a.activation(xnT[:, c, h * TOK + b * L:h * TOK + (b + 1) * L],
                                     gn_banks[2 * h + c][0:CK, b * L:(b + 1) * L],
                                     ACT.Identity, bias=gbi[:, s:s + 1], scale=grs[:, s:s + 1]).then_inc(S["xn"], 1)

            def front(step, h):
                if step == "xh":
                    if h:
                        act.wait_ge(S["conv"], 9 * h)
                    evac(f"xh_{h}", *[(xpad[:, b, 1:SIDE + 1, 1:SIDE + 1],
                                       bank(f"xh_{h}")[0:DI, b * L:(b + 1) * L].rearrange("p (y x) -> p y x", y=SIDE))
                                      for b in range(IMG)])
                if step == "z":
                    src = bank(f"z_{h}")[:, 0:TILES * DI].rearrange("p (t c) -> p t c", t=TILES)
                    fetched(act, f"z_{h}")
                    a.copy(z[:, h, :, :], src).then_inc(S["z_kept"], 1)
                    if h:
                        act.wait_ge(S["gate_s"], h)
                    a.activation(ze[:], src, ACT.Exp, scale=-1.0).then_inc(freed(f"z_{h}"), 1)
                    taken(act, f"z_{h}")
                    a.activation(ze[:], ze[:], ACT.Ln, bias=1.0).then_inc(S["gate_e"], 1)
                    act.wait_ge(S["gate_e"], 2 * h + 1)
                    a.activation(ze[:], ze[:], ACT.Exp, scale=-1.0).then_inc(S["gate_e"], 1)
                if step == "silu":
                    act.wait_ge(S["conv"], 9 * (h + 1))
                    if h:
                        act.wait_ge(S["xs0"], IMG * h)
                    for b in range(IMG):
                        a.activation(sg[:, b * L:(b + 1) * L], conv_out[b], ACT.Exp, scale=-1.0).then_inc(S["conv_e"], 1)
                    act.wait_ge(S["conv_e"], 4 * h + 2)
                    a.activation(sg[:], sg[:], ACT.Ln, bias=1.0).then_inc(S["conv_e"], 1)
                    act.wait_ge(S["conv_e"], 4 * h + 3)
                    a.activation(sg[:], sg[:], ACT.Exp, scale=-1.0).then_inc(S["conv_e"], 1)

            group_normed(0)
            act.wait_ge(S["const"], 8)
            front("xh", 0)
            front("silu", 0)
            group_normed(1)

            def weights(step):
                if step == "w_out":
                    evac("w_out", (outT[:], bank("w_out")[0:DI, 0:CH]))
                elif step[:4] == "w_qk":
                    i, rc, c = (int(d) for d in step[4:])
                    rows, n = CK + c, HPC * FEAT
                    dst = qw[0:rows, c, rc * n:(rc + 1) * n] if i == 0 else kvw[0:rows, c, rc, 0:n]
                    evac(step, (dst, bank(step)[0:rows, 0:n]))
                elif step in ("w_v", "w_proj"):
                    srcs = bank(step)[:, 0:2 * CH].rearrange("p (c o k) -> p c o k", c=2, o=2)
                    dsts = [kvw[0:CK + c, c, :, HPC * FEAT:] if step == "w_v" else
                            pjT[0:CK + c, c, :].rearrange("p (o k) -> p o k", o=2) for c in range(2)]
                    evac(step, *[(dsts[c], srcs[0:CK + c, c, :, :]) for c in range(2)])
                elif step[:3] == "w_f":
                    evac(step, (fT[:, int(step[3]), :, 0:CH], bank(step)[0:CK, 0:2 * CH].rearrange("p (o k) -> p o k", o=2)))

            def pre_softplus(n):
                act.wait_ge(S["sp_in"], n + 1)
                if n > 0:
                    act.wait_ge(S["sp_s"], n)
                a.activation(spe[:], spl[:], ACT.Exp).then_inc(S["sp_exp"], 1)
                act.wait_ge(S["sp_exp"], n + 1)
                a.activation(spl[:], spe[:], ACT.Ln, bias=1.0).then_inc(S["sp_ln"], 1)

            def pre_bc(n, which):
                name, dst, gone = (f"B{n}", b_rep, "drive") if which == "B" else (f"C{n}", c_rep, "outp")
                fetched(act, name)
                if n >= 2:
                    act.wait_ge(S[gone], UNITS * (n - 1))
                a.copy(dst[:, n % 2, :], bank(name)[:, :]).then_inc(freed(name), 1)

            def pre_hi(n):
                act.wait_ge(S["step"], n + 1)
                if n > 0:
                    act.wait_ge(S["stack"], 16 * 9 * n)
                a.copy(hi[:], step2[:]).then_inc(S["hi"], 1)

            def pre_mid(n):
                act.wait_ge(S["rest"], n + 1)
                a.copy(mid[:], step2[:]).then_inc(S["mid"], 1)

            def expo(u):
                act.wait_ge(S["bc_step"], u + 1)
                if u >= SLOTS:
                    act.wait_ge(S["state"], u - SLOTS + 1)
                at = u % (DIRS * UNITS)
                a.activation(decay[:, u % SLOTS, :, 1:L],
                             step_bc[u % 2][:, :].rearrange("p (b l) -> p b l", b=IMG)[:, :, 1:L],
                             ACT.Exp, scale=a_neg[:, at:at + 1]).then_inc(S["decay"], 1)

            def keep_y(n):
                if n == DIRS:
                    act.wait_ge(S["y_sum"], 1)
                act.wait_ge(S["y_mm"], UNITS * (n + 1))
                a.copy(y_dir[:, n % DIRS, :], y_acc[0:DI, :]).then_inc(S["y_ev"], 1)

            def exp_scores(n, j):
                p, before = of_set(n)
                m = before * TOPK + j
                name = f"s{n}{j}"
                act.wait_ge(S["prob_bias"][p], m + 1)
                if m >= 2:
                    fetched(act, f"pt{n - (j < 2)}{(j - 2) % TOPK}")
                    act.wait_ge(S["prob_rec"][p], m - 1)
                for q in range(2):
                    a.activation(prob[p][:, m % 2, q, :], bank(name)[:, q * L:(q + 1) * L], ACT.Exp,
                                 bias=nmaxs[p][:, m % 2, q:q + 1], scale=HD ** -0.5,
                                 accum_out=psum_row[p][:, m % 2, q:q + 1]).then_inc(S["prob"][p] if q == 0 else freed(name), 1)

            def side(step, n):
                h, b = n // IMG, n % IMG
                name = f"{step}_{n}"
                img = slice(b * L, (b + 1) * L)
                p, before = of_set(n)
                if step in WEIGHT_STEPS:
                    weights(step)
                elif step in ("xh", "z", "silu"):
                    front(step, n)
                elif step == "gT":
                    evac(name, (gT[:, img], bank(name)[0:DI, 0:L]))
                elif step in ("tT", "aT"):
                    if step == "tT" and n >= IMG:
                        fetched(act, f"fv_{n - IMG}")
                    evac(name, (tT[0:CK, :, img], bank(name)[0:CK, :].rearrange("p (c l) -> p c l", c=2)))
                elif step == "hT":
                    fetched(act, name)
                    for c in range(2):
                        a.activation(hT[0:CK, c, img], bank(name)[0:CK, c * L:(c + 1) * L], ACT.Copy,
                                     accum_out=rin[0:CK, c, b:b + 1]).then_inc(S["router_in"] if c == 0 else freed(name), 1)
                elif step[:2] == "kv":
                    t, j = 2 * b + int(step[2]), int(step[3])
                    fetched(act, name)
                    act.wait_ge(S["key"], key_count(n, step))
                    a.copy(v1[:, t, j * HPC:(j + 1) * HPC, 0:HD],
                           bank(name)[:, HPC * FEAT:HPC * FEAT + CK].rearrange("p (h d) -> p h d", d=HD)).then_inc(freed(name), 1)
                elif step == "cx":
                    fetched(act, name)
                    src = bank(name)[:, 0:PAIRS * 2 * (HD + 1)].rearrange("p (i d) -> p i d", i=PAIRS)
                    a.copy(cbd[0:FEAT, b, :, 0:HD + 1], src[0:FEAT, :, 0:HD + 1]).then_inc(S["ctx_lo"], 1)
                    a.copy(cbd[FEAT:P, b, :, HD + 1:], src[FEAT:P, :, HD + 1:]).then_inc(freed(name), 1)
                elif step in ("wq", "wk"):
                    i = int(step == "wk")
                    if before:
                        fetched(act, f"fo_{n - 1}")
                    src = bank(name)[:, 0:2 * CH].rearrange("p (c k) -> p c k", c=2)
                    evac(name, (wsel[p][0:CK, i, 0, :], src[0:CK, 0, :]), (wsel[p][0:CK + 1, i, 1, :], src[0:CK + 1, 1, :]))
                elif step == "wv":
                    src = bank(name)
                    if n == 0:
                        act.wait_ge(S["w_bo"], 16)
                    evac(name, (wsv[p][0:CK, 0, :], src[0:CK, 0:CK]), (wsv[p][0:CK + 1, 1, :], src[0:CK + 1, CK:2 * CK]),
                         (wos[p][0:CK, :], src[0:CK, CH:2 * CH]))
                elif step in ("fq", "fk"):
                    dst = (fq if step == "fq" else fk)[p]
                    evac(name, (dst[:, 0, :], bank(name)[:, 0:L]), (dst[0:64, 1, :], bank(name)[0:64, L:2 * L]))
                elif step == "fv":
                    evac(name, (fv[p][:].rearrange("p a b -> p (a b)"), bank(name)[:, 0:2 * CK]))
                elif step[0] == "h" and int(step[1:]) < TOPK:
                    exp_scores(n, int(step[1:]))
                elif step == "cT":
                    evac(name, (cT[p][0:CK, :], bank(name)[0:CK, 0:L]))

            pre_softplus(0)
            front("z", 0)
            pre_bc(0, "B")
            pre_bc(0, "C")
            pre_hi(0)
            pre_mid(0)
            act.wait_ge(S["neg_a"], 1)
            act.wait_ge(S["ones"], ONES)
            for u in range(SLOT_COUNT):
                n, g12 = pre_at(u)
                expo(u)
                if g12 == 3 and u > UNITS:
                    keep_y(n - 2)
                if n < SCANS:
                    if g12 == PRE_CLIP:
                        pre_softplus(n)
                    if g12 == PRE_HI:
                        pre_hi(n)
                    if g12 == PRE_MID:
                        pre_mid(n)
                for item in beside[u]:
                    side(*item)
                if n < SCANS and g12 == PRE_B:
                    pre_bc(n, "B")
                if n < SCANS and g12 == PRE_C:
                    pre_bc(n, "C")
            keep_y(SCANS - 1)
            act.wait_ge(S["wos_row"], 2)
            for item in rest:
                side(*item)

        @block.vector
        def _(dve):
            v = nc.vector

            v.memset(decay[:], 0.0).then_inc(S["ones"], 1)
            v.memset(tT[CK:CK + 1, :, :], 1.0).then_inc(S["ones"], 1)
            v.memset(cT[0][CK:CK + 1, :], 1.0).then_inc(S["ones"], 1)
            v.memset(v1[:, :, :, HD:HD + 1], 1.0).then_inc(S["ones"], 1)
            v.memset(cbd[:], 0.0).then_inc(S["ones"], 1)
            v.memset(rin[CK:CK + 1, :, :], float(L)).then_inc(S["ones"], 1)

            for i in range(4):
                h, c = i // 2, i % 2
                dve.wait_ge(S["gn_turned"], i + 1)
                for b in range(IMG):
                    v.bn_stats(gst[:, c * IMAGES + h * IMG + b, :], gn_banks[i][0:CK, b * L:(b + 1) * L]).then_inc(S["gn_stats"], 1)
            dve.wait_ge(S["gn_stats"], 8)
            for s in range(8):
                v.bn_aggr(gmv[:, s, :], gst[:, s, :]).then_inc(S["gn_stats"], 1)
            fetched(dve, "w_alog")
            v.tensor_scalar(a_log[:], bank("w_alog")[:, 0:DIRS * UNITS], LOG_MAX, None, ALU.min).then_inc(freed("w_alog"), 1)
            fetched(dve, "gm")
            dve.wait_ge(S["gn_stats"], 16)
            v.tensor_copy(gmean[:], bank("gm")[0:CK, 0:8]).then_inc(freed("gm"), 1)
            taken(dve, "gm")
            v.tensor_tensor(gdv[:], gmv[:, :, 0], gmean[:], ALU.subtract).then_inc(S["gn_dev"], 1)
            dve.wait_ge(S["gn_dev"], 1)
            v.tensor_tensor(gsq[:], gdv[:], gdv[:], ALU.mult).then_inc(S["gn_dev"], 1)
            dve.wait_ge(S["gn_dev"], 2)
            v.tensor_tensor(gva[:], gsq[:], gmv[:, :, 1], ALU.add).then_inc(S["gn_var"], 1)
            fetched(dve, "gv")
            v.tensor_scalar(gve[:], bank("gv")[0:CK, 0:8], 1e-5, None, ALU.add).then_inc(freed("gv"), 1)
            taken(dve, "gv")
            v.tensor_scalar(gmean[:], gmean[:], -1.0, None, ALU.mult).then_inc(S["gn_eps"], 1)
            dve.wait_ge(S["gn_rsqrt"], 1)
            v.tensor_tensor(gbi[:], gmean[:], grs[:], ALU.mult).then_inc(S["gn_bias"], 1)

            dve.wait_ge(S["w_small"], 64)
            v.reduce_sum(dsum[:], dsk[:], AX_X).then_inc(S["small"], 1)

            def front(step, h):
                if step in ("conv0", "conv1"):
                    for i in (range(5) if step == "conv0" else range(5, 9)):
                        window = xpad[:].rearrange("p b y x -> p (b y) x")[:, i // 3:i // 3 + ACC_ROWS, i % 3:i % 3 + SIDE]
                        sums = acc[:]
                        if i == 0:
                            taken(dve, f"xh_{h}")
                            if h:
                                dve.wait_ge(S["xs0"], IMG * h)
                            v.tensor_scalar(sums, window, cw[:, 0:1], cb[:, 0:1], ALU.mult, ALU.add).then_inc(S["conv"], 1)
                        else:
                            dve.wait_ge(S["conv"], 9 * h + i)
                            v.scalar_tensor_tensor(sums, window, cw[:, i:i + 1], sums, ALU.mult, ALU.add).then_inc(S["conv"], 1)
                if step == "silu":
                    dve.wait_ge(S["conv"], 9 * (h + 1))
                    dve.wait_ge(S["conv_e"], 4 * (h + 1))
                    for b in range(IMG):
                        img = slice(b * L, (b + 1) * L)
                        v.tensor_tensor(xs[:, h, 0, img], conv_out[b], sg[:, img], ALU.mult).then_inc(S["xs0"], 1)
                if step == "z":
                    dve.wait_ge(S["z_kept"], h + 1)
                    dve.wait_ge(S["gate_e"], 2 * (h + 1))
                    v.tensor_tensor(z[:, h, :, :], z[:, h, :, :], ze[:], ALU.mult).then_inc(S["gate_s"], 1)

            def weights(step):
                if step == "w_out":
                    dve.wait_ge(S["w_qkv"], 48)
                    dve.wait_ge(S["ident"], 1)
                    v.tensor_copy(prep[:], proj[:].unsqueeze(1).to_broadcast([FEAT, HPC, HD])).then_inc(S["repl"], 1)
                    v.tensor_copy(irep[:], ident[0:FEAT, 0:FEAT].unsqueeze(1).to_broadcast([FEAT, HPC, FEAT])).then_inc(S["repl"], 1)
                if step == "w_pbd":
                    fetched(dve, "w_pbd")
                    dve.wait_ge(S["const"], 8)
                    v.scalar_tensor_tensor(pbd[:], bank("w_pbd")[0:CK, 0:HPC * FEAT], float(HD) ** -0.25,
                                           pmask[:].rearrange("p a b -> p (a b)"), ALU.mult, ALU.mult).then_inc(freed("w_pbd"), 1)

            front("conv0", 0)
            front("conv1", 0)
            dve.wait_ge(S["a_exp"], 1)
            v.tensor_scalar(a_neg[:], a_neg[:], -1.0, None, ALU.mult).then_inc(S["neg_a"], 1)
            front("silu", 0)

            def pre_clip(n):
                fetched(dve, f"d{n}")
                v.tensor_scalar(spl[:], bank(f"d{n}")[0:DI, :], dtb[:, n % DIRS:n % DIRS + 1], SOFTPLUS_LINEAR,
                                ALU.add, ALU.min).then_inc(S["sp_in"], 1)

            def pre_step(n):
                h, k = n // DIRS, n % DIRS
                dve.wait_ge(S["sp_ln"], n + 1)
                v.scalar_tensor_tensor(spl[:], spe[:], SERIES_BELOW, spl[:], ALU.is_ge, ALU.mult).then_inc(S["sp_l"], 1)
                if n > 0:
                    dve.wait_ge(S["lo"], n)
                dve.wait_ge(S["sp_l"], n + 1)
                v.scalar_tensor_tensor(spl[:], bank(f"d{n}")[0:DI, :], dtb[:, k:k + 1], spl[:],
                                       ALU.add, ALU.max).then_inc(freed(f"d{n}"), 1)
                taken(dve, f"d{n}")
                dve.wait_ge(S["sp_s"], n + 1)
                v.tensor_tensor(step2[:, 0, :], spl[:], sps[:], ALU.max).then_inc(S["sp_max"], 1)
                dve.wait_ge(S["sp_max"], n + 1)
                if k > 0:
                    dve.wait_ge(S["xs"], 5 * (h + 1))
                v.tensor_tensor(step2[:, 1, :], step2[:, 0, :], xs[:, h, k, :], ALU.mult).then_inc(S["step"], 1)

            def drive_of(u):
                n = u // UNITS
                if u % UNITS == 0:
                    taken(dve, f"B{n}")
                if u >= SLOTS:
                    dve.wait_ge(S["state"], u - SLOTS + 1)
                dve.wait_ge(S["bc_inp"], u + 1)
                v.tensor_tensor(drive[:, u % SLOTS, :], b_rep[:, n % 2, :], inp_bc[u % 2][:, :],
                                ALU.mult).then_inc(S["drive"], 1)

            def scan(u):
                dve.wait_ge(S["drive"], u + 1)
                dve.wait_ge(S["decay"], u + 1)
                if u >= SLOTS:
                    dve.wait_ge(S["outp"], u - SLOTS + 1)
                v.tensor_tensor_scan(state[:, u % SLOTS, :], decay[:, u % SLOTS, :, :].rearrange("p b l -> p (b l)"),
                                     drive[:, u % SLOTS, :], 0.0, ALU.mult, ALU.add).then_inc(S["state"], 1)

            def merge_y(h):
                dve.wait_ge(S["y_ev"], DIRS * (h + 1))
                dve.wait_ge(S["small"], 1)
                turned = y_sum[:, h, :].rearrange("p (b y x) -> p b x y", b=IMG, x=SIDE)
                v.scalar_tensor_tensor(y_sum[:, h, :], xs[:, h, 0, :], dsum[:, 0:1], y_dir[:, 0, :],
                                       ALU.mult, ALU.add).then_inc(S["y_part"], 1)
                dve.wait_ge(S["y_part"], 5 * h + 1)
                for b in range(IMG):
                    src = y_dir[:, 1, b * L:(b + 1) * L].rearrange("p (x y) -> p x y", x=SIDE)
                    v.tensor_tensor(turned[:, b, :, :], turned[:, b, :, :], src, ALU.add).then_inc(S["y_part"], 1)
                dve.wait_ge(S["y_part"], 5 * h + 3)
                for b in range(IMG):
                    src = y_dir[:, 3, b * L:(b + 1) * L].rearrange("p (x y) -> p x y", x=SIDE)[:, ::-1, ::-1]
                    v.tensor_tensor(turned[:, b, :, :], turned[:, b, :, :], src, ALU.add).then_inc(S["y_part"], 1)
                dve.wait_ge(S["y_part"], 5 * h + 5)
                rows = y_sum[:, h, :].rearrange("p (b l) -> p b l", b=IMG)
                v.tensor_tensor(rows, rows, y_dir[:, 2, :].rearrange("p (b l) -> p b l", b=IMG)[:, :, ::-1],
                                ALU.add).then_inc(S["y_sum"], 1)

            def statistics(n, i, src_of, tag, eps):
                b = n % IMG
                for t in range(2):
                    v.bn_stats(mst[:, i, 2 * b + t, :], src_of(t)).then_inc(S["stat_" + tag], 1)
                dve.wait_ge(S["stat_" + tag], 2 * (n + 1))
                for t in range(2):
                    v.bn_aggr(mv[:, i, 2 * b + t, :], mst[:, i, 2 * b + t, :]).then_inc(S["agg_" + tag], 1)
                dve.wait_ge(S["agg_" + tag], 2 * (n + 1))
                v.tensor_scalar(mv[:, i, 2 * b:2 * b + 2, 1], mv[:, i, 2 * b:2 * b + 2, 1], eps, None, ALU.add).then_inc(S["eps_" + tag], 1)

            def normed(n, i, dst, src_of, tag):
                b = n % IMG
                dve.wait_ge(S["rsqrt_" + tag], n + 1)
                for t in range(2):
                    v.tensor_scalar(dst[:, 2 * b + t, :], src_of(t), mv[:, i, 2 * b + t, 0:1], rs[:, i, 2 * b + t:2 * b + t + 1],
                                    ALU.subtract, ALU.mult).then_inc(S["norm_" + tag], 1)

            def normed_affine(n, i, dst, src_of, tag, gain, bias, product=None):
                b = n % IMG
                dve.wait_ge(S["rsqrt_" + tag], n + 1)
                dve.wait_ge(S["w_gb"], 64)
                each = 3 if product else 4
                for t in range(2):
                    v.scalar_tensor_tensor(dst[:, 2 * b + t, :], src_of(t), mv[:, i, 2 * b + t, 0:1], gain, ALU.subtract,
                                           ALU.mult).then_inc(freed(product) if product and t == 1 else S["norm_" + tag], 1)
                dve.wait_ge(S["norm_" + tag], each * n + each - 2)
                if product:
                    taken(dve, product)
                for t in range(2):
                    v.scalar_tensor_tensor(dst[:, 2 * b + t, :], dst[:, 2 * b + t, :], rs[:, i, 2 * b + t:2 * b + t + 1], bias,
                                           ALU.mult, ALU.add).then_inc(S["norm_" + tag], 1)

            def residual(dst, src, name):
                fetched(dve, name)
                v.tensor_tensor(dst, src, bank(name)[:, 0:2 * CH].rearrange("p (t c) -> p t c", t=2), ALU.add).then_inc(freed(name), 1)
                taken(dve, name)

            def route(n):
                b = n % IMG
                name = f"lg_{n}"
                fetched(dve, name)
                lg_, val_, rank_, msum_ = lg[:, b, :], val[:, b, :, :], rank[:, b, :], msum[:, b, :]
                v.tensor_scalar(lg_, bank(name)[0:1, 0:HEADS], 1.0 / L, None, ALU.mult).then_inc(freed(name), 1)
                taken(dve, name)
                li = lg_.unsqueeze(2).to_broadcast([1, HEADS, HEADS])
                lj = lg_.unsqueeze(1).to_broadcast([1, HEADS, HEADS])
                v.tensor_tensor(eq[:], lj, li, ALU.is_equal).then_inc(S["logit_eq"], 1)
                v.tensor_tensor(gt[:], lj, li, ALU.is_gt).then_inc(S["rank"], 1)
                dve.wait_ge(S["logit_eq"], n + 1)
                v.tensor_tensor(eqt[:], eq[:], tri[:], ALU.mult).then_inc(S["rank"], 1)
                dve.wait_ge(S["rank"], 5 * n + 2)
                v.tensor_tensor(eq[:], gt[:], eqt[:], ALU.add).then_inc(S["rank"], 1)
                dve.wait_ge(S["rank"], 5 * n + 3)
                v.reduce_sum(rank_, eq[:], AX_X).then_inc(S["rank"], 1)
                dve.wait_ge(S["rank"], 5 * n + 4)
                v.tensor_scalar(val_[:, 2, :], rank_, float(TOPK), None, ALU.is_lt).then_inc(S["rank"], 1)
                dve.wait_ge(S["rank"], 5 * n + 5)
                v.tensor_tensor(gt[:], tri[:], val_[:, 2, :].unsqueeze(1).to_broadcast([1, HEADS, HEADS]), ALU.mult).then_inc(S["slot_of"], 1)
                v.tensor_tensor(msum_, val_[:, 2, :], lg_, ALU.add).then_inc(S["slot_of"], 1)
                dve.wait_ge(S["slot_of"], 2 * (n + 1))
                v.reduce_sum(val_[:, 0, :], gt[:], AX_X).then_inc(S["vals"], 1)
                v.tensor_tensor(val_[:, 1, :], msum_, lg_, ALU.subtract).then_inc(S["vals"], 1)
                dve.wait_ge(S["vals"], 2 * (n + 1))
                v.tensor_copy(valr[:, b, :, :], val_.rearrange("p a b -> p (a b)").unsqueeze(2).to_broadcast([1, 3 * HEADS, HD])).then_inc(S["val_rows"], 1)

            def row_max(n, j):
                p, before = of_set(n)
                m = before * TOPK + j
                name = f"s{n}{j}"
                fetched(dve, name)
                v.tensor_reduce(nmax[p][:, m % 2, :], bank(name)[:, :].rearrange("p (q k) -> p q k", q=2), AX_X, ALU.max).then_inc(S["prob_max"][p], 1)
                dve.wait_ge(S["prob_max"][p], m + 1)
                if m >= 2:
                    dve.wait_ge(S["prob"][p], m - 1)
                v.tensor_scalar(nmaxs[p][:, m % 2, :], nmax[p][:, m % 2, :], -(HD ** -0.5), None, ALU.mult).then_inc(S["prob_bias"][p], 1)

            def turned(n, j):
                p, before = of_set(n)
                m = before * TOPK + j
                name = f"pt{n}{j}"
                fetched(dve, name)
                if m >= 2:
                    fetched(dve, f"pv{n - (j < 2)}{(j - 2) % TOPK}")
                v.tensor_copy(probT[p][:, m % 2, :, :].rearrange("p a b -> p (a b)"), bank(name)[:, :]).then_inc(freed(name), 1)
                taken(dve, f"s{n}{j}")
                v.reciprocal(prec[p][:, m % 2, :], psum_row[p][:, m % 2, :]).then_inc(S["prob_rec"][p], 1)

            def weighted(n, j):
                p, before = of_set(n)
                m = before * TOPK + j
                name = f"pv{n}{j}"
                fetched(dve, name)
                dve.wait_ge(S["prob_rec"][p], m + 1)
                v.tensor_tensor(cx[p][:, :, j * HD:(j + 1) * HD], bank(name)[:, 0:2 * HD].rearrange("p (q d) -> p q d", q=2),
                                prec[p][:, m % 2, :].unsqueeze(2).to_broadcast([P, 2, HD]), ALU.mult).then_inc(freed(name), 1)

            def side(step, n):
                h, b = n // IMG, n % IMG
                p, before = of_set(n)
                name = f"{step}_{n}"
                ts = slice(2 * b, 2 * b + 2)
                tk = x_tok[:, 2 * n:2 * n + 2, :]
                if step in WEIGHT_STEPS:
                    weights(step)
                elif step in ("conv0", "conv1", "z", "silu"):
                    front(step, n)
                elif step == "yT":
                    fetched(dve, name)
                    statistics(n, 0, lambda t: bank(name)[:, t * DI:(t + 1) * DI], "y", 1e-5)
                elif step == "yn":
                    src = f"yT_{n}"
                    normed_affine(n, 0, yn, lambda t: bank(src)[:, t * DI:(t + 1) * DI], "y", gb[:, 0, 0:DI], gb[:, 1, 0:DI], src)
                elif step == "o":
                    residual(tk, tk, name)
                    statistics(n, 1, lambda t: tk[:, t, :], "t", 1e-5)
                elif step == "tn":
                    normed(n, 1, tn, lambda t: tk[:, t, :], "t")
                elif step[0] == "q":
                    fetched(dve, name)
                    i = 2 * int(step[1])
                    v.tensor_scalar(qp[:, i:i + 2, b * L:(b + 1) * L], bank(name)[:, :].rearrange("p (i l) -> p i l", i=2),
                                    KERNEL_EPS, KERNEL_EPS, ALU.add, ALU.max).then_inc(freed(name), 1)
                elif step[:2] == "kv":
                    t, j, w = 2 * b + int(step[2]), int(step[3]), HPC * FEAT
                    fetched(dve, name)
                    v.tensor_scalar(kp[:, t, j * w:(j + 1) * w], bank(name)[:, 0:w], KERNEL_EPS, KERNEL_EPS,
                                    ALU.add, ALU.max).then_inc(S["key"], 1)
                elif step == "at":
                    fetched(dve, name)
                    src = bank(name)[:, 0:2 * HEADS * (HD + 1)].rearrange("p (t h d) -> p t h d", t=2, h=HEADS)
                    v.reciprocal(arec[:, ts, :].unsqueeze(3), src[:, :, :, HD:HD + 1]).then_inc(S["a_rec"], 1)
                    dve.wait_ge(S["a_rec"], n + 1)
                    for t in range(2):
                        v.tensor_tensor(ao[:, 2 * b + t, :].rearrange("p (h d) -> p h d", d=HD), src[:, t, :, 0:HD],
                                        arec[:, 2 * b + t, :].unsqueeze(2).to_broadcast([P, HEADS, HD]),
                                        ALU.mult).then_inc(S["att"] if t == 0 else freed(name), 1)
                elif step == "p":
                    residual(tk, tk, name)
                    statistics(n, 2, lambda t: tk[:, t, :], "u", 1e-5)
                elif step == "un":
                    normed(n, 2, hn, lambda t: tk[:, t, :], "u")
                elif step == "lg":
                    route(n)
                elif step == "cr":
                    fetched(dve, name)
                    if n >= IMG:
                        dve.wait_ge(S["hot"], 4 * (n - 1))
                    v.tensor_copy(col[:, :, :, b], bank(name)[0:CK, 0:6].rearrange("p (u i) -> p u i", u=3)).then_inc(freed(name), 1)
                elif step[0] == "h" and step != "hT":
                    j = int(step[1:])
                    if j < TOPK:
                        row_max(n, j)
                    if j > 1:
                        weighted(n, j - 2)
                    if 0 < j <= TOPK:
                        turned(n, j - 1)
                elif step == "fo":
                    residual(res[:, ts, :], hn[:, ts, :], name)
                    statistics(n, 3, lambda t: res[:, 2 * b + t, :], "r", 1e-12)
                elif step == "rn":
                    normed_affine(n, 3, tn, lambda t: res[:, 2 * b + t, :], "r", gb[:, 2, :], gb[:, 3, :])

            pre_clip(0)
            pre_step(0)
            front("z", 0)
            for u in range(SLOT_COUNT):
                n, g12 = pre_at(u)
                drive_of(u)
                if u > 0:
                    scan(u - 1)
                if n < SCANS and g12 == PRE_CLIP:
                    pre_clip(n)
                if n < SCANS and g12 == PRE_STEP:
                    pre_step(n)
                if u == DIRS * UNITS + 4:
                    merge_y(0)
                for item in beside[u]:
                    side(*item)
            scan(SLOT_COUNT - 1)
            merge_y(1)
            dve.wait_ge(S["outp"], SLOT_COUNT)
            v.memset(cT[1][CK:CK + 1, :], 1.0).then_inc(S["wos_row"], 1)
            v.tensor_copy(wos[1][CK:CK + 1, :], wos[0][CK:CK + 1, :]).then_inc(S["wos_row"], 1)
            for item in rest:
                side(*item)

        @block.tensor
        def _(pe):
            t_ = nc.tensor
            idn = ident[:]

            def begin(name):
                reuse(pe, name)
                return bank(name)

            def done(ins):
                ins.then_inc(S["filled"], 1)

            pe.wait_ge(S["ident"], 1)
            for i in range(4):
                h, c = i // 2, i % 2
                if c == 0:
                    pe.wait_ge(S["x"][h], 16)
                for t in range(TILES):
                    ins = t_.transpose(gn_banks[i][0:CK, t * P:(t + 1) * P], x_tok[:, h * TILES + t, c * CK:(c + 1) * CK], idn)
                ins.then_inc(S["gn_turned"], 1)

            b_ = begin("w_in")
            pe.wait_ge(S["w_in"], 32)
            for ic in range(2):
                for oc in range(2):
                    ins = t_.transpose(b_[0:CK, (2 * ic + oc) * CK:(2 * ic + oc + 1) * CK], inw[:, oc, ic * CK:(ic + 1) * CK], ident[0:DI, 0:DI])
            done(ins)
            b_ = begin("w_xp")
            pe.wait_ge(S["w_xp"], 32)
            for k in range(DIRS):
                ins = t_.transpose(b_[0:DI, k * XROWS:(k + 1) * XROWS], xpw[:, k, :], ident[0:XROWS, 0:XROWS])
            done(ins)
            b_ = begin("w_dt")
            for k in range(DIRS):
                ins = t_.transpose(b_[0:RANK, k * DI:(k + 1) * DI], dtw[:, k, :], ident[0:DI, 0:DI])
            done(ins)
            b_ = begin("w_fold")
            taken(pe, "w_dt")
            for k in range(DIRS):
                ins = t_.matmul(b_[0:DI, k * DI:(k + 1) * DI], xpw[0:RANK, k, :], dtT[:, k, :], start=True, stop=True)
            done(ins)
            b_ = begin("w_alog")
            pe.wait_ge(S["w_alog"], 16)
            done(t_.transpose(b_[:, 0:DIRS * UNITS], alog[:], ident[0:DIRS * UNITS, 0:DIRS * UNITS]))

            b_ = begin("gm")
            pe.wait_ge(S["const"], 8)
            pe.wait_ge(S["gn_stats"], 16)
            done(t_.matmul(b_[0:CK, 0:8], avg6[:], gmv[:, :, 0], start=True, stop=True))
            b_ = begin("gv")
            pe.wait_ge(S["gn_var"], 1)
            done(t_.matmul(b_[0:CK, 0:8], avg6[:], gva[:], start=True, stop=True))
            taken(pe, "w_in")

            def front(step, h):
                b_ = begin(f"{step}_{h}")
                pe.wait_ge(S["xn"], 4 * (h + 1))
                if step == "xh":
                    for c in range(2):
                        ins = t_.matmul(b_[0:DI, :], inT[:, c, 0:DI], xnT[:, c, h * TOK:(h + 1) * TOK], start=(c == 0), stop=(c == 1))
                else:
                    for t in range(TILES):
                        for c in range(2):
                            at = h * TOK + t * P
                            ins = t_.matmul(b_[:, t * DI:(t + 1) * DI], xnT[:, c, at:at + P], inT[:, c, DI:2 * DI],
                                            start=(c == 0), stop=(c == 1))
                done(ins)

            def weights(name):
                b_ = begin(name)
                if name == "w_out":
                    for o in range(2):
                        ins = t_.transpose(b_[0:DI, o * CK:(o + 1) * CK], opw[:, o, :], ident[0:CK, 0:CK])
                elif name == "w_pbd":
                    pe.wait_ge(S["repl"], 2)
                    ins = t_.matmul(b_[0:CK, 0:HPC * FEAT], prep[:].rearrange("p a b -> p (a b)"),
                                    irep[:].rearrange("p a b -> p (a b)"), start=True, stop=True)
                elif name[:4] == "w_qk":
                    i, rc, c = (int(d) for d in name[4:])
                    taken(pe, "w_pbd")
                    ins = t_.matmul(b_[0:CK + c, 0:HPC * FEAT], qkvw[:, 2 * i + rc, c * CK:(c + 1) * CK + c], pbd[:],
                                    start=True, stop=True)
                elif name in ("w_v", "w_proj"):
                    w, base = (qkvw, 4) if name == "w_v" else (pjw, 0)
                    if name == "w_proj":
                        pe.wait_ge(S["w_proj"], 32)
                    for c in range(2):
                        for o in range(2):
                            ins = t_.transpose(b_[0:CK + c, (2 * c + o) * CK:(2 * c + o + 1) * CK],
                                               w[:, base + o, c * CK:(c + 1) * CK + c], ident[0:CK, 0:CK])
                else:
                    pe.wait_ge(S["w_ffn"], 96)
                    for oc in range(2):
                        for ic in range(2):
                            ins = t_.transpose(b_[0:CK, (2 * oc + ic) * CK:(2 * oc + ic + 1) * CK],
                                               fw[:, int(name[3]), ic, oc * CK:(oc + 1) * CK], ident[0:CK, 0:CK])
                done(ins)

            def pre(n, parts="dBC"):
                h, k = n // DIRS, n % DIRS
                if k == 0:
                    pe.wait_ge(S["xs0"], IMG * (h + 1))
                else:
                    pe.wait_ge(S["xs"], 5 * (h + 1))
                for part in parts:
                    at, m = {"d": (0, DI), "B": (DI, P), "C": (DI + P, P)}[part]
                    b_ = begin(f"{part}{n}")
                    done(t_.matmul(b_[0:m, :], pre_w[:, k, at:at + m], xs[:, h, k, :], start=True, stop=True))

            def spread_out(u):
                n, g12 = u // UNITS, u % UNITS
                j, q = g12 // PER_CHUNK, g12 % PER_CHUNK
                if g12 == 0:
                    pe.wait_ge(S["stack"], 16 * 9 * (n + 1))
                if u >= 2:
                    pe.wait_ge(S["decay"], u - 1)
                t_.matmul(step_bc[u % 2][:, :], spread[:, q, :], stack[:, n % 2, j, 0:TOK], start=True, stop=True
                          ).then_inc(S["bc_step"], 1)
                if u >= 2:
                    pe.wait_ge(S["drive"], u - 1)
                t_.matmul(inp_bc[u % 2][:, :], spread[:, q, :], stack[:, n % 2, j, TOK:2 * TOK], start=True, stop=True
                          ).then_inc(S["bc_inp"], 1)

            def sum_states(u):
                n, g12 = u // UNITS, u % UNITS
                pe.wait_ge(S["outp"], u + 1)
                if g12 == 0 and n > 0:
                    pe.wait_ge(S["y_ev"], n)
                at = DI - GRP - GRP * g12
                t_.matmul(y_acc[0:DI, :], band[:, at:at + DI], outp[:, u % SLOTS, :],
                          start=(g12 == 0), stop=(g12 == UNITS - 1)).then_inc(S["y_mm"], 1)

            def scores(n, j):
                p, _ = of_set(n)
                b_ = begin(f"s{n}{j}")
                r0, ch = 2 * HD * (j % 4), j // 4
                for q in range(2):
                    ins = t_.matmul(b_[:, q * L:(q + 1) * L], fq[p][r0:r0 + HD, ch, q * P:(q + 1) * P], fk[p][r0:r0 + HD, ch, :],
                                    start=True, stop=True)
                done(ins)

            def turn_probs(n, j):
                p, before = of_set(n)
                m = before * TOPK + j
                b_ = begin(f"pt{n}{j}")
                taken(pe, f"s{n}{j}")
                for kt in range(2):
                    for q in range(2):
                        ins = t_.transpose(b_[:, (2 * kt + q) * P:(2 * kt + q + 1) * P], prob[p][:, m % 2, q, kt * P:(kt + 1) * P], idn)
                done(ins)

            def weigh_values(n, j):
                p, before = of_set(n)
                m = before * TOPK + j
                b_ = begin(f"pv{n}{j}")
                taken(pe, f"pt{n}{j}")
                for q in range(2):
                    for kt in range(2):
                        ins = t_.matmul(b_[:, q * HD:(q + 1) * HD], probT[p][:, m % 2, kt, q * P:(q + 1) * P],
                                        fv[p][:, kt, j * HD:(j + 1) * HD], start=(kt == 0), stop=(kt == 1))
                done(ins)

            def turn(b_, src, b):
                for c in range(2):
                    for t in range(2):
                        ins = t_.transpose(b_[0:CK, c * L + t * P:c * L + (t + 1) * P], src[:, 2 * b + t, c * CK:(c + 1) * CK], idn)
                done(ins)

            def side(step, n):
                h, b = n // IMG, n % IMG
                p, _ = of_set(n)
                if step in NO_PRODUCT:
                    return
                if step in WEIGHT_STEPS:
                    weights(step)
                    return
                if step in ("xh", "z"):
                    front(step, n)
                    return
                if step[0] == "h" and step != "hT":
                    j = int(step[1:])
                    if j < TOPK:
                        scores(n, j)
                    if 0 < j <= TOPK:
                        turn_probs(n, j - 1)
                    if j > 1:
                        weigh_values(n, j - 2)
                    return
                b_ = begin(f"{step}_{n}")
                at0 = b * L
                if step == "yT":
                    pe.wait_ge(S["y_sum"], h + 1)
                    for t in range(2):
                        ins = t_.transpose(b_[:, t * DI:(t + 1) * DI], y_sum[:, h, at0 + t * P:at0 + (t + 1) * P], ident[0:DI, 0:DI])
                    done(ins)
                elif step == "gT":
                    pe.wait_ge(S["gate"], n + 1)
                    for t in range(2):
                        ins = t_.transpose(b_[0:DI, t * P:(t + 1) * P], yn[:, 2 * b + t, :], idn)
                    done(ins)
                elif step == "o":
                    taken(pe, f"gT_{n}")
                    for t in range(2):
                        ins = t_.matmul(b_[:, t * CH:(t + 1) * CH], gT[:, at0 + t * P:at0 + (t + 1) * P], outT[:], start=True, stop=True)
                    done(ins)
                elif step == "tT":
                    pe.wait_ge(S["norm_t"], 2 * (n + 1))
                    turn(b_, tn, b)
                elif step[0] == "q":
                    taken(pe, f"tT_{n}")
                    for u in range(2):
                        i = 2 * int(step[1]) + u
                        for c in range(2):
                            ins = t_.matmul(b_[:, u * L:(u + 1) * L], qw[0:CK + c, c, i * P:(i + 1) * P], tT[0:CK + c, c, at0:at0 + L],
                                            start=(c == 0), stop=(c == 1))
                    done(ins)
                elif step[:2] == "kv":
                    at, j, w = at0 + int(step[2]) * P, int(step[3]), HPC * FEAT + CK
                    for c in range(2):
                        ins = t_.matmul(b_[:, 0:w], tT[0:CK + c, c, at:at + P], kvw[0:CK + c, c, j, :], start=(c == 0), stop=(c == 1))
                    done(ins)
                elif step == "cx":
                    for tj in ("00", "01", "10", "11"):
                        taken(pe, f"kv{tj}_{n}")
                    w = 2 * (HD + 1)
                    for i in range(PAIRS):
                        for t in range(2):
                            ins = t_.matmul(b_[:, i * w:(i + 1) * w], kp[:, 2 * b + t, i * P:(i + 1) * P],
                                            v1[:, 2 * b + t, 2 * i:2 * i + 2, :].rearrange("p h d -> p (h d)"),
                                            start=(t == 0), stop=(t == 1))
                    done(ins)
                elif step == "at":
                    taken(pe, f"cx_{n}")
                    w = 2 * (HD + 1)
                    for t in range(2):
                        for i in range(PAIRS):
                            at = (t * PAIRS + i) * w
                            ins = t_.matmul(b_[:, at:at + w], qp[:, i, at0 + t * P:at0 + (t + 1) * P], cbd[:, b, i, :],
                                            start=True, stop=True)
                    done(ins)
                elif step == "aT":
                    taken(pe, f"at_{n}")
                    pe.wait_ge(S["att"], n + 1)
                    turn(b_, ao, b)
                elif step == "p":
                    taken(pe, f"aT_{n}")
                    for t in range(2):
                        for c in range(2):
                            ins = t_.matmul(b_[:, t * CH:(t + 1) * CH], aT[0:CK + c, c, at0 + t * P:at0 + (t + 1) * P],
                                            pjT[0:CK + c, c, :], start=(c == 0), stop=(c == 1))
                    done(ins)
                elif step == "hT":
                    pe.wait_ge(S["norm_u"], 2 * (n + 1))
                    turn(b_, hn, b)
                elif step == "lg":
                    taken(pe, f"hT_{n}")
                    pe.wait_ge(S["w_wo"], 48)
                    for c in range(2):
                        ins = t_.matmul(b_[0:1, 0:HEADS], rin[0:CK + c, c, b:b + 1], wr[0:CK + c, c, :], start=(c == 0), stop=(c == 1))
                    done(ins)
                elif step == "cr":
                    pe.wait_ge(S["val_rows"], n + 1)
                    for u in range(3):
                        for i in range(2):
                            rows = valr[:, b, u * HEADS + i * HPC:u * HEADS + (i + 1) * HPC, :].rearrange("p a b -> p (a b)")
                            ins = t_.matmul(b_[0:CK, 2 * u + i:2 * u + i + 1], rows, ident[0:1, 0:1], start=True, stop=True)
                    done(ins)
                elif step in ("wq", "wk"):
                    pe.wait_ge(S["sel"], 4 * (n + 1))
                    wi = int(step == "wk")
                    for c in range(2):
                        for o in range(2):
                            ins = t_.matmul(b_[0:CK + c, c * CH:(c + 1) * CH], fT[:, wi, o, c * CK:(c + 1) * CK + c],
                                            sel_m[:, b, o, :, :].rearrange("p a b -> p (a b)"), start=(o == 0), stop=(o == 1))
                    done(ins)
                elif step == "wv":
                    for c in range(2):
                        for o in range(2):
                            t_.matmul(b_[0:CK + c, c * CK:(c + 1) * CK], fT[:, 2, o, c * CK:(c + 1) * CK + c],
                                      sel_m[:, b, o, :, 0:HD], start=(o == 0), stop=(o == 1))
                    for o in range(2):
                        ins = t_.matmul(b_[0:CK, CH:2 * CH], sel_u[:, b, o, :, :].rearrange("p a b -> p (a b)"), wo[:, o, :],
                                        start=(o == 0), stop=(o == 1))
                    done(ins)
                elif step in ("fq", "fk"):
                    wi = int(step == "fk")
                    taken(pe, f"w{step[1]}_{n}")
                    for lo_, m, at in ((0, P, 0), (P, 64, L)):
                        for c in range(2):
                            ins = t_.matmul(b_[0:m, at:at + L], wsel[p][0:CK + c, wi, c, lo_:lo_ + m],
                                            hT[0:CK + c, c, at0:at0 + L], start=(c == 0), stop=(c == 1))
                    done(ins)
                elif step == "fv":
                    taken(pe, f"wv_{n}")
                    for t in range(2):
                        for c in range(2):
                            ins = t_.matmul(b_[:, t * CK:(t + 1) * CK], hT[0:CK + c, c, at0 + t * P:at0 + (t + 1) * P],
                                            wsv[p][0:CK + c, c, :], start=(c == 0), stop=(c == 1))
                    done(ins)
                    for w in "qkv":
                        taken(pe, f"f{w}_{n}")
                elif step == "cT":
                    for j in range(TOPK):
                        taken(pe, f"pv{n}{j}")
                    for q in range(2):
                        ins = t_.transpose(b_[0:CK, q * P:(q + 1) * P], cx[p][:, q, :], idn)
                    done(ins)
                elif step == "fo":
                    taken(pe, f"cT_{n}")
                    for q in range(2):
                        ins = t_.matmul(b_[:, q * CH:(q + 1) * CH], cT[p][:, q * P:(q + 1) * P], wos[p][:], start=True, stop=True)
                    done(ins)

            front("xh", 0)
            front("z", 0)
            pre(0)
            pe.wait_ge(S["const2"], CONST2)
            pe.wait_ge(S["ones"], ONES)
            pe.wait_ge(S["xn"], 8)
            for u in range(SLOT_COUNT):
                n, g12 = pre_at(u)
                spread_out(u)
                if u >= Y_LAG:
                    sum_states(u - Y_LAG)
                for item in beside[u]:
                    side(*item)
                if n < SCANS:
                    for part, at in (("d", PRE_STEP_MM), ("B", PRE_B), ("C", PRE_C)):
                        if g12 == at:
                            pre(n, part)
            for u in range(SLOT_COUNT - Y_LAG, SLOT_COUNT):
                sum_states(u)
            pe.wait_ge(S["y_ev"], SCANS)
            for item in rest:
                side(*item)


_INS = ["x"] + ["L0_conv_" + n for n in ("in_proj_w", "conv_w", "conv_b", "x_proj_w", "dt_projs_w", "dt_projs_b", "A_logs",
                                         "Ds", "out_norm_g", "out_norm_b", "out_proj_w")]
_INS += ["L1_attn_" + n for n in ("w_qkv", "b_qkv", "w_proj", "b_proj", "projection")]
_INS += ["L1_ffn_" + n for n in ("Wq", "bq", "Wk", "bk", "Wv", "bv", "Wr", "br", "Wo", "bo", "ln_g", "ln_b")]
_OUTS = [((4, 16, 16, 192), "float32")]


def kernel(**inputs):
    import numpy as _np
    import concourse.bacc as _bacc
    from concourse import mybir as _mybir
    from concourse.bass_utils import run_bass_kernel_spmd as _run

    nc = _bacc.Bacc("TRN2", target_bir_lowering=False, num_devices=1)
    arrays, args = {}, []
    for name in _INS:
        a = _np.ascontiguousarray(inputs[name])
        arrays[f"in_{name}_dram"] = a
        args.append(nc.dram_tensor(f"in_{name}_dram", a.shape, _mybir.dt.from_np(a.dtype), kind="ExternalInput").ap())
    for i, (shape, dtype) in enumerate(_OUTS):
        dt = _mybir.dt.from_np(_np.dtype(dtype))
        args.append(nc.dram_tensor(f"out_{i}_dram", shape, dt, kind="ExternalOutput").ap())
    hybrid_kernel(nc, *args)
    r = _run(nc, [arrays], core_ids=[0])
    got = tuple(r.results[0][f"out_{i}_dram"] for i in range(len(_OUTS)))
    return got[0]
```

```python
from contextlib import ExitStack

import concourse.bass as bass
from concourse import mybir

F32 = mybir.dt.float32
BF16 = mybir.dt.bfloat16
ALU = mybir.AluOpType
ACT = mybir.ActivationFunctionType
AX_X = mybir.AxisListType.X

P = 128
IMAGES, SIDE, CH = 4, 16, 192
L = SIDE * SIDE
HALVES = 2
IMG = IMAGES // HALVES
TOK = IMG * L
TILES = TOK // P
CK = CH // 2
DI, NS, RANK, DIRS = 96, 16, 12, 4
GRP = P // NS
UNITS = DI // GRP
CHUNK = 32
CHUNKS = DI // CHUNK
PER_CHUNK = CHUNK // GRP
XROWS = RANK + 2 * NS
GN_SIZE = CH // 32
HEADS, HD, FEAT, TOPK = 12, 16, 64, 6
HPC = CK // HD
PAIRS = HEADS // 2
KERNEL_EPS = 0.001
RING = 3
SLOTS = 3
STATE_SLOTS = 4
Y_LAG = 3
SOFTPLUS_LINEAR = 40.0
SERIES_BELOW = 0.0025
LAG = 1
PRE_RAW, PRE_CLIP, PRE_EXP, PRE_SERIES, PRE_LN = -4, -3, -2, -1, -1
PRE_MAX, PRE_MAX_SERIES, PRE_INP = 0, 1, 2
PRE_HI, PRE_REST, PRE_MID, PRE_LO = (2, 3), (4, 5), (5, 6), (6, 6)
LOG_MAX = 82.0

CONST2 = 3 + 1 + HPC + TOPK
ONES = 9
BEHIND = (0, 0, 0, 6)
FIRST_STEP = 4
ADD_Y = 3
ACC_ROWS = IMG * (SIDE + 2) - 2
SCANS = HALVES * DIRS
SLOT_COUNT = SCANS * UNITS
FINAL_RING = 8

ATTN_STEPS = (["yT", "yn", "gT", "o", "tn", "tT", "q0", "q1", "q2", "kv00", "kv01", "kv10", "kv11", "cx", "at", "aT",
               "p", "un", "hT", "lg", "cr"])
FFN_STEPS = ["wqk", "wv", "fq", "fk", "fv"] + [f"h{j}" for j in range(TOPK + 3)] + ["fo", "rn"]
WEIGHT_STEPS = (["w_out", "w_pbd"] + [f"w_qk{i}{rc}{c}" for i in range(2) for rc in range(2) for c in range(2)]
                + ["w_v", "w_proj", "w_f0", "w_f1", "w_f2"])
PE_COST = {"q0": 2.4, "q1": 2.4, "q2": 2.4, "kv00": 2.3, "kv01": 2.3, "kv10": 2.3, "kv11": 2.3, "cx": 3, "at": 3.5, "wqk": 2,
           "wv": 2, "fq": 2.4, "fk": 1.6, "fv": 2, "o": 3, "p": 3, "lg": 4, "h0": 3, "h1": 3.5, "h2": 3.5, "h3": 3.5, "h4": 3.5, "h5": 3.5}
PE_COST_ELSE = 1.5
PE_ROOM = 4.0
FRONT_BESIDE = ((1, "xh"), (8, "conv0"), (16, "conv1"), (19, "silu"), (21, "z"))
WEIGHTS_FIRST = 14
UNITS_AFTER = {step: 1 for step in ("q0", "q1", "q2", "kv00", "kv01", "kv10", "wqk", "wv", "fq", "fk")}
UNITS_AFTER_ELSE = 2
NO_PRODUCT = {"yn", "tn", "un", "rn", "conv0", "conv1", "silu"}


def side_work():
    beside = [[] for _ in range(SLOT_COUNT)]
    for at, step in FRONT_BESIDE:
        beside[at].append((step, 1))
    for i, step in enumerate(WEIGHT_STEPS):
        beside[WEIGHTS_FIRST + 2 * i].append((step, 0))
    steps = ATTN_STEPS + FFN_STEPS
    done, ready = [0, 0], [DIRS * UNITS + FIRST_STEP, DIRS * UNITS + FIRST_STEP + 1]
    for u in range(DIRS * UNITS, SLOT_COUNT):
        held = 0.0
        for n in (0, 1):
            if ready[n] > u or done[n] >= (len(steps) if n == 0 else done[0]):
                continue
            step = steps[done[n]]
            if held and held + PE_COST.get(step, PE_COST_ELSE) > PE_ROOM:
                continue
            held += PE_COST.get(step, PE_COST_ELSE)
            beside[u].append((step, n))
            done[n] += 1
            ready[n] = u + UNITS_AFTER.get(step, UNITS_AFTER_ELSE)
    at = {step: i for i, step in enumerate(steps)}
    done += [0, 0]
    rest = []
    while min(done) < len(steps):
        for n in range(IMAGES):
            if done[n] == len(steps) or (n and done[n - 1] < min(len(steps), done[n] + 1 + BEHIND[n])):
                continue
            if n >= IMG and (done[n] == at["tT"] and done[n - IMG] <= at["fv"] or done[n] == at["un"] and done[n - IMG] <= at["fo"]):
                continue
            rest.append((steps[done[n]], n))
            done[n] += 1
    return beside, rest


def products(step, n):
    if step in NO_PRODUCT:
        return []
    if step in WEIGHT_STEPS:
        return [step]
    if step[0] == "h" and step[1:].isdigit():
        j = int(step[1:])
        return [f"pt{n}{j - 2}"] * (1 < j <= TOPK + 1) + [f"pv{n}{j - 3}"] * (j > 2) + [f"s{n}{j}"] * (j < TOPK)
    return [f"{step}_{n}"]


def preparing(u, at):
    n = (u - at) // UNITS + 1
    if u == 0 and at < 0:
        return 1
    return n if (u - at) % UNITS == 0 and 1 <= n < SCANS and (at >= 0 or n > 1) else None


def ring_plan():
    beside, rest = side_work()
    names = ["w_in", "w_xp", "w_dt", "w_fold", "w_alog", "gm", "gv", "xh_0", "z_0", "d0"]
    for u in range(SLOT_COUNT):
        if preparing(u, PRE_RAW):
            names.append(f"d{preparing(u, PRE_RAW)}")
        for item in beside[u]:
            names += products(*item)
    early = len(names)
    for item in rest:
        names += products(*item)
    plan, held = {}, [0] * FINAL_RING
    for i, name in enumerate(names):
        at = i % RING if i < early else (i - early) % FINAL_RING
        plan[name] = (i, at, held[at])
        held[at] += 1
    return plan


def hybrid_kernel(nc, x, in_proj_w, conv_w, conv_b, x_proj_w, dt_w, dt_b, A_logs, Ds, norm_g, norm_b, out_proj_w,
                  w_qkv, b_qkv, w_proj, b_proj, projection, Wq, bq, Wk, bk, Wv, bv, Wr, br, Wo, bo, ln_g, ln_b, out):
    ring = ring_plan()
    x_d = x.rearrange("b h w c -> (b h w) c").rearrange("(t p) c -> p t c", p=P)
    out_d = out.rearrange("b h w c -> (b h w) c").rearrange("(t p) c -> p t c", p=P)

    with ExitStack() as ctx:
        ctx.enter_context(nc.allow_non_contiguous_dma(reason="small parameter vectors"))

        def sb(name, shape, dt=F32):
            return ctx.enter_context(nc.sbuf_tensor(name, shape, dt))

        def shared(name, *tenants):
            def words(shape, dt):
                n = 1
                for d in shape[1:]:
                    n *= d
                return n * (2 if dt == BF16 else 4) // 4
            room = sb(name, [P, max(sum(words(*t) for t in tenant) for tenant in tenants)])
            views = []
            for tenant in tenants:
                at = 0
                for shape, dt in tenant:
                    ap = room[0:shape[0], at:at + words(shape, dt)]
                    at += words(shape, dt)
                    if dt == BF16:
                        ap = ap.bitcast(BF16)
                    dims = "abcde"[:len(shape) - 1]
                    if len(dims) > 1:
                        ap = ap.rearrange(f"p ({' '.join(dims)}) -> p {' '.join(dims)}",
                                          **{d: shape[1 + i] for i, d in enumerate(dims)})
                    views.append(ap)
            return views

        def sem(name):
            return ctx.enter_context(nc.semaphore(name))

        step_bc = [ctx.enter_context(nc.psum_tensor(f"step_bc{i}", [P, TOK], F32)) for i in range(2)]
        inp_bc = [ctx.enter_context(nc.psum_tensor(f"inp_bc{i}", [P, TOK], F32)) for i in range(2)]
        y_acc = ctx.enter_context(nc.psum_tensor("y_acc", [P, TOK], F32))
        banks = [ctx.enter_context(nc.psum_tensor(f"ring{i}", [P, TOK], F32)) for i in range(RING)]
        banks += step_bc + inp_bc + [y_acc]

        def bank(name):
            return banks[ring[name][1]]

        x_tok = sb("x_tok", [P, HALVES * TILES, CH])
        cw = sb("cw", [DI, 9])
        cb = sb("cb", [DI, 2])
        dtb = sb("dtb", [DI, DIRS])
        dsk = sb("dsk", [DI, DIRS])
        gb = sb("gb", [P, 3, CH])
        proj = sb("proj", [FEAT, HD])
        wr = sb("wr", [CK + 1, 2, HEADS])
        wo = sb("wo", [CK, 2, CH])
        ident = sb("ident", [P, P])
        avg6 = sb("avg6", [CK, CK])
        band = sb("band", [P, 2 * DI - GRP])
        spread = sb("spread", [DI, PER_CHUNK, P], BF16)
        dmatch = sb("dmatch", [CK, HD])
        tri = sb("tri", [1, HEADS, HEADS])
        slot_no = sb("slot_no", [CK, TOPK])
        neg_half = sb("neg_half", [P, 8])
        a_log = sb("a_log", [P, DIRS * UNITS])
        a_neg = sb("a_neg", [P, DIRS * UNITS])
        outT = sb("outT", [DI, CH])
        dsum = sb("dsum", [DI, 1])
        qw = sb("qw", [CK + 1, 2, HEADS * FEAT])
        kvw = sb("kvw", [CK + 1, 2, 2, HPC * FEAT + CK])
        pjT = sb("pjT", [CK + 1, 2, CH])
        fT = sb("fT", [CK, 3, 2, CH + 1])
        qkvw, pjw, fw, kp = shared("room_a", [([CK, 6, CH + 1], F32), ([CK, 2, CH + 1], F32), ([CK, 3, 2, CH], F32)],
                                   [([P, TILES, HEADS * FEAT], F32)])
        xnT, irep, prep, pmask, qp = shared(
            "room_b", [([CK, 2, HALVES * TOK], F32), ([FEAT, HPC, FEAT], F32), ([FEAT, HPC, HD], F32), ([CK, HPC, FEAT], F32)],
            [([P, PAIRS, TOK], F32)])
        valr = sb("valr", [1, IMG, 3 * HEADS, HD])
        acc, opw, hn = shared("room_e", [([DI, ACC_ROWS, SIDE], F32), ([CK, 2, DI], F32)], [([P, TILES, CH], F32)])
        inT, dtT, yn, gt, eq = shared("room_f", [([CK, 2, CH], F32), ([RANK, DIRS, DI], F32)],
                                      [([P, TILES, DI], F32), ([1, HEADS, HEADS], F32), ([1, HEADS, HEADS], F32)])
        inw, xpw, dtw, alog, ze, tn = shared("room_h", [([DI, 2, CH], F32), ([XROWS, DIRS, DI], F32), ([DI, DIRS, RANK], F32),
                                                        ([DIRS * UNITS, P], F32)], [([P, TILES, DI], F32)],
                                             [([P, TILES, CH], F32)])
        sg, gT = shared("room_i", [([DI, TOK], F32)], [([DI, TOK], F32)])
        prob, probT = ([sb(f"{name}{i}", [P, 2, 2, L]) for i in range(IMG)] for name in ("prob", "probT"))
        fq = [sb("fq0", [CK, 2, L])]
        fk = [sb(f"fk{i}", [CK, L]) for i in range(IMG)]
        fv = [sb(f"fv{i}", [P, 2, TOPK, 2 * HD]) for i in range(IMG)]
        wsv = [sb(f"wsv{i}", [CK + 1, 2, CK]) for i in range(IMG)]
        wos = [sb(f"wos{i}", [CK + 1, CH]) for i in range(IMG)]
        xpad, wsel1 = shared("room_w", [([DI, IMG, SIDE + 2, SIDE + 2], F32)], [([CK + 1, 2, 3, CK], F32)])
        wsel = [sb("wsel0", [CK + 1, 2, 3, CK]), wsel1]
        pbd, cT0 = shared("room_j", [([CK, HPC * FEAT], F32)], [([CK + 1, L], F32)])
        cT = [cT0, sb("cT1", [CK + 1, L])]
        stack = sb("stack", [DI, 2, CHUNKS, 2 * TOK], BF16)
        b_rep = sb("b_rep", [P, 2, TOK])
        c_rep = sb("c_rep", [P, 2, TOK])
        pre_w = sb("pre_w", [DI, DIRS, DI + 2 * NS])
        bc = sb("bc", [P, TOK])
        spl = sb("spl", [DI, TOK])
        spe = sb("spe", [DI, TOK])
        sps = sb("sps", [DI, TOK])
        step2 = sb("step2", [DI, 2, TOK])
        hi = sb("hi", [DI, 2, TOK], BF16)
        mid = sb("mid", [DI, 2, TOK], BF16)
        lo = sb("lo", [DI, 2, TOK], BF16)
        sel_m = sb("sel_m", [CK, IMG, 2, TOPK, HD])
        sel_u = sb("sel_u", [CK, IMG, 2, TOPK, HD])
        (xs_room,) = shared("room_g", [([P, HALVES, DIRS, TOK], F32)])
        xs = xs_room[0:DI]
        later = xs_room[:, 0, 1:DIRS, :].rearrange("p k t -> p (k t)")
        fq.append(xs_room[0:CK, 0, 0, :].rearrange("p (c l) -> p c l", c=2))
        n = TILES * CH
        ao = later[:, 0:n].rearrange("p (t c) -> p t c", t=TILES)
        res = later[:, n:2 * n].rearrange("p (t c) -> p t c", t=TILES)
        conv_out = [acc[:, b * (SIDE + 2):b * (SIDE + 2) + SIDE, :].rearrange("p y x -> p (y x)") for b in range(IMG)]
        gst = sb("gst", [CK, 2 * IMAGES, 6])
        gmv = sb("gmv", [CK, 2 * IMAGES, 2])
        gdv = sb("gdv", [CK, 2 * IMAGES])
        gmean = sb("gmean", [CK, 2 * IMAGES])
        gva = sb("gva", [CK, 2 * IMAGES])
        gve = sb("gve", [CK, 2 * IMAGES])
        gsq = sb("gsq", [CK, 2 * IMAGES])
        grs = sb("grs", [CK, 2 * IMAGES])
        gbi = sb("gbi", [CK, 2 * IMAGES])
        z = sb("z", [P, HALVES, TILES, DI])
        decay = sb("decay", [P, SLOTS, IMG, L])
        state = drive = sb("state", [P, STATE_SLOTS, TOK])
        outp = sb("outp", [P, SLOTS, TOK])
        y_sum = sb("y_sum", [DI, TOK])
        mst = sb("mst", [P, 4, TILES, 6])
        mv = sb("mv", [P, 4, TILES, 2])
        rs = sb("rs", [P, 4, TILES])
        tT = sb("tT", [CK + 1, 2, TOK])
        aT = hT = tT
        v1 = sb("v1", [P, TILES, HEADS, HD + 1])
        cbd = sb("cbd", [P, IMG, PAIRS, 2 * (HD + 1)])
        arec = sb("arec", [P, TILES, HEADS])
        rin = sb("rin", [CK + 1, 2, IMG])
        lg = sb("lg", [1, IMG, HEADS])
        rank = sb("rank", [1, IMG, HEADS])
        val = sb("val", [1, IMG, 3, HEADS])
        msum = sb("msum", [1, IMG, HEADS])
        col = sb("col", [CK, 3, 2, IMG])
        hot = sb("hot", [CK, 2, 2, IMG, TOPK])
        nmax = [sb(f"nmax{i}", [P, 2, 2]) for i in range(2)]
        nmaxs = [sb(f"nmaxs{i}", [P, 2, 2]) for i in range(2)]
        psum_row = [sb(f"psum_row{i}", [P, 2, 2]) for i in range(2)]
        prec = [sb(f"prec{i}", [P, 2, 2]) for i in range(2)]

        gn_banks = [step_bc[0], step_bc[1], inp_bc[0], inp_bc[1]]
        S = {n: sem("s_" + n) for n in (
            "w_in w_xp w_alog w_small w_gb w_qkv w_proj w_ffn w_wo w_bo zeroed const const2 ones ident filled repl small neg_a "
            "gn_turned gn_stats gn_dev gn_var gn_eps gn_rsqrt gn_bias xn padded z_kept gate_e gate_s conv conv_e xs0 xs "
            "a_exp raw b_there c_there sp_t sp_s sp_l sp_max sp_in sp_exp sp_ln step hi rest mid lo stack bc_step bc_inp decay drive state outp y_mm y_ev y_part "
            "stat_y agg_y eps_y rsqrt_y norm_y gate stat_t agg_t eps_t rsqrt_t norm_t ctx_lo a_rec att "
            "stat_u agg_u eps_u rsqrt_u norm_u router_in logit_eq rank slot_of vals val_rows hot sel "
            "stat_r agg_r eps_r rsqrt_r norm_r wsel_zero fin"
        ).split()}
        S["outd"] = [sem(f"s_outd{b}") for b in range(IMG)]
        S["x"] = [sem(f"s_x{h}") for h in range(HALVES)]
        for n in ("key", "prob_max", "prob_bias", "prob", "prob_rec", "prob_divided"):
            S[n] = [sem(f"s_{n}{i}") for i in range(2)]
        free = [sem(f"s_free{i}") for i in range(FINAL_RING)]
        beside, rest = side_work()

        def fetched(eng, name):
            eng.wait_ge(S["filled"], ring[name][0] + 1)

        def reuse(eng, name):
            _, at, held = ring[name]
            if held:
                eng.wait_ge(free[at], held)

        def taken(eng, name):
            eng.wait_ge(freed(name), ring[name][2] + 1)

        def freed(name):
            return free[ring[name][1]]

        def key_count(n, step):
            return 4 * (n // IMG) + 2 * int(step[2]) + int(step[3]) + 1

        block = ctx.enter_context(nc.Block())

        @block.sync
        def _(sp):
            for h in range(HALVES):
                sp.dma_start(x_tok[:, h * TILES:(h + 1) * TILES, :], x_d[:, h * TILES:(h + 1) * TILES, :]).then_inc(S["x"][h], 16)
            sp.dma_start(inw[:], in_proj_w.rearrange("(o p) c -> p o c", p=DI)).then_inc(S["w_in"], 16)
            sp.dma_start(xpw[:], x_proj_w.rearrange("k r c -> r k c")).then_inc(S["w_xp"], 16)
            sp.dma_start(dtw[:], dt_w.rearrange("k c r -> c k r")).then_inc(S["w_xp"], 16)
            sp.dma_start(alog[:], A_logs.rearrange("(g c) n -> g (c n)", c=GRP)).then_inc(S["w_alog"], 16)
            sp.dma_start(cw[:], conv_w.rearrange("c a y x -> c (a y x)")).then_inc(S["w_small"], 16)
            sp.dma_start(cb[:, 0:1], conv_b.rearrange("(c a) -> c a", a=1)).then_inc(S["w_small"], 16)
            sp.dma_start(dtb[:], dt_b.rearrange("k c -> c k")).then_inc(S["w_small"], 16)
            sp.dma_start(dsk[:], Ds.rearrange("(k c) -> c k", c=DI)).then_inc(S["w_small"], 16)
            sp.dma_start(opw[:], out_proj_w.rearrange("(o p) c -> p o c", p=CK)).then_inc(S["w_in"], 16)
            for i, v in enumerate((norm_g, norm_b)):
                sp.dma_start(gb[:, 0, i * DI:(i + 1) * DI], v.rearrange("(a c) -> a c", a=1).to_broadcast([P, DI])).then_inc(S["w_gb"], 16)
            for i, v in enumerate((ln_g, ln_b)):
                sp.dma_start(gb[:, 1 + i, :], v.rearrange("(a c) -> a c", a=1).to_broadcast([P, CH])).then_inc(S["w_gb"], 16)
            sp.dma_start(qkvw[:, :, 0:CH], w_qkv.rearrange("(o p) c -> p o c", p=CK)).then_inc(S["w_qkv"], 16)
            sp.dma_start(qkvw[:, :, CH], b_qkv.rearrange("(o p) -> p o", p=CK)).then_inc(S["w_qkv"], 16)
            sp.dma_start(proj[:], projection).then_inc(S["w_qkv"], 16)
            sp.dma_start(pjw[:, :, 0:CH], w_proj.rearrange("(o p) c -> p o c", p=CK)).then_inc(S["w_proj"], 16)
            sp.dma_start(pjw[:, :, CH], b_proj.rearrange("(o p) -> p o", p=CK)).then_inc(S["w_proj"], 16)
            for i, (w, b) in enumerate(((Wq, bq), (Wk, bk), (Wv, bv))):
                sp.dma_start(fw[:, i, :, :], w.rearrange("(o p) c -> p o c", p=CK)).then_inc(S["w_ffn"], 16)
                sp.dma_start(fT[:, i, :, CH], b.rearrange("(o p) -> p o", p=CK)).then_inc(S["w_ffn"], 16)
            sp.dma_start(wr[0:CK, :, :], Wr.rearrange("(o p) c -> p o c", p=CK)).then_inc(S["w_wo"], 16)
            sp.dma_start(wr[CK:CK + 1, 1, :], br.rearrange("(a c) -> a c", a=1)).then_inc(S["w_wo"], 16)
            sp.dma_start(wo[:], Wo.rearrange("(o p) c -> p o c", p=CK)).then_inc(S["w_wo"], 16)
            for i in range(IMG):
                sp.dma_start(wos[i][CK:CK + 1, :], bo.rearrange("(a c) -> a c", a=1)).then_inc(S["w_bo"], 16)

            def repeat(n, at, dst, gone, there):
                if n >= 2:
                    sp.wait_ge(S[gone], UNITS * (n - 1))
                for c in range(GRP):
                    sp.dma_start(dst[c * NS:(c + 1) * NS, n % 2, :], bc[at:at + NS, :]).then_inc(S[there], 16)

            for n in range(SCANS):
                taken(sp, f"d{n}")
                repeat(n, DI, b_rep, "drive", "b_there")
                if n > 0:
                    repeat(n, DI + NS, c_rep, "outp", "c_there")
                if n >= 2:
                    sp.wait_ge(S["bc_inp"], UNITS * (n - 1))
                for part, (src, s) in enumerate(((hi, "hi"), (mid, "mid"), (lo, "lo"))):
                    sp.wait_ge(S[s], 2 * (n + 1))
                    for j in range(CHUNKS):
                        sp.dma_start(stack[CHUNK * part:CHUNK * (part + 1), n % 2, j, :],
                                     src[CHUNK * j:CHUNK * (j + 1), :, :]).then_inc(S["stack"], 16)
                if n == 0:
                    repeat(n, DI + NS, c_rep, "outp", "c_there")
            for n in range(IMAGES):
                h, b = n // IMG, n % IMG
                sp.wait_ge(S["fin"], n + 1)
                sp.dma_start(out_d[:, 2 * n:2 * n + 2, :], res[:, 2 * b:2 * b + 2, :]).then_inc(S["outd"][b], 16)
            for b in range(IMG):
                sp.wait_ge(S["outd"][b], 16 * HALVES)

        @block.gpsimd
        def _(pool):
            g = nc.gpsimd
            g.memset(ident[:], 0.0).then_inc(S["zeroed"], 1)
            g.memset(avg6[:], 1.0 / GN_SIZE).then_inc(S["zeroed"], 1)
            g.memset(pmask[:], 1.0).then_inc(S["zeroed"], 1)
            g.memset(band[:], 1.0).then_inc(S["zeroed"], 1)
            g.memset(spread[:], 0.0).then_inc(S["zeroed"], 1)
            g.memset(dmatch[:], 0.0).then_inc(S["zeroed"], 1)
            g.memset(tri[:], 1.0).then_inc(S["zeroed"], 1)
            pool.wait_ge(S["zeroed"], 7)
            g.affine_select(out=ident[:], in_=ident[:], pattern=[[-1, P]], compare_op=ALU.not_equal, fill=1.0,
                            base=0, channel_multiplier=1).then_inc(S["ident"], 1)
            avg = avg6[:].rearrange("p (g e) -> p g e", e=GN_SIZE)
            groups = CK // GN_SIZE
            at = NS * (DI - GRP)
            g.affine_select(out=avg, in_=avg, pattern=[[-GN_SIZE, groups], [0, GN_SIZE]], compare_op=ALU.is_ge,
                            fill=0.0, base=0, channel_multiplier=1).then_inc(S["const"], 1)
            g.affine_select(out=pmask[:], in_=pmask[:], pattern=[[-HD, HPC], [0, FEAT]], compare_op=ALU.is_ge,
                            fill=0.0, base=0, channel_multiplier=1).then_inc(S["const"], 1)
            g.affine_select(out=band[:], in_=band[:], pattern=[[-NS, 2 * DI - GRP]], compare_op=ALU.is_ge,
                            fill=0.0, base=at, channel_multiplier=1).then_inc(S["const"], 1)
            pool.wait_ge(S["const"], 3)
            g.affine_select(out=avg, in_=avg, pattern=[[GN_SIZE, groups], [0, GN_SIZE]], compare_op=ALU.is_ge,
                            fill=0.0, base=GN_SIZE - 1, channel_multiplier=-1).then_inc(S["const"], 1)
            g.affine_select(out=pmask[:], in_=pmask[:], pattern=[[HD, HPC], [0, FEAT]], compare_op=ALU.is_ge,
                            fill=0.0, base=HD - 1, channel_multiplier=-1).then_inc(S["const"], 1)
            g.affine_select(out=band[:], in_=band[:], pattern=[[NS, 2 * DI - GRP]], compare_op=ALU.is_ge,
                            fill=0.0, base=NS - 1 - at, channel_multiplier=-1).then_inc(S["const"], 1)
            g.memset(neg_half[:], -0.5).then_inc(S["const"], 1)
            g.memset(xpad[:], 0.0).then_inc(S["const"], 1)

            def inv_sqrt(dst, src, ready, count, done):
                pool.wait_ge(S[ready], count)
                g.tensor_tensor(dst, src, neg_half[0:dst.shape[0], 0:dst.shape[1]], ALU.pow).then_inc(S[done], 1)

            pool.wait_ge(S["const"], 8)
            inv_sqrt(grs[:], gve[:], "gn_eps", 1, "gn_rsqrt")
            sel_s = spread[:].rearrange("p q (c n) -> p q c n", n=NS)
            for part in range(3):
                g.affine_select(out=sel_s, in_=sel_s, pattern=[[-GRP, PER_CHUNK], [-1, GRP], [0, NS]],
                                compare_op=ALU.not_equal, fill=1.0, base=-CHUNK * part,
                                channel_multiplier=1).then_inc(S["const2"], 1)
                pool.wait_ge(S["const2"], part + 1)
            g.affine_select(out=tri[:], in_=tri[:], pattern=[[1, HEADS], [-1, HEADS]], compare_op=ALU.is_gt,
                            fill=0.0, base=0, channel_multiplier=0).then_inc(S["const2"], 1)
            for i in range(HPC):
                g.affine_select(out=dmatch[:], in_=dmatch[:], pattern=[[-1, HD]], compare_op=ALU.not_equal,
                                fill=1.0, base=-HD * i, channel_multiplier=1).then_inc(S["const2"], 1)
                pool.wait_ge(S["const2"], 5 + i)
            for j in range(TOPK):
                g.memset(slot_no[:, j:j + 1], float(j)).then_inc(S["const2"], 1)

            def orders(h):
                pool.wait_ge(S["xs0"], IMG * (h + 1))
                grid = xs[:, h, 0, :].rearrange("p (b y x) -> p b x y", b=IMG, x=SIDE)
                rows = xs[:, h, 0, :].rearrange("p (b l) -> p b l", b=IMG)
                for b in range(IMG):
                    g.tensor_copy(xs[:, h, 1, b * L:(b + 1) * L].rearrange("p (x y) -> p x y", x=SIDE),
                                  grid[:, b, :, :]).then_inc(S["xs"], 1)
                g.tensor_copy(xs[:, h, 2, :].rearrange("p (b l) -> p b l", b=IMG), rows[:, :, ::-1]).then_inc(S["xs"], 1)
                for b in range(IMG):
                    g.tensor_copy(xs[:, h, 3, b * L:(b + 1) * L].rearrange("p (x y) -> p x y", x=SIDE),
                                  grid[:, b, ::-1, ::-1]).then_inc(S["xs"], 1)

            def series(n):
                pool.wait_ge(S["sp_exp"], n + 1)
                if n > 0:
                    pool.wait_ge(S["sp_max"], n)
                g.tensor_scalar(sps[:], spe[:], -0.5, 1.0, ALU.mult, ALU.add).then_inc(S["sp_t"], 1)
                pool.wait_ge(S["sp_t"], n + 1)
                g.tensor_tensor(sps[:], sps[:], spe[:], ALU.mult).then_inc(S["sp_s"], 1)

            def left_of_mid(n, i):
                pool.wait_ge(S["mid"], 2 * n + i + 1)
                g.tensor_tensor(lo[:, i, :], step2[:, i, :], mid[:, i, :], ALU.subtract).then_inc(S["lo"], 1)

            def weigh(u):
                n, g12 = u // UNITS, u % UNITS
                if g12 == 0:
                    pool.wait_ge(S["c_there"], 16 * GRP * (n + 1))
                pool.wait_ge(S["state"], u + 1)
                if u >= SLOTS:
                    pool.wait_ge(S["y_mm"], u - SLOTS + 1)
                g.tensor_tensor(outp[:, u % SLOTS, :], state[:, u % STATE_SLOTS, :], c_rep[:, n % 2, :],
                                ALU.mult).then_inc(S["outp"], 1)

            def side(step, n):
                h, b = n // IMG, n % IMG
                ts = slice(2 * b, 2 * b + 2)
                if step == "silu":
                    orders(n)
                for at, (tag, where) in enumerate((("y", "yT"), ("t", "o"), ("u", "p"), ("r", "fo"))):
                    if step == where:
                        inv_sqrt(rs[:, at, ts], mv[:, at, ts, 1], "eps_" + tag, n + 1, "rsqrt_" + tag)
                if step == "yn":
                    pool.wait_ge(S["norm_y"], 3 * (n + 1))
                    g.tensor_tensor(yn[:, ts, :], yn[:, ts, :], z[:, h, ts, :], ALU.mult).then_inc(S["gate"], 1)
                if step == "rn":
                    pool.wait_ge(S["norm_r"], 4 * (n + 1))
                    g.tensor_tensor(res[:, ts, :], res[:, ts, :], x_tok[:, 2 * n:2 * n + 2, :], ALU.add).then_inc(S["fin"], 1)

            series(0)
            left_of_mid(0, 0)
            left_of_mid(0, 1)
            orders(0)
            for u in range(SLOT_COUNT):
                if u > 0:
                    weigh(u - 1)
                if preparing(u, PRE_SERIES):
                    series(preparing(u, PRE_SERIES))
                for i in range(2):
                    if preparing(u, PRE_LO[i]):
                        left_of_mid(preparing(u, PRE_LO[i]), i)
                for item in beside[u - LAG] if u >= LAG else []:
                    side(*item)
            weigh(SLOT_COUNT - 1)
            for item in beside[SLOT_COUNT - LAG]:
                side(*item)
            for item in rest:
                side(*item)

        @block.scalar
        def _(act):
            a = nc.scalar

            def evac(name, *copies):
                fetched(act, name)
                for dst, src in copies:
                    ins = a.copy(dst, src)
                ins.then_inc(freed(name), 1)

            a.preload_act_table_set("natural_log_exp_and_others")
            evac("w_in", (inT[:].rearrange("p a b -> p (a b)"), bank("w_in")[0:CK, 0:2 * CH]))
            src = bank("w_xp")[0:DI, 0:DIRS * XROWS].rearrange("p (k r) -> p k r", k=DIRS)
            evac("w_xp", (pre_w[:, :, DI:], src[:, :, RANK:]))
            evac("w_dt", (dtT[:].rearrange("p a b -> p (a b)"), bank("w_dt")[0:RANK, 0:DIRS * DI]))
            evac("w_fold", (pre_w[:, :, 0:DI], bank("w_fold")[0:DI, 0:DIRS * DI].rearrange("p (k c) -> p k c", k=DIRS)))
            taken(act, "w_alog")
            a.activation(a_neg[:], a_log[:], ACT.Exp).then_inc(S["a_exp"], 1)
            act.wait_ge(S["gn_bias"], 1)

            def group_normed(h):
                for c in range(2):
                    for b in range(IMG):
                        s = c * IMAGES + h * IMG + b
                        a.activation(xnT[:, c, h * TOK + b * L:h * TOK + (b + 1) * L],
                                     gn_banks[2 * h + c][0:CK, b * L:(b + 1) * L],
                                     ACT.Identity, bias=gbi[:, s:s + 1], scale=grs[:, s:s + 1]).then_inc(S["xn"], 1)

            def front(step, h):
                if step == "xh":
                    if h:
                        act.wait_ge(S["conv"], 9 * h)
                    evac(f"xh_{h}", *[(xpad[:, b, 1:SIDE + 1, 1:SIDE + 1],
                                       bank(f"xh_{h}")[0:DI, b * L:(b + 1) * L].rearrange("p (y x) -> p y x", y=SIDE))
                                      for b in range(IMG)])
                if step == "z":
                    src = bank(f"z_{h}")[:, 0:TILES * DI].rearrange("p (t c) -> p t c", t=TILES)
                    fetched(act, f"z_{h}")
                    a.copy(z[:, h, :, :], src).then_inc(S["z_kept"], 1)
                    if h:
                        act.wait_ge(S["gate_s"], h)
                    a.activation(ze[:], src, ACT.Exp, scale=-1.0).then_inc(freed(f"z_{h}"), 1)
                    taken(act, f"z_{h}")
                    a.activation(ze[:], ze[:], ACT.Ln, bias=1.0).then_inc(S["gate_e"], 1)
                    act.wait_ge(S["gate_e"], 2 * h + 1)
                    a.activation(ze[:], ze[:], ACT.Exp, scale=-1.0).then_inc(S["gate_e"], 1)
                if step == "silu":
                    act.wait_ge(S["conv"], 9 * (h + 1))
                    if h:
                        act.wait_ge(S["xs0"], IMG * h)
                    for b in range(IMG):
                        a.activation(sg[:, b * L:(b + 1) * L], conv_out[b], ACT.Exp, scale=-1.0).then_inc(S["conv_e"], 1)
                    act.wait_ge(S["conv_e"], 4 * h + 2)
                    a.activation(sg[:], sg[:], ACT.Ln, bias=1.0).then_inc(S["conv_e"], 1)
                    act.wait_ge(S["conv_e"], 4 * h + 3)
                    a.activation(sg[:], sg[:], ACT.Exp, scale=-1.0).then_inc(S["conv_e"], 1)

            group_normed(0)
            act.wait_ge(S["const"], 8)
            front("xh", 0)
            front("silu", 0)
            group_normed(1)

            def weights(step):
                if step == "w_out":
                    evac("w_out", (outT[:], bank("w_out")[0:DI, 0:CH]))
                elif step[:4] == "w_qk":
                    i, rc, c = (int(d) for d in step[4:])
                    rows, n = CK + c, HPC * FEAT
                    dst = qw[0:rows, c, rc * n:(rc + 1) * n] if i == 0 else kvw[0:rows, c, rc, 0:n]
                    evac(step, (dst, bank(step)[0:rows, 0:n]))
                elif step in ("w_v", "w_proj"):
                    srcs = bank(step)[:, 0:2 * CH].rearrange("p (c o k) -> p c o k", c=2, o=2)
                    dsts = [kvw[0:CK + c, c, :, HPC * FEAT:] if step == "w_v" else
                            pjT[0:CK + c, c, :].rearrange("p (o k) -> p o k", o=2) for c in range(2)]
                    evac(step, *[(dsts[c], srcs[0:CK + c, c, :, :]) for c in range(2)])
                elif step[:3] == "w_f":
                    evac(step, (fT[:, int(step[3]), :, 0:CH], bank(step)[0:CK, 0:2 * CH].rearrange("p (o k) -> p o k", o=2)))

            def pre_raw(n):
                fetched(act, f"d{n}")
                if n > 0:
                    act.wait_ge(S["lo"], 2 * n)
                a.activation(step2[:, 0, :], bank(f"d{n}")[0:DI, :], ACT.Identity,
                             bias=dtb[:, n % DIRS:n % DIRS + 1]).then_inc(S["raw"], 1)
                if n > 0:
                    act.wait_ge(S["b_there"], 16 * GRP * n)
                    act.wait_ge(S["c_there"], 16 * GRP * n)
                a.copy(bc[DI:, :], bank(f"d{n}")[DI:, :]).then_inc(freed(f"d{n}"), 1)

            def pre_softplus(n):
                act.wait_ge(S["sp_in"], n + 1)
                if n > 0:
                    act.wait_ge(S["sp_s"], n)
                a.activation(spe[:], spl[:], ACT.Exp).then_inc(S["sp_exp"], 1)
                act.wait_ge(S["sp_exp"], n + 1)
                a.activation(spl[:], spe[:], ACT.Ln, bias=1.0).then_inc(S["sp_ln"], 1)

            def pre_hi(n, i):
                act.wait_ge(S["step"] if i else S["sp_max"], n + 1)
                if n > 0:
                    act.wait_ge(S["stack"], 16 * 9 * n)
                a.copy(hi[:, i, :], step2[:, i, :]).then_inc(S["hi"], 1)

            def pre_mid(n, i):
                act.wait_ge(S["rest"], 2 * n + i + 1)
                a.copy(mid[:, i, :], step2[:, i, :]).then_inc(S["mid"], 1)

            def expo(u):
                act.wait_ge(S["bc_step"], u + 1)
                if u >= SLOTS:
                    act.wait_ge(S["state"], u - SLOTS + 1)
                at = u % (DIRS * UNITS)
                a.activation(decay[:, u % SLOTS, :, 1:L],
                             step_bc[u % 2][:, :].rearrange("p (b l) -> p b l", b=IMG)[:, :, 1:L],
                             ACT.Exp, scale=a_neg[:, at:at + 1]).then_inc(S["decay"], 1)

            def turned_probs(n, j):
                p, m = n % IMG, n // IMG * TOPK + j
                if m >= 2:
                    fetched(act, f"pv{n - IMG * (j < 2)}{(j - 2) % TOPK}")
                name = f"pt{n}{j}"
                evac(name, (probT[p][:, m % 2, :, :].rearrange("p a b -> p (a b)"), bank(name)[:, :]))

            def exp_scores(n, j):
                p, m = n % IMG, n // IMG * TOPK + j
                name = f"s{n}{j}"
                act.wait_ge(S["prob_bias"][p], m + 1)
                if m >= 2:
                    fetched(act, f"pt{n - IMG * (j < 2)}{(j - 2) % TOPK}")
                    act.wait_ge(S["prob_divided"][p], 2 * (m - 1))
                for q in range(2):
                    a.activation(prob[p][:, m % 2, q, :], bank(name)[:, q * L:(q + 1) * L], ACT.Exp,
                                 bias=nmaxs[p][:, m % 2, q:q + 1], scale=HD ** -0.5,
                                 accum_out=psum_row[p][:, m % 2, q:q + 1]).then_inc(S["prob"][p] if q == 0 else freed(name), 1)

            def side(step, n):
                h, b = n // IMG, n % IMG
                name = f"{step}_{n}"
                img = slice(b * L, (b + 1) * L)
                p = b
                if step in WEIGHT_STEPS:
                    weights(step)
                elif step in ("xh", "z", "silu"):
                    front(step, n)
                elif step == "gT":
                    evac(name, (gT[:, img], bank(name)[0:DI, 0:L]))
                elif step in ("tT", "aT"):
                    if step == "tT" and n >= IMG:
                        fetched(act, f"fv_{n - IMG}")
                    evac(name, (tT[0:CK, :, img], bank(name)[0:CK, :].rearrange("p (c l) -> p c l", c=2)))
                elif step == "hT":
                    fetched(act, name)
                    for c in range(2):
                        a.activation(hT[0:CK, c, img], bank(name)[0:CK, c * L:(c + 1) * L], ACT.Copy,
                                     accum_out=rin[0:CK, c, b:b + 1]).then_inc(S["router_in"] if c == 0 else freed(name), 1)
                elif step[:2] == "kv":
                    t, j = 2 * b + int(step[2]), int(step[3])
                    fetched(act, name)
                    act.wait_ge(S["key"][b], key_count(n, step))
                    a.copy(v1[:, t, j * HPC:(j + 1) * HPC, 0:HD],
                           bank(name)[:, HPC * FEAT:HPC * FEAT + CK].rearrange("p (h d) -> p h d", d=HD)).then_inc(freed(name), 1)
                elif step == "cx":
                    fetched(act, name)
                    src = bank(name)[:, 0:PAIRS * 2 * (HD + 1)].rearrange("p (i d) -> p i d", i=PAIRS)
                    a.copy(cbd[0:FEAT, b, :, 0:HD + 1], src[0:FEAT, :, 0:HD + 1]).then_inc(S["ctx_lo"], 1)
                    a.copy(cbd[FEAT:P, b, :, HD + 1:], src[FEAT:P, :, HD + 1:]).then_inc(freed(name), 1)
                elif step == "wqk":
                    if h:
                        fetched(act, f"fo_{n - IMG}")
                    act.wait_ge(S["wsel_zero"], IMG)
                    src = bank(name)[:, 0:4 * CK].rearrange("p (i c k) -> p i c k", i=2, c=2)
                    heads = lambda ap, e: ap.rearrange("p (j e d) -> p j e d", e=2, d=HD)[:, :, e, :]
                    evac(name, *[(heads(wsel[p][0:CK + c, c, e, :], e), heads(src[0:CK + c, 0, c, :], e))
                                 for c in range(2) for e in range(2)],
                         *[(wsel[p][0:CK + c, c, 2, :], src[0:CK + c, 1, c, :]) for c in range(2)])
                elif step == "wv":
                    src = bank(name)
                    if n == 0:
                        act.wait_ge(S["w_bo"], 16 * IMG)
                    evac(name, (wsv[p][0:CK, 0, :], src[0:CK, 0:CK]), (wsv[p][0:CK + 1, 1, :], src[0:CK + 1, CK:2 * CK]),
                         (wos[p][0:CK, :], src[0:CK, CH:2 * CH]))
                elif step in ("fq", "fk"):
                    if step == "fq":
                        evac(name, (fq[p][:].rearrange("p e l -> p (e l)") if b == 0 else fq[p].rearrange("p e l -> p (e l)"),
                                    bank(name)[0:CK, :]))
                    else:
                        evac(name, (fk[p][:], bank(name)[0:CK, 0:L]))
                elif step == "fv":
                    act.wait_ge(S["ones"], ONES)
                    src = bank(name)[:, 0:2 * CK].rearrange("p (t i e d) -> p t i e d", t=2, e=2, d=HD)
                    dst = fv[p][:].rearrange("p t (i e) c -> p t i e c", e=2)
                    evac(name, *[(dst[:, t, :, e, e * HD:(e + 1) * HD], src[:, t, :, e, :]) for t in range(2) for e in range(2)])
                elif step[0] == "h":
                    j = int(step[1:])
                    if 1 < j <= TOPK + 1:
                        turned_probs(n, j - 2)
                    if j < TOPK:
                        exp_scores(n, j)

            pre_raw(0)
            pre_softplus(0)
            front("z", 0)
            for i in range(2):
                pre_hi(0, i)
            for i in range(2):
                pre_mid(0, i)
            act.wait_ge(S["neg_a"], 1)
            act.wait_ge(S["ones"], ONES)
            for u in range(SLOT_COUNT):
                expo(u)
                if preparing(u, PRE_RAW + LAG):
                    pre_raw(preparing(u, PRE_RAW + LAG))
                if preparing(u, PRE_EXP):
                    pre_softplus(preparing(u, PRE_EXP))
                for i in range(2):
                    if preparing(u, PRE_HI[i]):
                        pre_hi(preparing(u, PRE_HI[i]), i)
                    if preparing(u, PRE_MID[i]):
                        pre_mid(preparing(u, PRE_MID[i]), i)
                for item in beside[u - LAG] if u >= LAG else []:
                    side(*item)
            for item in beside[SLOT_COUNT - LAG]:
                side(*item)
            for item in rest:
                side(*item)

        @block.vector
        def _(dve):
            v = nc.vector

            v.memset(decay[:], 0.0).then_inc(S["ones"], 1)
            v.memset(tT[CK:CK + 1, :, :], 1.0).then_inc(S["ones"], 1)
            for i in range(IMG):
                v.memset(fv[i][:], 0.0).then_inc(S["ones"], 1)
                v.memset(cT[i][CK:CK + 1, :], 1.0).then_inc(S["ones"], 1)
            v.memset(v1[:, :, :, HD:HD + 1], 1.0).then_inc(S["ones"], 1)
            v.memset(cbd[:], 0.0).then_inc(S["ones"], 1)
            v.memset(rin[CK:CK + 1, :, :], float(L)).then_inc(S["ones"], 1)

            for i in range(4):
                h, c = i // 2, i % 2
                dve.wait_ge(S["gn_turned"], i + 1)
                for b in range(IMG):
                    v.bn_stats(gst[:, c * IMAGES + h * IMG + b, :], gn_banks[i][0:CK, b * L:(b + 1) * L]).then_inc(S["gn_stats"], 1)
            dve.wait_ge(S["gn_stats"], 8)
            for s in range(8):
                v.bn_aggr(gmv[:, s, :], gst[:, s, :]).then_inc(S["gn_stats"], 1)
            fetched(dve, "w_alog")
            v.tensor_scalar(a_log[:], bank("w_alog")[:, 0:DIRS * UNITS], LOG_MAX, None, ALU.min).then_inc(freed("w_alog"), 1)
            fetched(dve, "gm")
            dve.wait_ge(S["gn_stats"], 16)
            v.tensor_copy(gmean[:], bank("gm")[0:CK, 0:8]).then_inc(freed("gm"), 1)
            taken(dve, "gm")
            v.tensor_tensor(gdv[:], gmv[:, :, 0], gmean[:], ALU.subtract).then_inc(S["gn_dev"], 1)
            dve.wait_ge(S["gn_dev"], 1)
            v.tensor_tensor(gsq[:], gdv[:], gdv[:], ALU.mult).then_inc(S["gn_dev"], 1)
            dve.wait_ge(S["gn_dev"], 2)
            v.tensor_tensor(gva[:], gsq[:], gmv[:, :, 1], ALU.add).then_inc(S["gn_var"], 1)
            fetched(dve, "gv")
            v.tensor_scalar(gve[:], bank("gv")[0:CK, 0:8], 1e-5, None, ALU.add).then_inc(freed("gv"), 1)
            taken(dve, "gv")
            v.tensor_scalar(gmean[:], gmean[:], -1.0, None, ALU.mult).then_inc(S["gn_eps"], 1)
            dve.wait_ge(S["gn_rsqrt"], 1)
            v.tensor_tensor(gbi[:], gmean[:], grs[:], ALU.mult).then_inc(S["gn_bias"], 1)

            dve.wait_ge(S["w_small"], 64)
            v.reduce_sum(dsum[:], dsk[:], AX_X).then_inc(S["small"], 1)

            def front(step, h):
                if step in ("conv0", "conv1"):
                    for i in (range(5) if step == "conv0" else range(5, 9)):
                        window = xpad[:].rearrange("p b y x -> p (b y) x")[:, i // 3:i // 3 + ACC_ROWS, i % 3:i % 3 + SIDE]
                        sums = acc[:]
                        if i == 0:
                            taken(dve, f"xh_{h}")
                            if h:
                                dve.wait_ge(S["xs0"], IMG * h)
                            v.tensor_scalar(sums, window, cw[:, 0:1], cb[:, 0:1], ALU.mult, ALU.add).then_inc(S["conv"], 1)
                        else:
                            dve.wait_ge(S["conv"], 9 * h + i)
                            v.scalar_tensor_tensor(sums, window, cw[:, i:i + 1], sums, ALU.mult, ALU.add).then_inc(S["conv"], 1)
                if step == "silu":
                    dve.wait_ge(S["conv"], 9 * (h + 1))
                    dve.wait_ge(S["conv_e"], 4 * (h + 1))
                    for b in range(IMG):
                        img = slice(b * L, (b + 1) * L)
                        v.tensor_tensor(xs[:, h, 0, img], conv_out[b], sg[:, img], ALU.mult).then_inc(S["xs0"], 1)
                    v.memset(wsel[h][:], 0.0).then_inc(S["wsel_zero"], 1)
                if step == "z":
                    dve.wait_ge(S["z_kept"], h + 1)
                    dve.wait_ge(S["gate_e"], 2 * (h + 1))
                    v.tensor_tensor(z[:, h, :, :], z[:, h, :, :], ze[:], ALU.mult).then_inc(S["gate_s"], 1)

            def weights(step):
                if step == "w_out":
                    dve.wait_ge(S["w_qkv"], 48)
                    dve.wait_ge(S["ident"], 1)
                    v.tensor_copy(prep[:], proj[:].unsqueeze(1).to_broadcast([FEAT, HPC, HD])).then_inc(S["repl"], 1)
                    v.tensor_copy(irep[:], ident[0:FEAT, 0:FEAT].unsqueeze(1).to_broadcast([FEAT, HPC, FEAT])).then_inc(S["repl"], 1)
                if step == "w_pbd":
                    fetched(dve, "w_pbd")
                    dve.wait_ge(S["const"], 8)
                    v.scalar_tensor_tensor(pbd[:], bank("w_pbd")[0:CK, 0:HPC * FEAT], float(HD) ** -0.25,
                                           pmask[:].rearrange("p a b -> p (a b)"), ALU.mult, ALU.mult).then_inc(freed("w_pbd"), 1)

            front("conv0", 0)
            front("conv1", 0)
            dve.wait_ge(S["a_exp"], 1)
            v.tensor_scalar(a_neg[:], a_neg[:], -1.0, None, ALU.mult).then_inc(S["neg_a"], 1)
            front("silu", 0)

            def pre_clip(n):
                dve.wait_ge(S["raw"], n + 1)
                v.tensor_scalar(spl[:], step2[:, 0, :], SOFTPLUS_LINEAR, None, ALU.min).then_inc(S["sp_in"], 1)

            def pre_ln(n):
                dve.wait_ge(S["sp_ln"], n + 1)
                v.scalar_tensor_tensor(spl[:], spe[:], SERIES_BELOW, spl[:], ALU.is_ge, ALU.mult).then_inc(S["sp_l"], 1)

            def pre_max(n):
                dve.wait_ge(S["sp_l"], 2 * n + 1)
                v.tensor_tensor(step2[:, 0, :], step2[:, 0, :], spl[:], ALU.max).then_inc(S["sp_l"], 1)

            def pre_max_series(n):
                dve.wait_ge(S["sp_l"], 2 * n + 2)
                dve.wait_ge(S["sp_s"], n + 1)
                v.tensor_tensor(step2[:, 0, :], step2[:, 0, :], sps[:], ALU.max).then_inc(S["sp_max"], 1)

            def pre_inp(n):
                h, k = n // DIRS, n % DIRS
                dve.wait_ge(S["sp_max"], n + 1)
                if k > 0:
                    dve.wait_ge(S["xs"], 5 * (h + 1))
                v.tensor_tensor(step2[:, 1, :], step2[:, 0, :], xs[:, h, k, :], ALU.mult).then_inc(S["step"], 1)

            def left_of_hi(n, i):
                dve.wait_ge(S["hi"], 2 * n + i + 1)
                v.tensor_tensor(step2[:, i, :], step2[:, i, :], hi[:, i, :], ALU.subtract).then_inc(S["rest"], 1)

            def drive_of(u):
                n = u // UNITS
                if u % UNITS == 0:
                    dve.wait_ge(S["b_there"], 16 * GRP * (n + 1))
                if u >= STATE_SLOTS:
                    dve.wait_ge(S["outp"], u - STATE_SLOTS + 1)
                dve.wait_ge(S["bc_inp"], u + 1)
                v.tensor_tensor(drive[:, u % STATE_SLOTS, :], b_rep[:, n % 2, :], inp_bc[u % 2][:, :],
                                ALU.mult).then_inc(S["drive"], 1)

            def scan(u):
                dve.wait_ge(S["drive"], u + 1)
                dve.wait_ge(S["decay"], u + 1)
                v.tensor_tensor_scan(state[:, u % STATE_SLOTS, :], decay[:, u % SLOTS, :, :].rearrange("p b l -> p (b l)"),
                                     drive[:, u % STATE_SLOTS, :], 0.0, ALU.mult, ALU.add).then_inc(S["state"], 1)

            def add_y(n):
                h, k = n // DIRS, n % DIRS
                dve.wait_ge(S["y_mm"], UNITS * (n + 1))
                rows = y_sum[:].rearrange("p (b l) -> p b l", b=IMG)
                turned = y_sum[:].rearrange("p (b y x) -> p b x y", b=IMG, x=SIDE)
                if n > 0:
                    dve.wait_ge(S["y_ev"], n)
                if k == 0:
                    dve.wait_ge(S["small"], 1)
                    if h:
                        fetched(dve, f"yT_{IMG * h - 1}")
                    v.scalar_tensor_tensor(y_sum[:], xs[:, h, 0, :], dsum[:, 0:1], y_acc[0:DI, :],
                                           ALU.mult, ALU.add).then_inc(S["y_ev"], 1)
                elif k == 2:
                    v.tensor_tensor(rows, rows, y_acc[0:DI, :].rearrange("p (b l) -> p b l", b=IMG)[:, :, ::-1],
                                    ALU.add).then_inc(S["y_ev"], 1)
                else:
                    for b in range(IMG):
                        src = y_acc[0:DI, b * L:(b + 1) * L].rearrange("p (x y) -> p x y", x=SIDE)
                        if k == 3:
                            src = src[:, ::-1, ::-1]
                        v.tensor_tensor(turned[:, b, :, :], turned[:, b, :, :], src, ALU.add).then_inc(S["y_ev" if b else "y_part"], 1)

            def statistics(n, i, src_of, tag, eps):
                b = n % IMG
                for t in range(2):
                    v.bn_stats(mst[:, i, 2 * b + t, :], src_of(t)).then_inc(S["stat_" + tag], 1)
                dve.wait_ge(S["stat_" + tag], 2 * (n + 1))
                for t in range(2):
                    v.bn_aggr(mv[:, i, 2 * b + t, :], mst[:, i, 2 * b + t, :]).then_inc(S["agg_" + tag], 1)
                dve.wait_ge(S["agg_" + tag], 2 * (n + 1))
                v.tensor_scalar(mv[:, i, 2 * b:2 * b + 2, 1], mv[:, i, 2 * b:2 * b + 2, 1], eps, None, ALU.add).then_inc(S["eps_" + tag], 1)

            def normed(n, i, dst, src_of, tag):
                b = n % IMG
                dve.wait_ge(S["rsqrt_" + tag], n + 1)
                for t in range(2):
                    v.tensor_scalar(dst[:, 2 * b + t, :], src_of(t), mv[:, i, 2 * b + t, 0:1], rs[:, i, 2 * b + t:2 * b + t + 1],
                                    ALU.subtract, ALU.mult).then_inc(S["norm_" + tag], 1)

            def normed_affine(n, i, dst, src_of, tag, gain, bias, product=None):
                b = n % IMG
                dve.wait_ge(S["rsqrt_" + tag], n + 1)
                dve.wait_ge(S["w_gb"], 64)
                each = 3 if product else 4
                for t in range(2):
                    v.scalar_tensor_tensor(dst[:, 2 * b + t, :], src_of(t), mv[:, i, 2 * b + t, 0:1], gain, ALU.subtract,
                                           ALU.mult).then_inc(freed(product) if product and t == 1 else S["norm_" + tag], 1)
                dve.wait_ge(S["norm_" + tag], each * n + each - 2)
                if product:
                    taken(dve, product)
                for t in range(2):
                    v.scalar_tensor_tensor(dst[:, 2 * b + t, :], dst[:, 2 * b + t, :], rs[:, i, 2 * b + t:2 * b + t + 1], bias,
                                           ALU.mult, ALU.add).then_inc(S["norm_" + tag], 1)

            def residual(dst, src, name):
                fetched(dve, name)
                v.tensor_tensor(dst, src, bank(name)[:, 0:2 * CH].rearrange("p (t c) -> p t c", t=2), ALU.add).then_inc(freed(name), 1)
                taken(dve, name)

            def route(n):
                b = n % IMG
                name = f"lg_{n}"
                fetched(dve, name)
                lg_, val_, rank_, msum_ = lg[:, b, :], val[:, b, :, :], rank[:, b, :], msum[:, b, :]
                v.tensor_scalar(lg_, bank(name)[0:1, 0:HEADS], 1.0 / L, None, ALU.mult).then_inc(freed(name), 1)
                taken(dve, name)
                li = lg_.unsqueeze(2).to_broadcast([1, HEADS, HEADS])
                lj = lg_.unsqueeze(1).to_broadcast([1, HEADS, HEADS])
                v.tensor_tensor(eq[:], lj, li, ALU.is_equal).then_inc(S["logit_eq"], 1)
                v.tensor_tensor(gt[:], lj, li, ALU.is_gt).then_inc(S["rank"], 1)
                dve.wait_ge(S["logit_eq"], n + 1)
                v.tensor_tensor(eq[:], eq[:], tri[:], ALU.mult).then_inc(S["rank"], 1)
                dve.wait_ge(S["rank"], 5 * n + 2)
                v.tensor_tensor(eq[:], gt[:], eq[:], ALU.add).then_inc(S["rank"], 1)
                dve.wait_ge(S["rank"], 5 * n + 3)
                v.reduce_sum(rank_, eq[:], AX_X).then_inc(S["rank"], 1)
                dve.wait_ge(S["rank"], 5 * n + 4)
                v.tensor_scalar(val_[:, 2, :], rank_, float(TOPK), None, ALU.is_lt).then_inc(S["rank"], 1)
                dve.wait_ge(S["rank"], 5 * n + 5)
                v.tensor_tensor(gt[:], tri[:], val_[:, 2, :].unsqueeze(1).to_broadcast([1, HEADS, HEADS]), ALU.mult).then_inc(S["slot_of"], 1)
                v.tensor_tensor(msum_, val_[:, 2, :], lg_, ALU.add).then_inc(S["slot_of"], 1)
                dve.wait_ge(S["slot_of"], 2 * (n + 1))
                v.reduce_sum(val_[:, 0, :], gt[:], AX_X).then_inc(S["vals"], 1)
                v.tensor_tensor(val_[:, 1, :], msum_, lg_, ALU.subtract).then_inc(S["vals"], 1)
                dve.wait_ge(S["vals"], 2 * (n + 1))
                v.tensor_copy(valr[:, b, :, :], val_.rearrange("p a b -> p (a b)").unsqueeze(2).to_broadcast([1, 3 * HEADS, HD])).then_inc(S["val_rows"], 1)

            def row_max(n, j):
                p, m = n % IMG, n // IMG * TOPK + j
                name = f"s{n}{j}"
                fetched(dve, name)
                v.tensor_reduce(nmax[p][:, m % 2, :], bank(name)[:, :].rearrange("p (q k) -> p q k", q=2), AX_X, ALU.max).then_inc(S["prob_max"][p], 1)
                dve.wait_ge(S["prob_max"][p], m + 1)
                if m >= 2:
                    dve.wait_ge(S["prob"][p], m - 1)
                v.tensor_scalar(nmaxs[p][:, m % 2, :], nmax[p][:, m % 2, :], -(HD ** -0.5), None, ALU.mult).then_inc(S["prob_bias"][p], 1)

            def divide_by_sum(n, j):
                p, m = n % IMG, n // IMG * TOPK + j
                taken(dve, f"s{n}{j}")
                v.reciprocal(prec[p][:, m % 2, :], psum_row[p][:, m % 2, :]).then_inc(S["prob_rec"][p], 1)
                dve.wait_ge(S["prob_rec"][p], m + 1)
                for q in range(2):
                    v.tensor_scalar(prob[p][:, m % 2, q, :], prob[p][:, m % 2, q, :], prec[p][:, m % 2, q:q + 1], None,
                                    ALU.mult).then_inc(S["prob_divided"][p], 1)

            def keep_head(n, j):
                p = n % IMG
                name = f"pv{n}{j}"
                fetched(dve, name)
                rows = slice(2 * HD * (j // 2), 2 * HD * (j // 2 + 1))
                if j % 2 == 0:
                    v.tensor_copy(cT[p][rows, :], bank(name)[rows, 0:L]).then_inc(freed(name), 1)
                else:
                    taken(dve, f"pv{n}{j - 1}")
                    v.tensor_tensor(cT[p][rows, :], cT[p][rows, :], bank(name)[rows, 0:L], ALU.add).then_inc(freed(name), 1)

            def side(step, n):
                h, b = n // IMG, n % IMG
                p = b
                name = f"{step}_{n}"
                ts = slice(2 * b, 2 * b + 2)
                tk = x_tok[:, 2 * n:2 * n + 2, :]
                if step in WEIGHT_STEPS:
                    weights(step)
                elif step in ("conv0", "conv1", "z", "silu"):
                    front(step, n)
                elif step == "yT":
                    fetched(dve, name)
                    statistics(n, 0, lambda t: bank(name)[:, t * DI:(t + 1) * DI], "y", 1e-5)
                elif step == "yn":
                    src = f"yT_{n}"
                    normed_affine(n, 0, yn, lambda t: bank(src)[:, t * DI:(t + 1) * DI], "y", gb[:, 0, 0:DI], gb[:, 0, DI:], src)
                elif step == "o":
                    residual(tk, tk, name)
                    statistics(n, 1, lambda t: tk[:, t, :], "t", 1e-5)
                elif step == "tn":
                    normed(n, 1, tn, lambda t: tk[:, t, :], "t")
                elif step[0] == "q":
                    fetched(dve, name)
                    i = 2 * int(step[1])
                    v.tensor_scalar(qp[:, i:i + 2, b * L:(b + 1) * L], bank(name)[:, :].rearrange("p (i l) -> p i l", i=2),
                                    KERNEL_EPS, KERNEL_EPS, ALU.add, ALU.max).then_inc(freed(name), 1)
                elif step[:2] == "kv":
                    t, j, w = 2 * b + int(step[2]), int(step[3]), HPC * FEAT
                    fetched(dve, name)
                    v.tensor_scalar(kp[:, t, j * w:(j + 1) * w], bank(name)[:, 0:w], KERNEL_EPS, KERNEL_EPS,
                                    ALU.add, ALU.max).then_inc(S["key"][b], 1)
                elif step == "at":
                    fetched(dve, name)
                    src = bank(name)[:, 0:2 * HEADS * (HD + 1)].rearrange("p (t h d) -> p t h d", t=2, h=HEADS)
                    v.reciprocal(arec[:, ts, :].unsqueeze(3), src[:, :, :, HD:HD + 1]).then_inc(S["a_rec"], 1)
                    dve.wait_ge(S["a_rec"], n + 1)
                    for t in range(2):
                        v.tensor_tensor(ao[:, 2 * b + t, :].rearrange("p (h d) -> p h d", d=HD), src[:, t, :, 0:HD],
                                        arec[:, 2 * b + t, :].unsqueeze(2).to_broadcast([P, HEADS, HD]),
                                        ALU.mult).then_inc(S["att"] if t == 0 else freed(name), 1)
                elif step == "p":
                    residual(tk, tk, name)
                    statistics(n, 2, lambda t: tk[:, t, :], "u", 1e-5)
                elif step == "un":
                    normed(n, 2, hn, lambda t: tk[:, t, :], "u")
                elif step == "lg":
                    route(n)
                elif step == "cr":
                    fetched(dve, name)
                    if n >= IMG:
                        dve.wait_ge(S["hot"], 4 * (n - 1))
                    v.tensor_copy(col[:, :, :, b], bank(name)[0:CK, 0:6].rearrange("p (u i) -> p u i", u=3)).then_inc(freed(name), 1)
                    taken(dve, f"cr_{n}")
                    if n >= IMG:
                        dve.wait_ge(S["sel"], 4 * (n - 1))
                    for i in range(2):
                        for u, w in ((0, 1), (1, 2)):
                            v.tensor_scalar(hot[:, u, i, b, :], slot_no[:], col[:, 0, i, b:b + 1], col[:, w, i, b:b + 1],
                                            ALU.is_equal, ALU.mult).then_inc(S["hot"], 1)
                    dve.wait_ge(S["hot"], 4 * (n + 1))
                    if n >= IMG:
                        fetched(dve, f"wv_{n - IMG}")
                    for i in range(2):
                        v.tensor_tensor(sel_m[:, b, i, :, :], dmatch[:].unsqueeze(1).to_broadcast([CK, TOPK, HD]),
                                        hot[:, 0, i, b, :].unsqueeze(2).to_broadcast([CK, TOPK, HD]), ALU.mult).then_inc(S["sel"], 1)
                        v.tensor_tensor(sel_u[:, b, i, :, :], dmatch[:].unsqueeze(1).to_broadcast([CK, TOPK, HD]),
                                        hot[:, 1, i, b, :].unsqueeze(2).to_broadcast([CK, TOPK, HD]), ALU.mult).then_inc(S["sel"], 1)
                elif step[0] == "h" and step != "hT":
                    j = int(step[1:])
                    if 0 < j <= TOPK:
                        divide_by_sum(n, j - 1)
                    if j > 2:
                        keep_head(n, j - 3)
                    if j < TOPK:
                        row_max(n, j)
                elif step == "fo":
                    if h:
                        dve.wait_ge(S["outd"][b], 16 * h)
                    residual(res[:, ts, :], hn[:, ts, :], name)
                    statistics(n, 3, lambda t: res[:, 2 * b + t, :], "r", 1e-12)
                elif step == "rn":
                    normed_affine(n, 3, res, lambda t: res[:, 2 * b + t, :], "r", gb[:, 1, :], gb[:, 2, :])

            pre_clip(0)
            pre_ln(0)
            pre_max(0)
            pre_max_series(0)
            pre_inp(0)
            left_of_hi(0, 0)
            left_of_hi(0, 1)
            front("z", 0)
            for u in range(SLOT_COUNT):
                if u % UNITS == ADD_Y and u > UNITS:
                    add_y(u // UNITS - 1)
                drive_of(u)
                if u > 0:
                    scan(u - 1)
                for at, part in ((PRE_CLIP, pre_clip), (PRE_LN, pre_ln), (PRE_MAX, pre_max), (PRE_MAX_SERIES, pre_max_series), (PRE_INP, pre_inp)):
                    if preparing(u, at):
                        part(preparing(u, at))
                for i in range(2):
                    if preparing(u, PRE_REST[i]):
                        left_of_hi(preparing(u, PRE_REST[i]), i)
                for item in beside[u - LAG] if u >= LAG else []:
                    side(*item)
            scan(SLOT_COUNT - 1)
            add_y(SCANS - 1)
            for item in beside[SLOT_COUNT - LAG]:
                side(*item)
            for item in rest:
                side(*item)

        @block.tensor
        def _(pe):
            t_ = nc.tensor
            idn = ident[:]

            def begin(name):
                reuse(pe, name)
                return bank(name)

            def done(ins):
                ins.then_inc(S["filled"], 1)

            pe.wait_ge(S["ident"], 1)
            for i in range(4):
                h, c = i // 2, i % 2
                if c == 0:
                    pe.wait_ge(S["x"][h], 16)
                for t in range(TILES):
                    ins = t_.transpose(gn_banks[i][0:CK, t * P:(t + 1) * P], x_tok[:, h * TILES + t, c * CK:(c + 1) * CK], idn)
                ins.then_inc(S["gn_turned"], 1)

            b_ = begin("w_in")
            pe.wait_ge(S["w_in"], 32)
            for ic in range(2):
                for oc in range(2):
                    ins = t_.transpose(b_[0:CK, (2 * ic + oc) * CK:(2 * ic + oc + 1) * CK], inw[:, oc, ic * CK:(ic + 1) * CK], ident[0:DI, 0:DI])
            done(ins)
            b_ = begin("w_xp")
            pe.wait_ge(S["w_xp"], 32)
            for k in range(DIRS):
                ins = t_.transpose(b_[0:DI, k * XROWS:(k + 1) * XROWS], xpw[:, k, :], ident[0:XROWS, 0:XROWS])
            done(ins)
            b_ = begin("w_dt")
            for k in range(DIRS):
                ins = t_.transpose(b_[0:RANK, k * DI:(k + 1) * DI], dtw[:, k, :], ident[0:DI, 0:DI])
            done(ins)
            b_ = begin("w_fold")
            taken(pe, "w_dt")
            for k in range(DIRS):
                ins = t_.matmul(b_[0:DI, k * DI:(k + 1) * DI], xpw[0:RANK, k, :], dtT[:, k, :], start=True, stop=True)
            done(ins)
            b_ = begin("w_alog")
            pe.wait_ge(S["w_alog"], 16)
            done(t_.transpose(b_[:, 0:DIRS * UNITS], alog[:], ident[0:DIRS * UNITS, 0:DIRS * UNITS]))

            b_ = begin("gm")
            pe.wait_ge(S["const"], 8)
            pe.wait_ge(S["gn_stats"], 16)
            done(t_.matmul(b_[0:CK, 0:8], avg6[:], gmv[:, :, 0], start=True, stop=True))
            b_ = begin("gv")
            pe.wait_ge(S["gn_var"], 1)
            done(t_.matmul(b_[0:CK, 0:8], avg6[:], gva[:], start=True, stop=True))
            taken(pe, "w_in")

            def front(step, h):
                b_ = begin(f"{step}_{h}")
                pe.wait_ge(S["xn"], 4 * (h + 1))
                if step == "xh":
                    for c in range(2):
                        ins = t_.matmul(b_[0:DI, :], inT[:, c, 0:DI], xnT[:, c, h * TOK:(h + 1) * TOK], start=(c == 0), stop=(c == 1))
                else:
                    for t in range(TILES):
                        for c in range(2):
                            at = h * TOK + t * P
                            ins = t_.matmul(b_[:, t * DI:(t + 1) * DI], xnT[:, c, at:at + P], inT[:, c, DI:2 * DI],
                                            start=(c == 0), stop=(c == 1))
                done(ins)

            def weights(name):
                b_ = begin(name)
                if name == "w_out":
                    for o in range(2):
                        ins = t_.transpose(b_[0:DI, o * CK:(o + 1) * CK], opw[:, o, :], ident[0:CK, 0:CK])
                elif name == "w_pbd":
                    pe.wait_ge(S["repl"], 2)
                    ins = t_.matmul(b_[0:CK, 0:HPC * FEAT], prep[:].rearrange("p a b -> p (a b)"),
                                    irep[:].rearrange("p a b -> p (a b)"), start=True, stop=True)
                elif name[:4] == "w_qk":
                    i, rc, c = (int(d) for d in name[4:])
                    taken(pe, "w_pbd")
                    ins = t_.matmul(b_[0:CK + c, 0:HPC * FEAT], qkvw[:, 2 * i + rc, c * CK:(c + 1) * CK + c], pbd[:],
                                    start=True, stop=True)
                elif name in ("w_v", "w_proj"):
                    w, base = (qkvw, 4) if name == "w_v" else (pjw, 0)
                    if name == "w_proj":
                        pe.wait_ge(S["w_proj"], 32)
                    for c in range(2):
                        for o in range(2):
                            ins = t_.transpose(b_[0:CK + c, (2 * c + o) * CK:(2 * c + o + 1) * CK],
                                               w[:, base + o, c * CK:(c + 1) * CK + c], ident[0:CK, 0:CK])
                else:
                    pe.wait_ge(S["w_ffn"], 96)
                    for oc in range(2):
                        for ic in range(2):
                            ins = t_.transpose(b_[0:CK, (2 * oc + ic) * CK:(2 * oc + ic + 1) * CK],
                                               fw[:, int(name[3]), ic, oc * CK:(oc + 1) * CK], ident[0:CK, 0:CK])
                done(ins)

            def pre(n):
                h, k = n // DIRS, n % DIRS
                if k == 0:
                    pe.wait_ge(S["xs0"], IMG * (h + 1))
                else:
                    pe.wait_ge(S["xs"], 5 * (h + 1))
                b_ = begin(f"d{n}")
                done(t_.matmul(b_[:, :], pre_w[:, k, :], xs[:, h, k, :], start=True, stop=True))

            def spread_out(u):
                n, g12 = u // UNITS, u % UNITS
                j, q = g12 // PER_CHUNK, g12 % PER_CHUNK
                if g12 == 0:
                    pe.wait_ge(S["stack"], 16 * 9 * (n + 1))
                if u >= 2:
                    pe.wait_ge(S["decay"], u - 1)
                t_.matmul(step_bc[u % 2][:, :], spread[:, q, :], stack[:, n % 2, j, 0:TOK], start=True, stop=True
                          ).then_inc(S["bc_step"], 1)
                if u >= 2:
                    pe.wait_ge(S["drive"], u - 1)
                t_.matmul(inp_bc[u % 2][:, :], spread[:, q, :], stack[:, n % 2, j, TOK:2 * TOK], start=True, stop=True
                          ).then_inc(S["bc_inp"], 1)

            def sum_states(u):
                n, g12 = u // UNITS, u % UNITS
                pe.wait_ge(S["outp"], u + 1)
                if g12 == 0 and n > 0:
                    pe.wait_ge(S["y_ev"], n)
                at = DI - GRP - GRP * g12
                t_.matmul(y_acc[0:DI, :], band[:, at:at + DI], outp[:, u % SLOTS, :],
                          start=(g12 == 0), stop=(g12 == UNITS - 1)).then_inc(S["y_mm"], 1)

            def scores(n, j):
                p = n % IMG
                b_ = begin(f"s{n}{j}")
                rows = slice(2 * HD * (j // 2), 2 * HD * (j // 2 + 1))
                for q in range(2):
                    ins = t_.matmul(b_[:, q * L:(q + 1) * L], fq[p][rows, j % 2, q * P:(q + 1) * P], fk[p][rows, :],
                                    start=True, stop=True)
                done(ins)

            def turn_probs(n, j):
                p, m = n % IMG, n // IMG * TOPK + j
                b_ = begin(f"pt{n}{j}")
                pe.wait_ge(S["prob_divided"][p], 2 * (m + 1))
                for kt in range(2):
                    for q in range(2):
                        ins = t_.transpose(b_[:, (2 * kt + q) * P:(2 * kt + q + 1) * P], prob[p][:, m % 2, q, kt * P:(kt + 1) * P], idn)
                done(ins)

            def weigh_values(n, j):
                p, m = n % IMG, n // IMG * TOPK + j
                b_ = begin(f"pv{n}{j}")
                taken(pe, f"pt{n}{j}")
                for kt in range(2):
                    ins = t_.matmul(b_[2 * HD * (j // 2):2 * HD * (j // 2 + 1), 0:L], fv[p][:, kt, j, :], probT[p][:, m % 2, kt, :],
                                    start=(kt == 0), stop=(kt == 1))
                done(ins)

            def turn(b_, src, b):
                for c in range(2):
                    for t in range(2):
                        ins = t_.transpose(b_[0:CK, c * L + t * P:c * L + (t + 1) * P], src[:, 2 * b + t, c * CK:(c + 1) * CK], idn)
                done(ins)

            def side(step, n):
                h, b = n // IMG, n % IMG
                p = b
                if step in NO_PRODUCT:
                    return
                if step in WEIGHT_STEPS:
                    weights(step)
                    return
                if step in ("xh", "z"):
                    front(step, n)
                    return
                if step[0] == "h" and step != "hT":
                    j = int(step[1:])
                    if 1 < j <= TOPK + 1:
                        turn_probs(n, j - 2)
                    if j > 2:
                        weigh_values(n, j - 3)
                    if j < TOPK:
                        scores(n, j)
                    return
                b_ = begin(f"{step}_{n}")
                at0 = b * L
                if step == "yT":
                    pe.wait_ge(S["y_ev"], DIRS * (h + 1))
                    for t in range(2):
                        ins = t_.transpose(b_[:, t * DI:(t + 1) * DI], y_sum[:, at0 + t * P:at0 + (t + 1) * P], ident[0:DI, 0:DI])
                    done(ins)
                elif step == "gT":
                    pe.wait_ge(S["gate"], n + 1)
                    for t in range(2):
                        ins = t_.transpose(b_[0:DI, t * P:(t + 1) * P], yn[:, 2 * b + t, :], idn)
                    done(ins)
                elif step == "o":
                    taken(pe, f"gT_{n}")
                    for t in range(2):
                        ins = t_.matmul(b_[:, t * CH:(t + 1) * CH], gT[:, at0 + t * P:at0 + (t + 1) * P], outT[:], start=True, stop=True)
                    done(ins)
                elif step == "tT":
                    pe.wait_ge(S["norm_t"], 2 * (n + 1))
                    turn(b_, tn, b)
                elif step[0] == "q":
                    taken(pe, f"tT_{n}")
                    for u in range(2):
                        i = 2 * int(step[1]) + u
                        for c in range(2):
                            ins = t_.matmul(b_[:, u * L:(u + 1) * L], qw[0:CK + c, c, i * P:(i + 1) * P], tT[0:CK + c, c, at0:at0 + L],
                                            start=(c == 0), stop=(c == 1))
                    done(ins)
                elif step[:2] == "kv":
                    at, j, w = at0 + int(step[2]) * P, int(step[3]), HPC * FEAT + CK
                    for c in range(2):
                        ins = t_.matmul(b_[:, 0:w], tT[0:CK + c, c, at:at + P], kvw[0:CK + c, c, j, :], start=(c == 0), stop=(c == 1))
                    done(ins)
                elif step == "cx":
                    for tj in ("00", "01", "10", "11"):
                        taken(pe, f"kv{tj}_{n}")
                    w = 2 * (HD + 1)
                    for i in range(PAIRS):
                        for t in range(2):
                            ins = t_.matmul(b_[:, i * w:(i + 1) * w], kp[:, 2 * b + t, i * P:(i + 1) * P],
                                            v1[:, 2 * b + t, 2 * i:2 * i + 2, :].rearrange("p h d -> p (h d)"),
                                            start=(t == 0), stop=(t == 1))
                    done(ins)
                elif step == "at":
                    taken(pe, f"cx_{n}")
                    w = 2 * (HD + 1)
                    for t in range(2):
                        for i in range(PAIRS):
                            at = (t * PAIRS + i) * w
                            ins = t_.matmul(b_[:, at:at + w], qp[:, i, at0 + t * P:at0 + (t + 1) * P], cbd[:, b, i, :],
                                            start=True, stop=True)
                    done(ins)
                elif step == "aT":
                    taken(pe, f"at_{n}")
                    pe.wait_ge(S["att"], n + 1)
                    turn(b_, ao, b)
                elif step == "p":
                    taken(pe, f"aT_{n}")
                    for t in range(2):
                        for c in range(2):
                            ins = t_.matmul(b_[:, t * CH:(t + 1) * CH], aT[0:CK + c, c, at0 + t * P:at0 + (t + 1) * P],
                                            pjT[0:CK + c, c, :], start=(c == 0), stop=(c == 1))
                    done(ins)
                elif step == "hT":
                    pe.wait_ge(S["norm_u"], 2 * (n + 1))
                    turn(b_, hn, b)
                elif step == "lg":
                    taken(pe, f"hT_{n}")
                    pe.wait_ge(S["w_wo"], 48)
                    for c in range(2):
                        ins = t_.matmul(b_[0:1, 0:HEADS], rin[0:CK + c, c, b:b + 1], wr[0:CK + c, c, :], start=(c == 0), stop=(c == 1))
                    done(ins)
                elif step == "cr":
                    pe.wait_ge(S["val_rows"], n + 1)
                    for u in range(3):
                        for i in range(2):
                            rows = valr[:, b, u * HEADS + i * HPC:u * HEADS + (i + 1) * HPC, :].rearrange("p a b -> p (a b)")
                            ins = t_.matmul(b_[0:CK, 2 * u + i:2 * u + i + 1], rows, ident[0:1, 0:1], start=True, stop=True)
                    done(ins)
                elif step == "wqk":
                    pe.wait_ge(S["sel"], 4 * (n + 1))
                    for i in range(2):
                        for c in range(2):
                            for o in range(2):
                                ins = t_.matmul(b_[0:CK + c, (2 * i + c) * CK:(2 * i + c + 1) * CK],
                                                fT[:, i, o, c * CK:(c + 1) * CK + c],
                                                sel_m[:, b, o, :, :].rearrange("p a b -> p (a b)"), start=(o == 0), stop=(o == 1))
                    done(ins)
                elif step == "wv":
                    for c in range(2):
                        for o in range(2):
                            t_.matmul(b_[0:CK + c, c * CK:(c + 1) * CK], fT[:, 2, o, c * CK:(c + 1) * CK + c],
                                      sel_m[:, b, o, :, :].rearrange("p a b -> p (a b)"), start=(o == 0), stop=(o == 1))
                    for o in range(2):
                        ins = t_.matmul(b_[0:CK, CH:2 * CH], sel_u[:, b, o, :, :].rearrange("p a b -> p (a b)"), wo[:, o, :],
                                        start=(o == 0), stop=(o == 1))
                    done(ins)
                elif step in ("fq", "fk"):
                    taken(pe, f"wqk_{n}")
                    for u, which in enumerate((0, 1) if step == "fq" else (2,)):
                        for c in range(2):
                            ins = t_.matmul(b_[0:CK, u * L:(u + 1) * L], wsel[p][0:CK + c, c, which, :],
                                            hT[0:CK + c, c, at0:at0 + L], start=(c == 0), stop=(c == 1))
                    done(ins)
                elif step == "fv":
                    taken(pe, f"wv_{n}")
                    for t in range(2):
                        for c in range(2):
                            ins = t_.matmul(b_[:, t * CK:(t + 1) * CK], hT[0:CK + c, c, at0 + t * P:at0 + (t + 1) * P],
                                            wsv[p][0:CK + c, c, :], start=(c == 0), stop=(c == 1))
                    done(ins)
                    for w in "qkv":
                        taken(pe, f"f{w}_{n}")
                elif step == "fo":
                    for j in range(TOPK - 3, TOPK):
                        taken(pe, f"pv{n}{j}")
                    for q in range(2):
                        ins = t_.matmul(b_[:, q * CH:(q + 1) * CH], cT[p][:, q * P:(q + 1) * P], wos[p][:], start=True, stop=True)
                    done(ins)

            front("xh", 0)
            front("z", 0)
            pre(0)
            pe.wait_ge(S["const2"], CONST2)
            pe.wait_ge(S["ones"], ONES)
            pe.wait_ge(S["xn"], 8)
            spread_out(0)
            for u in range(SLOT_COUNT):
                if u + 1 < SLOT_COUNT:
                    spread_out(u + 1)
                if u >= Y_LAG:
                    sum_states(u - Y_LAG)
                if preparing(u, PRE_RAW):
                    pre(preparing(u, PRE_RAW))
                for item in beside[u]:
                    side(*item)
            for u in range(SLOT_COUNT - Y_LAG, SLOT_COUNT):
                sum_states(u)
            pe.wait_ge(S["y_ev"], SCANS)
            for item in rest:
                side(*item)


_INS = ["x"] + ["L0_conv_" + n for n in ("in_proj_w", "conv_w", "conv_b", "x_proj_w", "dt_projs_w", "dt_projs_b", "A_logs",
                                         "Ds", "out_norm_g", "out_norm_b", "out_proj_w")]
_INS += ["L1_attn_" + n for n in ("w_qkv", "b_qkv", "w_proj", "b_proj", "projection")]
_INS += ["L1_ffn_" + n for n in ("Wq", "bq", "Wk", "bk", "Wv", "bv", "Wr", "br", "Wo", "bo", "ln_g", "ln_b")]
_OUTS = [((4, 16, 16, 192), "float32")]


def kernel(**inputs):
    import numpy as _np
    import concourse.bacc as _bacc
    from concourse import mybir as _mybir
    from concourse.bass_utils import run_bass_kernel_spmd as _run

    nc = _bacc.Bacc("TRN2", target_bir_lowering=False, num_devices=1)
    arrays, args = {}, []
    for name in _INS:
        a = _np.ascontiguousarray(inputs[name])
        arrays[f"in_{name}_dram"] = a
        args.append(nc.dram_tensor(f"in_{name}_dram", a.shape, _mybir.dt.from_np(a.dtype), kind="ExternalInput").ap())
    for i, (shape, dtype) in enumerate(_OUTS):
        dt = _mybir.dt.from_np(_np.dtype(dtype))
        args.append(nc.dram_tensor(f"out_{i}_dram", shape, dt, kind="ExternalOutput").ap())
    hybrid_kernel(nc, *args)
    r = _run(nc, [arrays], core_ids=[0])
    got = tuple(r.results[0][f"out_{i}_dram"] for i in range(len(_OUTS)))
    return got[0]
```
